# Optimizing a Trainium2 kernel written in Bass

```python
import numpy as np
import jax
import jax.numpy as jnp

def _softmax(x, axis=-1):
    return jax.nn.softmax(x, axis=axis)

def _gelu(x):
    return jax.nn.gelu(x, approximate=True)

def _silu(x):
    return jax.nn.silu(x)

def _sigmoid(x):
    return jax.nn.sigmoid(x)

def _layernorm(x, axis=-1, eps=1e-05):
    m = jnp.mean(x, axis=axis, keepdims=True)
    v = jnp.var(x, axis=axis, keepdims=True)
    return (x - m) / jnp.sqrt(v + eps)

def _scatter_add(tgt, idx, src, axis=0):
    return tgt.at[idx].add(src)

def _segment_sum(src, seg, n):
    return jax.ops.segment_sum(src, seg, n)
kernel_name = 'mk_decoder_preln_d1_seqx_r8_92bb44'

def setup_inputs(seed: int=0):
    np.random.seed(seed)
    _w = jnp.asarray

    def _rec_inputs():
        import jax
        import jax.numpy as jnp
        _rk = jax.random.key(seed)
        x = -0.0003929 + 0.9999 * jax.random.normal(jax.random.fold_in(_rk, 1), (8, 256, 256), jnp.float32)
        _lenS = 256 - jax.random.randint(jax.random.fold_in(_rk, 7), (8,), 0, max(1, 256 // 4) + 1, jnp.int32)
        _lenS2 = 64 - jax.random.randint(jax.random.fold_in(_rk, 8), (8,), 0, max(1, 64 // 4) + 1, jnp.int32)
        _ctx_1024P = jax.random.normal(jax.random.fold_in(_rk, 11), (8, 16, 128), jnp.float32)
        _ctx_1024c = jax.random.dirichlet(jax.random.fold_in(_rk, 511), 0.3 * jnp.ones((16,), jnp.float32), (8, 64))
        _ctx_1024t = jnp.einsum('bsk,bkd->bsd', _ctx_1024c, _ctx_1024P)
        _ctx_1024t = _ctx_1024t * jax.lax.rsqrt(jnp.mean(jnp.square(_ctx_1024t)) + 1e-12) * 0.953939
        ctx_1024 = -0.000494167 + 1.00018 * (_ctx_1024t + 0.3 * jax.random.normal(jax.random.fold_in(_rk, 611), (8, 64, 128), jnp.float32))
        _validS = jnp.arange(256)[None, :] < _lenS[:, None]
        _validS2 = jnp.arange(64)[None, :] < _lenS2[:, None]
        _causal = jnp.tril(jnp.ones((256, 256), dtype=bool))
        mask_BxS2_bf1 = jnp.ones((8, 64), dtype=bool)
        return (x, ctx_1024, mask_BxS2_bf1)
    x, ctx_1024, mask_BxS2_bf1 = _rec_inputs()

    def _L0_attn_setup():
        import jax, jax.numpy as jnp
        import numpy as np
        B, S, HID = (1, 512, 256)
        NH, NKV, D = (16, 4, 128)
        QPG = NH // NKV
        GROUP = (QPG + 2) * D
        TOTAL = NKV * GROUP
        key = jax.random.key(seed)
        k0, k1, k2 = jax.random.split(key, 3)
        x = jax.random.normal(k0, (B, S, HID), dtype=jnp.float32)
        weight_qkv = jax.random.normal(k1, (TOTAL, HID), dtype=jnp.float32) * 0.02
        weight_proj = jax.random.normal(k2, (HID, NH * D), dtype=jnp.float32) * 0.02
        return {'x': x, 'weight_qkv': weight_qkv, 'weight_proj': weight_proj}
    _L0_attn_all = _L0_attn_setup()
    _L0_attn_in = {k: v for k, v in _L0_attn_all.items() if k in ('weight_qkv', 'weight_proj')}
    del _L0_attn_all

    def _L0_xattn_setup():
        import jax, jax.numpy as jnp
        import numpy as np
        N_HEADS = 16
        N_KV_HEADS = 8
        HEAD_DIM = 128
        D_TEXT = 256
        D_VISION = 128
        GROUPS = N_HEADS // N_KV_HEADS
        key = jax.random.key(seed)
        ks = jax.random.split(key, 6)
        B, T_text, T_vis = (4, 256, 72)
        text_hidden = jax.random.normal(ks[0], (B, T_text, D_TEXT), dtype=jnp.float32)
        vision_tokens = jax.random.normal(ks[1], (B, T_vis, D_VISION), dtype=jnp.float32)
        vision_mask = jnp.ones((B, T_vis), dtype=bool)
        s = 0.02
        Wq = jax.random.normal(ks[2], (D_TEXT, N_HEADS * HEAD_DIM), dtype=jnp.float32) * s
        Wk = jax.random.normal(ks[3], (D_VISION, N_KV_HEADS * HEAD_DIM), dtype=jnp.float32) * s
        Wv = jax.random.normal(ks[4], (D_VISION, N_KV_HEADS * HEAD_DIM), dtype=jnp.float32) * s
        Wo = jax.random.normal(ks[5], (N_HEADS * HEAD_DIM, D_TEXT), dtype=jnp.float32) * s
        return {'text_hidden': text_hidden, 'vision_tokens': vision_tokens, 'vision_mask': vision_mask, 'Wq': Wq, 'Wk': Wk, 'Wv': Wv, 'Wo': Wo}
    _L0_xattn_all = _L0_xattn_setup()
    _L0_xattn_in = {k: v for k, v in _L0_xattn_all.items() if k in ('Wq', 'Wk', 'Wv', 'Wo')}
    del _L0_xattn_all

    def _L0_ffn_setup():
        import jax, jax.numpy as jnp
        import numpy as np
        NUM_EXPERTS = 8
        TOP_K = 2
        EMB = 256
        MLP = 512
        B, S = (4, 128)
        key = jax.random.key(seed)
        ks = jax.random.split(key, 5)
        scale_x = 1.0
        return {'x': jax.random.normal(ks[0], (B, S, EMB), dtype=jnp.float32), 'gate_kernel': jax.random.normal(ks[1], (EMB, NUM_EXPERTS), dtype=jnp.float32) / np.sqrt(EMB), 'w0_kernel': jax.random.normal(ks[2], (NUM_EXPERTS, EMB, MLP), dtype=jnp.float32) / np.sqrt(EMB), 'w1_kernel': jax.random.normal(ks[3], (NUM_EXPERTS, EMB, MLP), dtype=jnp.float32) / np.sqrt(EMB), 'wo_kernel': jax.random.normal(ks[4], (NUM_EXPERTS, MLP, EMB), dtype=jnp.float32) / np.sqrt(MLP)}
    _L0_ffn_all = _L0_ffn_setup()
    _L0_ffn_in = {k: v for k, v in _L0_ffn_all.items() if k in ('gate_kernel', 'w0_kernel', 'w1_kernel', 'wo_kernel')}
    del _L0_ffn_all
    return {'x': x, 'ctx_1024': ctx_1024, 'mask_BxS2_bf1': mask_BxS2_bf1, 'L0_attn_weight_qkv': _L0_attn_in['weight_qkv'], 'L0_attn_weight_proj': _L0_attn_in['weight_proj'], 'L0_xattn_Wq': _L0_xattn_in['Wq'], 'L0_xattn_Wk': _L0_xattn_in['Wk'], 'L0_xattn_Wv': _L0_xattn_in['Wv'], 'L0_xattn_Wo': _L0_xattn_in['Wo'], 'L0_ffn_gate_kernel': _L0_ffn_in['gate_kernel'], 'L0_ffn_w0_kernel': _L0_ffn_in['w0_kernel'], 'L0_ffn_w1_kernel': _L0_ffn_in['w1_kernel'], 'L0_ffn_wo_kernel': _L0_ffn_in['wo_kernel']}

def reference(x, ctx_1024, mask_BxS2_bf1, L0_attn_weight_qkv, L0_attn_weight_proj, L0_xattn_Wq, L0_xattn_Wk, L0_xattn_Wv, L0_xattn_Wo, L0_ffn_gate_kernel, L0_ffn_w0_kernel, L0_ffn_w1_kernel, L0_ffn_wo_kernel):
    import jax
    import jax.numpy as jnp

    def _L0_attn_ref(x, weight_qkv, weight_proj):
        import jax, jax.numpy as jnp
        import numpy as np
        B, S, HID = (1, 512, 256)
        NH, NKV, D = (16, 4, 128)
        QPG = NH // NKV
        GROUP = (QPG + 2) * D
        TOTAL = NKV * GROUP
        b, s, _ = x.shape
        qkv = jnp.einsum('bsh,ph->bsp', x, weight_qkv).reshape(b, s, NKV, GROUP)
        q = qkv[..., :QPG * D].reshape(b, s, NKV, QPG, D)
        k = qkv[..., QPG * D:(QPG + 1) * D]
        v = qkv[..., (QPG + 1) * D:]
        scale = 1.0 / jnp.sqrt(jnp.float32(D))
        scores = jnp.einsum('bsgqd,btgd->bgqst', q, k) * scale
        causal = jnp.tril(jnp.ones((s, s), dtype=bool))
        scores = jnp.where(causal, scores, jnp.finfo(scores.dtype).min)
        attn = jax.nn.softmax(scores, axis=-1)
        out = jnp.einsum('bgqst,btgd->bsgqd', attn, v)
        out = out.reshape(b, s, NH * D)
        return jnp.einsum('bse,he->bsh', out, weight_proj)

    def _L0_xattn_ref(text_hidden, vision_tokens, vision_mask, Wq, Wk, Wv, Wo):
        import jax, jax.numpy as jnp
        import numpy as np
        N_HEADS = 16
        N_KV_HEADS = 8
        HEAD_DIM = 128
        D_TEXT = 256
        D_VISION = 128
        GROUPS = N_HEADS // N_KV_HEADS
        B, T_text, _ = text_hidden.shape
        T_vis = vision_tokens.shape[1]
        scale = jnp.float32(np.sqrt(HEAD_DIM))
        q = (text_hidden @ Wq).reshape(B, T_text, N_HEADS, HEAD_DIM).transpose(0, 2, 1, 3)
        k = (vision_tokens @ Wk).reshape(B, T_vis, N_KV_HEADS, HEAD_DIM).transpose(0, 2, 1, 3)
        v = (vision_tokens @ Wv).reshape(B, T_vis, N_KV_HEADS, HEAD_DIM).transpose(0, 2, 1, 3)
        k = jnp.repeat(k, GROUPS, axis=1)
        v = jnp.repeat(v, GROUPS, axis=1)
        scores = jnp.einsum('bhtd,bhsd->bhts', q, k) / scale
        mask = vision_mask[:, None, None, :]
        scores = jnp.where(mask, scores, -jnp.inf)
        attn = jax.nn.softmax(scores, axis=-1)
        attn = jnp.nan_to_num(attn, nan=0.0)
        out = jnp.einsum('bhts,bhsd->bhtd', attn, v)
        out = out.transpose(0, 2, 1, 3).reshape(B, T_text, N_HEADS * HEAD_DIM)
        return out @ Wo

    def _L0_ffn_ref(x, gate_kernel, w0_kernel, w1_kernel, wo_kernel):
        import jax, jax.numpy as jnp
        import numpy as np
        NUM_EXPERTS = 8
        TOP_K = 2
        EMB = 256
        MLP = 512
        B, S = (4, 128)
        gate_logits = jnp.einsum('bsd,de->bse', x, gate_kernel)
        top_k_weights, top_k_indices = jax.lax.top_k(gate_logits, TOP_K)
        top_k_weights = jax.nn.softmax(top_k_weights.astype(jnp.float32), axis=-1).astype(x.dtype)
        one_hot = jax.nn.one_hot(top_k_indices, NUM_EXPERTS, dtype=x.dtype)
        combine = jnp.einsum('bsk,bske->bse', top_k_weights, one_hot)
        h0 = jnp.einsum('bsd,edm->bsem', x, w0_kernel)
        h1 = jnp.einsum('bsd,edm->bsem', x, w1_kernel)
        inter = jax.nn.silu(h0) * h1
        out = jnp.einsum('bse,bsem,emd->bsd', combine, inter, wo_kernel)
        return out
    x = x + _L0_attn_ref(_layernorm(x, axis=-1), L0_attn_weight_qkv, L0_attn_weight_proj)
    x = x + _L0_xattn_ref(_layernorm(x, axis=-1), ctx_1024, mask_BxS2_bf1, L0_xattn_Wq, L0_xattn_Wk, L0_xattn_Wv, L0_xattn_Wo)
    x = x + _L0_ffn_ref(_layernorm(x, axis=-1), L0_ffn_gate_kernel, L0_ffn_w0_kernel, L0_ffn_w1_kernel, L0_ffn_wo_kernel)
    return x

_drawn_inputs = setup_inputs


def setup_inputs(seed=0):
    import zlib

    import numpy as np

    out = dict(_drawn_inputs(seed))
    spreads = {}
    factors = {'L0_xattn_Wq': 4.371, 'L0_xattn_Wk': 3.76}
    for name, (base, spread) in spreads.items():
        noise = np.random.default_rng([zlib.crc32(name.encode()), seed]).standard_normal(out[name].shape)
        drawn = base * np.exp(spread * noise) if base else spread * noise
        out[name] = jnp.asarray(drawn.astype(out[name].dtype))
    for name, factor in factors.items():
        out[name] = (out[name] * factor).astype(out[name].dtype)
    return out
```

```python
from contextlib import ExitStack

import concourse.bass as bass
from concourse import mybir

F32 = mybir.dt.float32
F32R = mybir.dt.float32r
BF16 = mybir.dt.bfloat16
U8 = mybir.dt.uint8
ALU = mybir.AluOpType
ACT = mybir.ActivationFunctionType
AX_X = mybir.AxisListType.X

P = 128
EPS = 1e-5
NEG = -1e30
BIG = 3e38


class Split:

    def __init__(self, hi, lo):
        self.hi, self.lo = hi, lo

    def __getitem__(self, at):
        return Split(self.hi[at], self.lo[at])

    def view(self, pattern, **sizes):
        return Split(self.hi.rearrange(pattern, **sizes), self.lo.rearrange(pattern, **sizes))


def mm3(pe, out, lhsT, rhs, first, last):
    pe.matmul(out, lhsT.hi, rhs.hi, start=first, stop=False, skip_group_check=True)
    pe.matmul(out, lhsT.hi, rhs.lo, start=False, stop=False, skip_group_check=True)
    return pe.matmul(out, lhsT.lo, rhs.hi, start=False, stop=last, skip_group_check=True)


class Uses:

    def __init__(self, first, body, quiet=()):
        self.full, self.freed, self.before = {}, {}, {}
        n, f, last = {}, {}, {}
        for part, steps in enumerate((first, body)):
            base_n, base_f = dict(n), dict(f)
            for name, bank in steps:
                key = (part, name)
                self.before[key] = last.get(bank)
                n[bank] = n.get(bank, 0) + 1
                f[bank] = f.get(bank, 0) + (name[0] not in quiet)
                self.full[key], self.freed[key] = n[bank], f[bank]
                last[bank] = name
            if part == 1:
                self.per_full = {b: n[b] - base_n.get(b, 0) for b in n}
                self.per_freed = {b: f[b] - base_f.get(b, 0) for b in f}
                self.last = last
        self.bank = {(part, name): bank for part, steps in enumerate((first, body)) for name, bank in steps}

    def count_full(self, p, name):
        if p is None:
            return self.full[0, name]
        return p * self.per_full[self.bank[1, name]] + self.full[1, name]

    def count_freed(self, p, name):
        if p is None:
            return self.freed[0, name]
        return p * self.per_freed[self.bank[1, name]] + self.freed[1, name]

    def bank_of(self, p, name):
        return self.bank[0 if p is None else 1, name]


class Common:
    pass


def self_attention(nc, cm, w_qkv, w_proj):
    B, S, HID, NT, D, HC = cm.B, cm.S, cm.HID, cm.NT, P, cm.HC
    NH = w_proj.shape[1] // D
    NKV = (w_qkv.shape[0] // D - NH) // 2
    QPG = NH // NKV
    NR = NH + 2 * NKV
    PAIRS, TP, TT = cm.PAIRS, cm.TP, cm.TT
    SCALE = float(D) ** -0.5
    UNITS = 2 * NH
    CW = P + 2 * P
    x_all, ident, bank = cm.x_all, cm.ident, cm.bank

    with ExitStack() as ctx:
        def sb(name, shape, dt=F32):
            return ctx.enter_context(nc.sbuf_tensor(name, shape, dt))

        def split(name, shape):
            return Split(sb(name + "_hi", shape, F32R), sb(name + "_lo", shape, F32R))

        def sem(name):
            return cm.sems.enter_context(nc.semaphore("a_" + name))

        causal = sb("causal", [P, CW])
        WqkvT = split("WqkvT", [P, HC, NR * D])
        WprojT = split("WprojT", [P, NH, HID])
        xn = sb("xn", [P, TT, HID])
        xnT = split("xnT", [P, HC, TP])
        kT = split("kT", [P, NKV, TP])
        v = split("v", [P, TT, NKV * D])
        qT = split("qT", [P, 2, TP])
        oT = split("oT", [P, 2, TP])
        pT = split("pT", [P, 2, CW])
        masked = sb("masked", [P, 2, CW])
        prob = sb("prob", [P, 3, CW])
        negmax = sb("negmax", [P, 4, 2])
        rowsum = sb("rowsum", [P, 4, 2])
        rinv = sb("rinv", [P, 4, 2])
        stage = sb("stage", [P, NR * HID])
        ln_stats = sb("ln_stats", [P, NT, 6])
        ln_mv = sb("ln_mv", [P, NT, 2])
        ln_var = sb("ln_var", [P, NT])
        ln_rstd = sb("ln_rstd", [P, NT])
        minus_half = sb("minus_half", [P, NT])

        full = {n: sem("full_" + n) for n in bank}
        half = {n: sem("half_" + n) for n in bank}
        free = {n: sem("free_" + n) for n in bank}
        x_loaded = sem("x_loaded")
        w_loaded = [sem(f"w_loaded{i}") for i in range(2)]
        ident_made = sem("ident_made")
        mask_made = sem("mask_made")
        stats_done = sem("stats_done")
        half_made = sem("half_made")
        var_ready = sem("var_ready")
        rstd_ready = sem("rstd_ready")
        xn_ready = sem("xn_ready")
        masked_ready = sem("masked_ready")
        exp_done = sem("exp_done")
        rinv_ready = sem("rinv_ready")
        prob_ready = sem("prob_ready")
        x_updated = sem("x_updated")

        setup_banks = ("q", "t", "s0", "s1", "o0")
        stage_qkv = stage[:].rearrange("p (r k) -> p r k", k=HID)
        stage_proj = stage[:, 0:2 * NH * D].rearrange("p (j e) -> p j e", j=2)
        fills = []
        for c in range(HC):
            for r in range(0, NR, 4):
                fills.append((WqkvT[:, c, r * P:(r + 4) * P],
                              [stage_qkv[:, r + i, c * P:(c + 1) * P] for i in range(4)]))
        QKV_FILLS = len(fills)
        for h in range(0, NH, 2):
            fills.append((WprojT[:, h:h + 2, :],
                          [stage_proj[:, i % 2, (h + i // 2) * P:(h + i // 2 + 1) * P] for i in range(4)]))
        setup = [(("w", i), setup_banks[i % len(setup_banks)]) for i in range(len(fills))]
        front = ([(("xt", c), "q") for c in range(HC)] + [(("k", g), ("q", "o0")[g % 2]) for g in range(NKV)]
                 + [(("v", t), ("s0", "s1")[t % 2]) for t in range(TT)] + [(("q", 0), "q")])
        body = []
        LAST = UNITS + 6
        for s in range(LAST):
            if s < UNITS:
                body.append((("scores", s), ("s0", "s1")[s % 2]))
                if s % 2 == 0 and s // 2 + 1 < NH:
                    body.append((("q", s // 2 + 1), "q"))
                if s >= 5 and s % 2 == 1 and (s - 5) // 2 < NH - 2:
                    body.append((("o", (s - 5) // 2), ("o0", "o1")[(s - 5) // 2 % 2]))
            if s >= 7 and s % 2 == 1 and (s - 7) // 2 < NH:
                body.append((("proj", (s - 7) // 2), None))
            if 0 <= s - 2 < UNITS:
                body.append((("t", s - 2), "t"))
            if 0 <= s - 3 < UNITS:
                body.append((("pv", s - 3), None))
                h = (s - 3) // 2
                if (s - 3) % 2 == 1 and h >= NH - 2:
                    body.append((("o", h), ("o0", "o1")[h % 2]))
            if 22 <= s < 22 + TT:
                body.append((("next_xn", s - 22), None))
            more = {29: front[0:1], 30: front[1:2], UNITS: front[2:4], UNITS + 1: front[4:6], UNITS + 2: front[6:8],
                    UNITS + 3: front[8:]}
            body += [(("next",) + name, b) for name, b in more.get(s, [])]
        body.append((("residual",), None))
        real = [(n, b) for n, b in body if b]
        uses = Uses(setup + front, [((n[1:] if n[0] == "next" else n), b) for n, b in real], quiet=("scores",))

        w_qkv_v = w_qkv.rearrange("(r p) k -> p r k", p=P)
        w_proj_v = w_proj.rearrange("(j p) e -> p j e", p=P)
        x_v = cm.x.rearrange("b (t p) k -> p (b t) k", p=P)

        def dst_of(name):
            what, i = name
            return {"w": lambda: (fills[i][0], 512), "xt": lambda: (xnT[:, i, :], TP), "k": lambda: (kT[:, i, :], TP),
                    "v": lambda: (v[:, i, :], NKV * D), "q": lambda: (qT[:, i % 2, :], TP),
                    "t": lambda: (pT[:, i % 2, :], CW), "o": lambda: (oT[:, i % 2, :], TP)}[what]()

        def passes(eng, run):
            with eng.Fori(0, PAIRS - 1) as p:
                for name, _ in body:
                    run(p, name)
            for name, _ in body:
                if not name[0].startswith("next"):
                    run(PAIRS - 1, name)

        with nc.Block() as block:

            @block.sync
            def _(sp):
                sp.dma_start(stage_qkv, w_qkv_v).then_inc(w_loaded[0], 16)
                sp.dma_start(x_all[:], x_v).then_inc(x_loaded, 16)
                at = ("w", QKV_FILLS - 1)
                sp.wait_ge(full[uses.bank_of(None, at)], uses.count_full(None, at))
                sp.dma_start(stage_proj, w_proj_v).then_inc(w_loaded[1], 16)

            @block.gpsimd
            def _(pool):
                pool.memset(ident[:], 0.0).then_inc(ident_made, 1)
                pool.memset(causal[:], 0.0).then_inc(mask_made, 1)
                pool.wait_ge(ident_made, 1)
                pool.affine_select(out=ident[:], in_=ident[:], compare_op=ALU.not_equal, fill=1.0, base=0,
                                   pattern=[[-1, P]], channel_multiplier=1).then_inc(ident_made, 1)
                pool.wait_ge(mask_made, 1)
                for at in (0, 2 * P):
                    pool.affine_select(out=causal[:, at:at + P], in_=causal[:, at:at + P], compare_op=ALU.is_ge,
                                       fill=NEG, base=0, pattern=[[-1, P]], channel_multiplier=1)\
                        .then_inc(mask_made, 1)
                pool.memset(minus_half[:], -0.5).then_inc(half_made, 1)
                pool.wait_ge(half_made, 1)
                pool.wait_ge(var_ready, 1)
                pool.tensor_tensor(ln_rstd[:], ln_var[:], minus_half[:], ALU.pow).then_inc(rstd_ready, 1)

                def run(p, name):
                    if name[0] != "scores":
                        return
                    u = name[1]
                    pool.wait_ge(rinv_ready, p * UNITS + (u + 1))
                    for i, (a, b) in enumerate(((0, P), (P, CW))):
                        pool.tensor_tensor(prob[:, u % 3, a:b], prob[:, u % 3, a:b],
                                           rinv[:, u % 4, i:i + 1].to_broadcast([P, b - a]), ALU.mult)\
                            .then_inc(prob_ready, 1)

                passes(pool, run)

            @block.scalar
            def _(act):
                def high(p, name):
                    n = uses.bank_of(p, name)
                    dst, width = dst_of(name)
                    act.wait_ge(full[n], uses.count_full(p, name))
                    act.activation(dst.hi, bank[n][:, 0:width], ACT.Copy).then_inc(half[n], 1)

                for name, _ in setup + front:
                    high(None, name)

                def run(p, name):
                    if name[0] == "next":
                        high(p, name[1:])
                    elif name[0] in ("q", "t") or name[0] == "o" and name[1] >= NH - 2:
                        high(p, name)
                    elif name[0] == "scores":
                        s = name[1]
                        if s >= 5 and s % 2 == 1:
                            high(p, ("o", (s - 5) // 2))
                        act.wait_ge(masked_ready, p * 2 * UNITS + 2 * (s + 1))
                        for i, (a, b) in enumerate(((0, P), (P, CW))):
                            act.activation(prob[:, s % 3, a:b], masked[:, s % 2, a:b], ACT.Exp, scale=-1.0,
                                           bias=negmax[:, s % 4, i:i + 1],
                                           accum_out=rowsum[:, s % 4, i:i + 1]).then_inc(exp_done, 1)

                passes(act, run)

            @block.vector
            def _(dve):
                def low(p, name):
                    n = uses.bank_of(p, name)
                    dst, width = dst_of(name)
                    src = bank[n][:, 0:width]
                    if len(dst.lo.shape) == 3:
                        src = src.rearrange("p (a b) -> p a b", a=dst.lo.shape[1])
                    dve.wait_ge(half[n], uses.count_freed(p, name))
                    dve.tensor_tensor(dst.lo, src, dst.hi.bitcast(F32), ALU.subtract).then_inc(free[n], 1)

                def normalize(p, t):
                    xt = x_all[:, bass.ds(p * TT + t, 1), :].rearrange("p a k -> p (a k)")
                    mu = ln_mv[:, bass.ds(p * TT + t, 1), 0]
                    rs = ln_rstd[:, bass.ds(p * TT + t, 1)]
                    dve.tensor_scalar(xn[:, t, :], xt, mu, rs, ALU.subtract, ALU.mult).then_inc(xn_ready, 1)

                def invert(p, s):
                    dve.wait_ge(exp_done, p * 2 * UNITS + 2 * (s + 1))
                    dve.reciprocal(rinv[:, s % 4, :], rowsum[:, s % 4, :]).then_inc(rinv_ready, 1)

                dve.wait_ge(x_loaded, 16)
                for t in range(NT):
                    dve.bn_stats(ln_stats[:, t, :], x_all[:, t, :]).then_inc(stats_done, 1)
                for t in range(NT):
                    dve.wait_ge(stats_done, t + 1)
                    dve.bn_aggr(ln_mv[:, t, :], ln_stats[:, t, :]).then_inc(stats_done, 1)
                dve.wait_ge(stats_done, 2 * NT)
                dve.tensor_scalar(ln_var[:], ln_mv[:, :, 1], EPS, None, ALU.add).then_inc(var_ready, 1)
                for name, _ in setup:
                    low(None, name)
                dve.wait_ge(rstd_ready, 1)
                for t in range(TT):
                    normalize(0, t)
                for name, _ in front:
                    low(None, name)
                dve.wait_ge(mask_made, 3)

                def run(p, name):
                    if name[0] == "next":
                        low(p, name[1:])
                    elif name[0] == "next_xn":
                        normalize(p + 1, name[1])
                    elif name[0] in ("q", "o"):
                        low(p, name)
                    elif name[0] == "scores":
                        s = name[1]
                        n = uses.bank_of(p, name)
                        dve.wait_ge(full[n], uses.count_full(p, name))
                        if s == 0:
                            dve.tensor_copy(rinv[:, 3, :], ident[:, 0:2])
                        else:
                            invert(p, s - 1)
                        for i, (a, b) in enumerate(((0, P), (P, CW))):
                            dve.tensor_tensor_reduce(masked[:, s % 2, a:b], bank[n][:, a:b], causal[:, a:b],
                                                     -SCALE, BIG, ALU.add, ALU.min, negmax[:, s % 4, i:i + 1])\
                                .then_inc(masked_ready, 1)
                    elif name[0] == "t":
                        low(p, name)
                    elif name[0] == "residual":
                        for j, n in enumerate(("y0", "y1")):
                            dve.wait_ge(full[n], p + 1)
                            xt = x_all[:, bass.ds(p * TT + 2 * j, 2), :]
                            dve.tensor_tensor(xt, bank[n][:].rearrange("p (t k) -> p t k", t=2), xt, ALU.add)\
                                .then_inc(x_updated, 1)
                    if name == ("t", UNITS - 3):
                        invert(p, UNITS - 1)

                passes(dve, run)

            @block.tensor
            def _(pe):
                def wait_free(p, name):
                    n = uses.bank_of(p, name)
                    before = uses.before[0 if p is None else 1, name]
                    if before is None:
                        return
                    if before[0] == "scores":
                        pe.wait_ge(masked_ready, p * 2 * UNITS + 2 * (before[1] + 1))
                    else:
                        pe.wait_ge(free[n], uses.count_freed(p, name) - (name[0] != "scores"))

                def fill(p, name):
                    what, i = name
                    n = uses.bank_of(p, name)
                    wait_free(p, name)
                    if what == "w":
                        for j, src in enumerate(fills[i][1]):
                            ins = pe.transpose(bank[n][:, j * P:(j + 1) * P], src, ident[:])
                    elif what == "xt":
                        for t in range(TT):
                            ins = pe.transpose(bank[n][:, t * P:(t + 1) * P], xn[:, t, i * P:(i + 1) * P], ident[:])
                    elif what == "v":
                        for c in range(HC):
                            wv = WqkvT.view("p c (g i d) -> p c g i d", g=NKV, d=D)[:, c, :, QPG + 1, :]
                            ins = mm3(pe, bank[n][:].rearrange("p (g d) -> p g d", g=NKV),
                                      xnT[:, c, i * P:(i + 1) * P], wv, c == 0, c == HC - 1)
                    else:
                        col = {"k": (i * (QPG + 2) + QPG) * D, "q": ((i // QPG) * (QPG + 2) + i % QPG) * D}[what]
                        for c in range(HC):
                            ins = mm3(pe, bank[n][:], WqkvT[:, c, col:col + D], xnT[:, c, :], c == 0, c == HC - 1)
                    ins.then_inc(full[n], 1)

                def wait_copied(p, name):
                    pe.wait_ge(free[uses.bank_of(p, name)], uses.count_freed(p, name))

                pe.wait_ge(ident_made, 2)
                for name, _ in setup:
                    if name == ("w", 0):
                        pe.wait_ge(w_loaded[0], 16)
                    if name == ("w", QKV_FILLS):
                        pe.wait_ge(w_loaded[1], 16)
                    fill(None, name)
                for name, _ in setup[-len(setup_banks):]:
                    wait_copied(None, name)
                pe.wait_ge(xn_ready, TT)
                for name, _ in front:
                    if name == ("k", 0):
                        wait_copied(None, ("xt", 0))
                        wait_copied(None, ("xt", 1))
                    fill(None, name)
                for name, _ in front[HC:]:
                    wait_copied(None, name)

                def run(p, name):
                    what = name[0]
                    if what == "next":
                        if name == ("next", "xt", 0):
                            pe.wait_ge(xn_ready, p * TT + 2 * TT)
                        if name == ("next", "k", 0):
                            wait_copied(p, ("xt", 0))
                            wait_copied(p, ("xt", 1))
                        fill(p, name[1:])
                        if name == ("next", "q", 0):
                            for other, _ in front[HC:-1]:
                                wait_copied(p, other)
                    elif what == "q":
                        fill(p, name)
                    elif what == "scores":
                        u = name[1]
                        h, b = u // 2, u % 2
                        g = h // QPG
                        n = uses.bank_of(p, name)
                        wait_free(p, name)
                        if b == 0 and h > 0:
                            wait_copied(p, ("q", h))
                        if u == 0:
                            pe.wait_ge(free["q"], uses.count_freed(p, ("q", 1)) - 1)
                        mm3(pe, bank[n][:, 0:P], qT[:, h % 2, b * S:b * S + P], kT[:, g, b * S:b * S + P], True, True)
                        mm3(pe, bank[n][:, P:CW], qT[:, h % 2, b * S + P:b * S + S], kT[:, g, b * S:b * S + S],
                            True, True).then_inc(full[n], 1)
                    elif what == "t":
                        u = name[1]
                        pe.wait_ge(prob_ready, p * 2 * UNITS + 2 * (u + 1))
                        wait_free(p, name)
                        for j in range(3):
                            ins = pe.transpose(bank["t"][:, j * P:(j + 1) * P], prob[:, u % 3, j * P:(j + 1) * P],
                                               ident[:])
                        ins.then_inc(full["t"], 1)
                    elif what == "pv":
                        u = name[1]
                        h, b = u // 2, u % 2
                        g = h // QPG
                        wait_copied(p, ("t", u))
                        if b == 0:
                            wait_free(p, ("o", h))
                        n = uses.bank_of(p, ("o", h))
                        vg = v[:, :, g * D:(g + 1) * D]
                        mm3(pe, bank[n][:, b * S:b * S + S], vg[:, 2 * b, :], pT[:, u % 2, 0:S], True, False)
                        ins = mm3(pe, bank[n][:, b * S + P:b * S + S], vg[:, 2 * b + 1, :], pT[:, u % 2, S:CW],
                                  False, True)
                        if b == 1:
                            ins.then_inc(full[n], 1)
                    elif what == "proj":
                        h = name[1]
                        wait_copied(p, ("o", h))
                        for t in range(TT):
                            y = ("y0", "y1")[t // 2]
                            ins = mm3(pe, bank[y][:, (t % 2) * HID:(t % 2 + 1) * HID],
                                      oT[:, h % 2, t * P:(t + 1) * P], WprojT[:, h, :],
                                      h == 0 and t % 2 == 0, h == NH - 1)
                            if h == NH - 1 and t % 2 == 1:
                                ins.then_inc(full[y], 1)

                passes(pe, run)


class Order:

    def __init__(self, first, body):
        self.at, last, n = {}, {}, {}
        for part, steps in enumerate((first, body)):
            base = {k: tuple(v) for k, v in n.items()}
            for name, bank, who in steps:
                c = n.setdefault(bank, [0, 0, 0])
                c[0] += 1
                c[1] += who == "both"
                c[2] += who != ""
                self.at[part, name] = (bank, tuple(c), last.get(bank), who)
                last[bank] = name
        self.per = {k: tuple(b - a for a, b in zip(base.get(k, (0, 0, 0)), v)) for k, v in n.items()}

    def _count(self, p, name, which):
        bank, c, _, _ = self.at[0 if p is None else 1, name]
        return c[which] if p is None else p * self.per[bank][which] + c[which]

    def bank(self, p, name):
        return self.at[0 if p is None else 1, name][0]

    def who(self, p, name):
        return self.at[0 if p is None else 1, name][3]

    def full(self, p, name):
        return self._count(p, name, 0)

    def half(self, p, name):
        return self._count(p, name, 1)

    def free(self, p, name):
        return self._count(p, name, 2)

    def before(self, p, name):
        return self.at[0 if p is None else 1, name][2]


def cross_attention(nc, cm, ctx_in, mask, Wq, Wk, Wv, Wo):
    HID, NT, HC, PAIRS, TP, TT, S = cm.HID, cm.NT, cm.HC, cm.PAIRS, cm.TP, cm.TT, cm.S
    D = P
    S2, DV = ctx_in.shape[1:]
    NH = Wq.shape[1] // D
    NG = Wk.shape[1] // D
    KP = 2 * S2
    SCALE = float(D) ** -0.5
    HALF = NH // 2 * S2
    NJ = NH * S2 // P
    x_all, ident, bank = cm.x_all, cm.ident, cm.bank

    with ExitStack() as ctx:
        def sb(name, shape, dt=F32, at=ctx):
            return at.enter_context(nc.sbuf_tensor("b_" + name, shape, dt))

        def split(name, shape):
            return Split(sb(name + "_hi", shape, F32R), sb(name + "_lo", shape, F32R))

        def sem(name):
            return cm.sems.enter_context(nc.semaphore("b_" + name))

        WqT = sb("WqT", [P, NH, HID])
        wk = sb("wk", [P, NG * D])
        wv = sb("wv", [P, NG * D])
        wo = sb("wo", [P, NH, HID])
        ctxT = sb("ctxT", [P, PAIRS * KP])
        kT = sb("kT", [P, NG, KP])
        vT = sb("vT", [P, NG, KP])
        xn = sb("xn", [P, TT, HID])
        xnT = split("xnT", [P, HC, TP])
        M = split("M", [P, HC, 2, NH, S2])
        VW = split("VW", [P, NG, 2, HID])
        prob = sb("prob", [P, 2, NH * S2])
        pT = split("pT", [P, 2, NJ, P])
        rowmax = sb("rowmax", [P, 2, NH])
        rowsum = sb("rowsum", [P, 2, NH])
        rinv = sb("rinv", [P, 2, NH])
        ln_stats = sb("ln_stats", [P, TT, 6])
        ln_mv = sb("ln_mv", [P, 2, TT, 2])
        ln_var = sb("ln_var", [P, TT])
        ln_rstd = sb("ln_rstd", [P, 2, TT])
        minus_half = sb("minus_half", [P, TT])
        mask_u8 = sb("mask_u8", [1, PAIRS * KP], U8)
        mask_bf = sb("mask_bf", [1, PAIRS * KP], BF16)
        bias_bf = sb("bias_bf", [1, PAIRS * KP], BF16)
        ones_bf = sb("ones_bf", [1, P], BF16)
        keep = sb("keep", [P, PAIRS])
        with ExitStack() as early:
            stage = sb("stage", [P, HC, NH * D], at=early)
            ctx_sb = sb("ctx", [P, PAIRS, DV], at=early)
        VWs = split("VWs", [P, NG, 2 * HID])

        full = {n: sem("full_" + n) for n in bank}
        half = {n: sem("half_" + n) for n in bank}
        free = {n: sem("free_" + n) for n in bank}
        small_loaded = sem("small_loaded")
        wq_loaded = sem("wq_loaded")
        kv_loaded = sem("kv_loaded")
        wo_loaded = sem("wo_loaded")
        consts = sem("consts")
        mask_ready = sem("mask_ready")
        ctx_masked = sem("ctx_masked")
        stats_done = sem("stats_done")
        var_ready = sem("var_ready")
        rstd_ready = sem("rstd_ready")
        xn_ready = sem("xn_ready")
        max_ready = sem("max_ready")
        shifted = sem("shifted")
        exp_done = sem("exp_done")
        sum_ready = sem("sum_ready")
        rinv_ready = sem("rinv_ready")
        prob_ready = sem("prob_ready")
        VW_moved = sem("VW_moved")
        y_added = sem("y_added")

        setup = [(("keep", 0), "y0", "dve")] + \
                [(("w", i), ("q", "t", "s0", "s1")[i % 4], ("act", "dve")[i % 2]) for i in range(NH * HC // 4)] + \
                [(("ctx", 0), "o0", "act")]
        rot = ("q", "t", "s0", "s1")
        front = [(("xt", c), ("q", "t")[c], "both") for c in range(HC)]
        front += [(("k", i), ("s0", "s1")[i], "act") for i in range(2)]
        front += [(("v", i), ("q", "t")[i], "act") for i in range(2)]
        front += [(("m", i), rot[(i + 2) % 4], "both") for i in range(NH // 4 * HC)]

        def s_step(t):
            return [(("s", t, j), (("q", "t"), ("s0", "s1"))[t % 2][j], "") for j in range(2)]

        def t_step(t):
            return [(("t", t, j), ("o0", "o1")[j], "both") for j in range(2)]

        def vw_step(gs):
            return [(("vw", g), ("y1", "o0", "o1")[g % 3], "both") for g in gs]

        def y_step(t):
            return [(("y", t), "y0", "")]

        def quiet(*name):
            return [(name, None, "")]

        nxt = [(("next",) + n, b, w) for n, b, w in front]
        body = (s_step(0) + vw_step((0, 1)) + s_step(1) + quiet("sum", 0) + vw_step((2, 3)) + quiet("move", 0)
                + vw_step((4, 5)) + quiet("sum", 1) + vw_step((6, 7)) + quiet("move", 1)
                + t_step(0) + s_step(2) + y_step(0) + quiet("next_ln", 0) + quiet("sum", 2) + t_step(1) + s_step(3)
                + y_step(1) + quiet("next_xn", 0) + quiet("sum", 3)
                + t_step(2) + nxt[0:2] + y_step(2) + nxt[2:6] + nxt[6:10] + t_step(3) + nxt[10:] + y_step(3))
        order = Order(setup + front, [((n[1:] if n[0] == "next" else n), b, w) for n, b, w in body if b])

        def dst_of(name):
            what, i = name[0], name[1]
            n = name_bank[name]
            b = bank[n][:]
            if what == "w":
                return WqT[:, 2 * i:2 * i + 2, :], b.rearrange("p (h k) -> p h k", h=2)
            if what == "ctx":
                return ctxT[:], b
            if what == "xt":
                return xnT[:, i, :], b
            if what in ("k", "v"):
                return {"k": kT, "v": vT}[what][:, 4 * i:4 * i + 4, :], b.rearrange("p (g k) -> p g k", g=4)
            if what == "m":
                h, c = 4 * (i // HC), i % HC
                return (M[:, c, :, h:h + 4, :].view("p b h s -> p h b s"),
                        b.rearrange("p (h b s) -> p h b s", h=4, b=2))
            if what == "vw":
                return VWs[:, i, :], b
            if what == "t":
                return (pT[:, i % 2, 4 * name[2]:4 * name[2] + 4, :], b.rearrange("p (j q) -> p j q", j=4))

        name_bank = {name: b for name, b, _ in setup + front}
        name_bank.update({(n[1:] if n[0] == "next" else n): b for n, b, _ in body if b})

        def passes(eng, run):
            with eng.Fori(0, PAIRS - 1) as p:
                for name, _, _ in body:
                    run(p, name)
            for name, _, _ in body:
                if not name[0].startswith("next"):
                    run(PAIRS - 1, name)

        with nc.Block() as block:

            @block.sync
            def _(sp):
                sp.dma_start(mask_u8[:], mask.rearrange("(a b) s -> a (b s)", a=1)).then_inc(small_loaded, 16)
                sp.dma_start(ctx_sb[:], ctx_in.rearrange("(p b) s d -> (b s) p d", b=2)).then_inc(small_loaded, 16)
                sp.dma_start(stage[:], Wq.rearrange("(c p) n -> p c n", p=P)).then_inc(wq_loaded, 16)
                sp.dma_start(wk[:], Wk).then_inc(kv_loaded, 16)
                sp.dma_start(wv[:], Wv).then_inc(kv_loaded, 16)
                sp.dma_start(wo[:], Wo.rearrange("(h p) n -> p h n", p=P)).then_inc(wo_loaded, 16)

                def run(p, name):
                    if name[0] != "move":
                        return
                    g0 = NG // 2 * name[1]
                    at = ("vw", g0 + 3)
                    sp.wait_ge(free[order.bank(p, at)], order.free(p, at))
                    for src, dst in ((VWs.hi, VW.hi), (VWs.lo, VW.lo)):
                        for b in range(2):
                            for h in range(2):
                                sp.dma_start(dst[h * S2:(h + 1) * S2, g0:g0 + 4, b, :].bitcast(F32),
                                             src[b * S2:(b + 1) * S2, g0:g0 + 4, h * HID:(h + 1) * HID].bitcast(F32))\
                                    .then_inc(VW_moved, 16)

                passes(sp, run)

            @block.gpsimd
            def _(pool):
                pool.memset(minus_half[:], -0.5).then_inc(consts, 1)
                pool.memset(ones_bf[:], 1.0).then_inc(consts, 1)

                def power(count, slot):
                    pool.wait_ge(consts, 2)
                    pool.wait_ge(var_ready, count)
                    pool.tensor_tensor(ln_rstd[:, slot, :], ln_var[:], minus_half[:], ALU.pow).then_inc(rstd_ready, 1)

                power(1, 0)

                def run(p, name):
                    if name[0] == "next_ln":
                        power(p + 2, 0)
                    if name[0] == "sum":
                        t = name[1]
                        pool.wait_ge(rinv_ready, p * TT + (t + 1))
                        pr = prob[:, t % 2, :].rearrange("p (h s) -> p h s", s=S2)
                        pool.tensor_tensor(pr, pr, rinv[:, t % 2, :].unsqueeze(2).to_broadcast([P, NH, S2]), ALU.mult)\
                            .then_inc(prob_ready, 1)

                passes(pool, run)

            @block.scalar
            def _(act):
                def copy_out(p, name):
                    who = order.who(p, name)
                    if who in ("both", "act"):
                        n = order.bank(p, name)
                        dst, src = dst_of(name)
                        act.wait_ge(full[n], order.full(p, name))
                        act.activation(dst.hi if who == "both" else dst, src, ACT.Copy)\
                            .then_inc(half[n] if who == "both" else free[n], 1)

                for name, _, _ in setup + front:
                    copy_out(None, name)

                def run(p, name):
                    if name[0] == "next":
                        copy_out(p, name[1:])
                    elif name[0] in ("vw", "t"):
                        copy_out(p, name)
                    elif name[0] == "sum":
                        t = name[1]
                        act.wait_ge(shifted, p * 2 * TT + 2 * (t + 1))
                        act.activation(prob[:, t % 2, :], prob[:, t % 2, :], ACT.Exp, scale=SCALE)\
                            .then_inc(exp_done, 1)

                passes(act, run)

            @block.vector
            def _(dve):
                def copy_out(p, name):
                    who = order.who(p, name)
                    n = order.bank(p, name)
                    if who == "both":
                        dst, src = dst_of(name)
                        dve.wait_ge(half[n], order.half(p, name))
                        dve.tensor_tensor(dst.lo, src, dst.hi.bitcast(F32), ALU.subtract).then_inc(free[n], 1)
                    elif who == "dve":
                        dst, src = dst_of(name)
                        dve.wait_ge(full[n], order.full(p, name))
                        dve.tensor_copy(dst, src).then_inc(free[n], 1)

                def tile(p, t):
                    return x_all[:, bass.ds(p * TT + t, 1), :].rearrange("p a k -> p (a k)")

                def layer_norm_stats(p, q):
                    for t in range(TT):
                        dve.bn_stats(ln_stats[:, t, :], tile(p, t)).then_inc(stats_done, 1)
                    dve.wait_ge(stats_done, q * 2 * TT + TT)
                    dve.tensor_copy(ln_var[:, 0:1], ln_stats[:, 0, 0:1])
                    for t in range(TT):
                        dve.bn_aggr(ln_mv[:, 0, t, :], ln_stats[:, t, :]).then_inc(stats_done, 1)
                    dve.wait_ge(stats_done, q * 2 * TT + 2 * TT)
                    dve.tensor_scalar(ln_var[:], ln_mv[:, 0, :, 1], EPS, None, ALU.add).then_inc(var_ready, 1)

                def normalize(p, q):
                    dve.wait_ge(rstd_ready, q + 1)
                    for t in range(TT):
                        dve.tensor_scalar(xn[:, t, :], tile(p, t), ln_mv[:, 0, t, 0:1], ln_rstd[:, 0, t:t + 1],
                                          ALU.subtract, ALU.mult).then_inc(xn_ready, 1)

                layer_norm_stats(0, 0)
                dve.wait_ge(small_loaded, 32)
                dve.tensor_copy(mask_bf[:], mask_u8[:]).then_inc(mask_ready, 1)
                dve.wait_ge(mask_ready, 1)
                dve.tensor_scalar(bias_bf[:], mask_bf[:], -1.0, -NEG, ALU.add, ALU.mult).then_inc(mask_ready, 1)
                dve.wait_ge(full["y0"], 1)
                dve.tensor_copy(keep[:], bank["y0"][:, 0:PAIRS]).then_inc(free["y0"], 1)
                dve.wait_ge(free["y0"], 1)
                for p in range(PAIRS):
                    dve.tensor_scalar(ctx_sb[:, p, :], ctx_sb[:, p, :], keep[:, p:p + 1], None, ALU.mult)\
                        .then_inc(ctx_masked, 1)
                normalize(0, 0)
                for name, _, _ in setup[1:] + front:
                    copy_out(None, name)

                def run(p, name):
                    if name[0] == "next":
                        copy_out(p, name[1:])
                    elif name[0] in ("vw", "t"):
                        copy_out(p, name)
                    elif name[0] == "next_ln":
                        layer_norm_stats(p + 1, p + 1)
                    elif name[0] == "next_xn":
                        normalize(p + 1, p + 1)
                    elif name[0] == "s" and name[2] == 1:
                        t = name[1]
                        heads = NH // 2
                        banks = [bank[order.bank(p, ("s", t, j))][:].rearrange("p (h s) -> p h s", s=S2)
                                 for j in range(2)]
                        for j in range(2):
                            n = order.bank(p, ("s", t, j))
                            dve.wait_ge(full[n], order.full(p, ("s", t, j)))
                            dve.tensor_reduce(rowmax[:, t % 2, j * heads:(j + 1) * heads], banks[j], AX_X, ALU.max)\
                                .then_inc(max_ready, 1)
                        if t >= 2:
                            for j in range(2):
                                n = order.bank(p, ("t", t - 2, j))
                                dve.wait_ge(full[n], order.full(p, ("t", t - 2, j)))
                        for j in range(2):
                            n = order.bank(p, ("s", t, j))
                            dve.wait_ge(max_ready, p * 2 * TT + (2 * t + j + 1))
                            dve.tensor_tensor(
                                prob[:, t % 2, j * HALF:(j + 1) * HALF].rearrange("p (h s) -> p h s", s=S2), banks[j],
                                rowmax[:, t % 2, j * heads:(j + 1) * heads].unsqueeze(2).to_broadcast([P, heads, S2]),
                                ALU.subtract).then_inc(shifted, 1)
                    elif name[0] == "sum":
                        t = name[1]
                        dve.wait_ge(exp_done, p * TT + (t + 1))
                        dve.tensor_reduce(rowsum[:, t % 2, :], prob[:, t % 2, :].rearrange("p (h s) -> p h s", s=S2),
                                          AX_X, ALU.add).then_inc(sum_ready, 1)
                        dve.wait_ge(sum_ready, p * TT + (t + 1))
                        dve.reciprocal(rinv[:, t % 2, :], rowsum[:, t % 2, :]).then_inc(rinv_ready, 1)
                    elif name[0] == "y":
                        t = name[1]
                        dve.wait_ge(full["y0"], order.full(p, name))
                        dve.tensor_tensor(tile(p, t), bank["y0"][:, 0:HID], tile(p, t), ALU.add)\
                            .then_inc(y_added, 1)

                passes(dve, run)

            @block.tensor
            def _(pe):
                def wait_free(p, name):
                    n = order.bank(p, name)
                    if order.before(p, name) is None:
                        return
                    before = order.before(p, name)
                    if before[0] == "s":
                        pe.wait_ge(shifted, p * 2 * TT + (2 * before[1] + before[2] + 1))
                    elif name[0] == "y":
                        if name[1] > 0:
                            pe.wait_ge(y_added, p * TT + name[1])
                    else:
                        pe.wait_ge(free[n], order.free(p, name) - (order.who(p, name) != ""))

                def wait_copied(p, name):
                    n = order.bank(p, name)
                    pe.wait_ge(free[n], order.free(p, name))

                def fill(p, name):
                    what, i = name[0], name[1]
                    n = order.bank(p, name)
                    wait_free(p, name)
                    if what == "w":
                        for j in range(4):
                            h, c = 2 * i + j // 2, j % 2
                            ins = pe.transpose(bank[n][:, j * P:(j + 1) * P], stage[:, c, h * P:(h + 1) * P], ident[:])
                    elif what == "ctx":
                        for j in range(PAIRS):
                            ins = pe.transpose(bank[n][:, j * P:(j + 1) * P], ctx_sb[:, j, :], ident[:])
                    elif what == "xt":
                        for t in range(TT):
                            ins = pe.transpose(bank[n][:, t * P:(t + 1) * P], xn[:, t, i * P:(i + 1) * P], ident[:])
                    elif what in ("k", "v"):
                        w = {"k": wk, "v": wv}[what]
                        q = 0 if p is None else p + 1
                        for j in range(4):
                            g = 4 * i + j
                            ins = pe.matmul(bank[n][:, j * P:(j + 1) * P], w[:, g * D:(g + 1) * D],
                                            ctxT[:, bass.ds(q * KP, KP)], start=True, stop=True,
                                            skip_group_check=True)
                    elif what == "m":
                        for j in range(4):
                            h, c = 4 * (i // HC) + j, i % HC
                            ins = pe.matmul(bank[n][:, j * P:(j + 1) * P], WqT[:, h, c * P:(c + 1) * P],
                                            kT[:, h // 2, :], start=True, stop=True, skip_group_check=True)
                    elif what == "vw":
                        ins = pe.matmul(bank[n][:], vT[:, i, :], wo[:, 2 * i:2 * i + 2, :].rearrange("p h n -> p (h n)"),
                                        start=True, stop=True, skip_group_check=True)
                    ins.then_inc(full[n], 1)

                pe.wait_ge(mask_ready, 2)
                pe.wait_ge(consts, 2)
                for p in range(PAIRS):
                    ins = pe.matmul(bank["y0"][:, p:p + 1], mask_bf[:, p * KP:(p + 1) * KP], ones_bf[:, 0:1],
                                    start=True, stop=True, skip_group_check=True)
                ins.then_inc(full["y0"], 1)
                pe.wait_ge(wq_loaded, 16)
                for name, _, _ in setup[1:]:
                    if name[0] == "ctx":
                        pe.wait_ge(ctx_masked, PAIRS)
                    fill(None, name)
                for name, _, _ in setup[-5:]:
                    wait_copied(None, name)

                def needs(p, name):
                    q = 0 if p is None else p + 1
                    if name == ("xt", 0):
                        pe.wait_ge(xn_ready, q * TT + TT)
                    if name == ("k", 0) and p is None:
                        pe.wait_ge(kv_loaded, 32)
                    if name == ("m", 0):
                        wait_copied(p, ("k", 0))
                        wait_copied(p, ("k", 1))

                for name, _, _ in front:
                    needs(None, name)
                    fill(None, name)
                pe.wait_ge(wo_loaded, 16)

                def run(p, name):
                    what = name[0]
                    if what == "next":
                        needs(p, name[1:])
                        fill(p, name[1:])
                    elif what == "s":
                        t, j = name[1], name[2]
                        n = order.bank(p, name)
                        if t == 0 and j == 0:
                            for other, b, _ in front[-4:]:
                                pe.wait_ge(free[b], p * order.per[b][2] + order.free(None, other))
                        wait_free(p, name)
                        b = t // 2
                        for c in range(HC):
                            mm3(pe, bank[n][:], xnT[:, c, t * P:(t + 1) * P],
                                M[:, c, b, 8 * j:8 * j + 8, :].view("p h s -> p (h s)"), c == 0, False)
                        bias = bias_bf[:, bass.ds(p * KP + b * S2, S2)].unsqueeze(1).to_broadcast([1, NH // 2, S2])
                        pe.matmul(bank[n][:].rearrange("p (h s) -> p h s", s=S2), ones_bf[:, :], bias,
                                  start=False, stop=True, skip_group_check=True).then_inc(full[n], 1)
                    elif what == "vw":
                        fill(p, name)
                    elif what == "t":
                        t, j = name[1], name[2]
                        n = order.bank(p, name)
                        wait_free(p, name)
                        pe.wait_ge(prob_ready, p * TT + (t + 1))
                        for i in range(4):
                            at = (4 * j + i) * P
                            ins = pe.transpose(bank[n][:, i * P:(i + 1) * P], prob[:, t % 2, at:at + P], ident[:])
                        ins.then_inc(full[n], 1)
                    elif what == "y":
                        t = name[1]
                        b = t // 2
                        wait_free(p, name)
                        for j in range(2):
                            wait_copied(p, ("t", t, j))
                        if t == 0:
                            pe.wait_ge(VW_moved, p * 256 + 256)
                        for j in range(NJ):
                            ins = mm3(pe, bank["y0"][:, 0:HID], pT[:, t % 2, j, :], VW[:, j, b, :],
                                      j == 0, j == NJ - 1)
                        ins.then_inc(full["y0"], 1)

                passes(pe, run)


def feed_forward(nc, cm, gate, w0, w1, wo):
    E, HID, MLP = w0.shape
    NT, HC = cm.NT, cm.HC
    MC = MLP // P
    BT = 512
    NB = NT * P // BT
    TB = BT // P
    BODY = 2 * NB
    NEVER = -3e38
    x_all, ident, bank = cm.x_all, cm.ident, cm.bank
    H_BANKS = (("q", "t"), ("s0", "s1"))
    O_BANKS = ("o0", "o1", "y0", "y1")

    with ExitStack() as ctx:
        def sb(name, shape, dt=F32):
            return ctx.enter_context(nc.sbuf_tensor(name, shape, dt))

        def split(name, shape):
            return Split(sb(name + "_hi", shape, F32R), sb(name + "_lo", shape, F32R))

        def sem(name):
            return cm.sems.enter_context(nc.semaphore("c_" + name))

        WCOLS = 2 * HC * MLP + MC * HID
        stage = sb("f_stage", [P, 2, WCOLS])
        W = split("f_W", [P, 2, WCOLS])
        xnT = split("f_xnT", [P, HC, NT * P])
        inter = split("f_inter", [P, 2, MC, BT])
        sil = sb("f_sil", [P, 2, BT])
        inter_f = sb("f_inter_f", [P, 2, BT])
        xn = sb("f_xn", [P, 4, HID])
        gate_sb = sb("f_gate", [P, HC, E])
        gate_w = split("f_gate_w", [P, HC, E])
        ln_stats = sb("f_ln_stats", [P, NT, 6])
        ln_mv = sb("f_ln_mv", [P, NT, 2])
        ln_var = sb("f_ln_var", [P, NT])
        ln_rstd = sb("f_ln_rstd", [P, NT])
        minus_half = sb("f_minus_half", [P, NT])
        iota = sb("f_iota", [P, NT, E])
        logits = sb("f_logits", [P, NT, E])
        work = sb("f_work", [P, NT, E])
        onehot = [sb("f_onehot%d" % k, [P, NT, E]) for k in range(2)]
        top = [sb("f_top%d" % k, [P, NT]) for k in range(2)]
        chosen = sb("f_chosen", [P, NT])
        gap = sb("f_gap", [P, NT])
        wt = [sb("f_wt%d" % k, [P, NT]) for k in range(2)]
        comb = sb("f_comb", [P, NT, E])

        gate_loaded, even_loaded, odd_loaded = sem("gate_loaded"), sem("even_loaded"), sem("odd_loaded")
        loaded = (even_loaded, odd_loaded)
        consts, stats_done, var_ready, rstd_ready = sem("consts"), sem("stats_done"), sem("var_ready"), sem("rstd_ready")
        xn_ready, xt_full, xt_hi, xt_lo = sem("xn_ready"), sem("xt_full"), sem("xt_hi"), sem("xt_lo")
        gate_hi, gate_lo, logits_full, routed = sem("gate_hi"), sem("gate_lo"), sem("logits_full"), sem("routed")
        gap_ready, gap_exp = sem("gap_ready"), sem("gap_exp")
        w_hi, w_lo = sem("w_hi"), sem("w_lo")
        h_full, silu_done, inter_done = sem("h_full"), sem("silu_done"), sem("inter_done")
        i_hi, i_lo, o_free, o_full = sem("i_hi"), sem("i_lo"), sem("o_free"), sem("o_full")

        def w0_of(e, c, m):
            return W[:, e, c * MLP + m * P:c * MLP + (m + 1) * P]

        def w1_of(e, c, m):
            at = (HC + c) * MLP + m * P
            return W[:, e, at:at + P]

        def wo_of(e, m):
            at = 2 * HC * MLP + m * HID
            return W[:, e, at:at + HID]

        CH = WCOLS // 4

        def steps(last):
            out = []
            for g in range(BODY):
                for m in range(MC):
                    out.append(("h", g, m))
                    if m % 2 == 1 and g % NB in (1, 2) and (g < NB or not last):
                        out.append(("w", g // NB, 2 * (g % NB - 1) + m // 2))
                    if g > 0:
                        out.append(("o", g - 1, m))
            for t in range(TB):
                out.append(("o", BODY - 1, t))
            return out

        def passes(eng, run, before=None):
            with eng.Fori(0, E // 2 - 1) as p:
                if before:
                    before(p)
                for s in steps(False):
                    run(p, *s)
            for s in steps(True):
                run(E // 2 - 1, *s)

        with nc.Block() as block:
            @block.sync
            def _(sp):
                def load(e, half):
                    def at(w):
                        return w[bass.ds(e, 1)].rearrange("a (c p) n -> p (a c) n", p=P)
                    size = HC * MLP
                    sp.dma_start(stage[:, half, 0:size].rearrange("p (c n) -> p c n", c=HC), at(w0))\
                        .then_inc(loaded[half], 16)
                    sp.dma_start(stage[:, half, size:2 * size].rearrange("p (c n) -> p c n", c=HC), at(w1))\
                        .then_inc(loaded[half], 16)
                    sp.dma_start(stage[:, half, 2 * size:].rearrange("p (c n) -> p c n", c=MC), at(wo))\
                        .then_inc(loaded[half], 16)

                sp.dma_start(gate_sb[:], gate.rearrange("(c p) e -> p c e", p=P)).then_inc(gate_loaded, 16)
                load(0, 0)
                load(1, 1)
                with sp.Fori(0, E // 2 - 1) as p:
                    sp.wait_ge(w_lo, p * 8 + 4)
                    load(2 * p + 2, 0)
                    sp.wait_ge(w_lo, p * 8 + 8)
                    load(2 * p + 3, 1)

            @block.gpsimd
            def _(pool):
                for e in range(E):
                    pool.memset(iota[:, :, e:e + 1], float(e)).then_inc(consts, 1)
                pool.memset(minus_half[:], -0.5).then_inc(consts, 1)
                pool.memset(inter_f[:, 0, 0:1], 0.0).then_inc(i_lo, 2)
                pool.wait_ge(consts, E + 1)
                pool.wait_ge(var_ready, 1)
                pool.tensor_tensor(ln_rstd[:], ln_var[:], minus_half[:], ALU.pow).then_inc(rstd_ready, 1)
                pool.wait_ge(gate_hi, 1)
                pool.tensor_tensor(gate_w.lo[:], gate_sb[:], gate_w.hi[:].bitcast(F32), ALU.subtract)\
                    .then_inc(gate_lo, 1)

                def split_lo(p, half, j, count):
                    pool.wait_ge(w_hi, count)
                    at = slice(j * CH, (j + 1) * CH)
                    pool.tensor_tensor(W.lo[:, half, at], stage[:, half, at], W.hi[:, half, at].bitcast(F32),
                                       ALU.subtract).then_inc(w_lo, 1)

                for j in range(4):
                    split_lo(None, 0, j, j + 1)

                def run(p, what, g, i):
                    if what == "h":
                        k = g * MC + i
                        pool.wait_ge(i_hi, p * BODY * MC + (k + 1))
                        pool.tensor_tensor(inter.lo[:, g % 2, i, :], inter_f[:, k % 2, :],
                                           inter.hi[:, g % 2, i, :].bitcast(F32), ALU.subtract).then_inc(i_lo, 1)
                    elif what == "w":
                        split_lo(p, 1 - g, i, p * 8 + (4 * g + i + 5))

                passes(pool, run)

            @block.scalar
            def _(act):
                def copy_hi(n):
                    act.wait_ge(xt_full, n + 1)
                    c, q = n % HC, n // HC
                    act.activation(xnT.hi[:, c, q * BT:(q + 1) * BT], bank[O_BANKS[n % 4]][:], ACT.Copy)\
                        .then_inc(xt_hi, 1)

                def split_hi(half, j):
                    at = slice(j * CH, (j + 1) * CH)
                    act.activation(W.hi[:, half, at], stage[:, half, at], ACT.Copy).then_inc(w_hi, 1)

                act.wait_ge(gate_loaded, 16)
                act.activation(gate_w.hi[:], gate_sb[:], ACT.Copy).then_inc(gate_hi, 1)
                act.wait_ge(loaded[0], 48)
                for j in range(4):
                    split_hi(0, j)
                for n in range(HC * NB):
                    copy_hi(n)
                act.wait_ge(gap_ready, 1)
                act.activation(gap[:], gap[:], ACT.Exp).then_inc(gap_exp, 1)

                def run(p, what, g, i):
                    if what == "h":
                        k = g * MC + i
                        act.wait_ge(h_full, p * BODY * MC + (k + 1))
                        act.activation(sil[:, k % 2, :], bank[H_BANKS[k % 2][0]][:], ACT.Silu).then_inc(silu_done, 1)
                        act.wait_ge(inter_done, p * BODY * MC + (k + 3))
                        act.activation(inter.hi[:, g % 2, i, :], inter_f[:, k % 2, :], ACT.Copy).then_inc(i_hi, 1)
                    elif what == "w":
                        if i == 0:
                            act.wait_ge(loaded[1 - g], p * 48 + 48 * (1 + g))
                        split_hi(1 - g, i)

                passes(act, run)

            @block.vector
            def _(dve):
                for t in range(NT):
                    dve.bn_stats(ln_stats[:, t, :], x_all[:, t, :]).then_inc(stats_done, 1)
                dve.wait_ge(stats_done, NT)
                for t in range(NT):
                    dve.bn_aggr(ln_mv[:, t, :], ln_stats[:, t, :]).then_inc(stats_done, 1)
                dve.wait_ge(stats_done, 2 * NT)
                dve.tensor_scalar(ln_var[:], ln_mv[:, :, 1], EPS, None, ALU.add).then_inc(var_ready, 1)
                dve.wait_ge(rstd_ready, 1)

                def copy_lo(n):
                    c, q = n % HC, n // HC
                    dve.wait_ge(xt_hi, n + 1)
                    dve.tensor_tensor(xnT.lo[:, c, q * BT:(q + 1) * BT], bank[O_BANKS[n % 4]][:],
                                      xnT.hi[:, c, q * BT:(q + 1) * BT].bitcast(F32), ALU.subtract).then_inc(xt_lo, 1)

                for q in range(NB):
                    if q > 0:
                        dve.wait_ge(xt_full, HC * q)
                    for t in range(TB):
                        n = q * TB + t
                        dve.tensor_scalar(xn[:, t, :], x_all[:, n, :], ln_mv[:, n, 0:1], ln_rstd[:, n:n + 1],
                                          ALU.subtract, ALU.mult).then_inc(xn_ready, 1)
                    for c in range(HC):
                        copy_lo(q * HC + c)

                n = 0

                def wide(a):
                    return a[:].unsqueeze(2).to_broadcast([P, NT, E])

                def then(ins):
                    ins.then_inc(routed, 1)

                dve.wait_ge(consts, E + 1)
                dve.wait_ge(logits_full, 1)
                dve.tensor_copy(logits[:], bank["q"][:, 0:NT * E].rearrange("p (t e) -> p t e", e=E))\
                    .then_inc(routed, 1)
                for k in range(2):
                    r = 6 * k
                    dve.wait_ge(routed, r + 1)
                    dve.tensor_reduce(top[k][:], logits[:], AX_X, ALU.max).then_inc(routed, 1)
                    dve.wait_ge(routed, r + 2)
                    dve.tensor_tensor(work[:], logits[:], wide(top[k]), ALU.is_lt).then_inc(routed, 1)
                    dve.wait_ge(routed, r + 3)
                    dve.scalar_tensor_tensor(work[:], work[:], 1000.0, iota[:], ALU.mult, ALU.add).then_inc(routed, 1)
                    dve.wait_ge(routed, r + 4)
                    dve.tensor_reduce(chosen[:], work[:], AX_X, ALU.min).then_inc(routed, 1)
                    dve.wait_ge(routed, r + 5)
                    dve.tensor_tensor(onehot[k][:], iota[:], wide(chosen), ALU.is_equal).then_inc(routed, 1)
                    dve.wait_ge(routed, r + 6)
                    if k == 0:
                        dve.scalar_tensor_tensor(logits[:], onehot[0][:], NEVER, logits[:], ALU.mult, ALU.add)\
                            .then_inc(routed, 1)
                dve.tensor_tensor(gap[:], top[1][:], top[0][:], ALU.subtract).then_inc(gap_ready, 1)
                dve.wait_ge(gap_exp, 1)
                dve.tensor_scalar(wt[0][:], gap[:], 1.0, None, ALU.add).then_inc(routed, 1)
                dve.wait_ge(routed, 13)
                dve.reciprocal(wt[0][:], wt[0][:]).then_inc(routed, 1)
                dve.wait_ge(routed, 14)
                dve.tensor_tensor(wt[1][:], gap[:], wt[0][:], ALU.mult).then_inc(routed, 1)
                dve.tensor_tensor(comb[:], onehot[0][:], wide(wt[0]), ALU.mult).then_inc(routed, 1)
                dve.wait_ge(routed, 16)
                dve.tensor_tensor(work[:], onehot[1][:], wide(wt[1]), ALU.mult).then_inc(routed, 1)
                dve.wait_ge(routed, 17)
                dve.tensor_tensor(comb[:], comb[:], work[:], ALU.add).then_inc(routed, 1)
                dve.memset(sil[:, 1, 0:1], 0.0).then_inc(o_free, 4)
                dve.memset(sil[:, 0, 0:1], 0.0).then_inc(inter_done, 2)

                def run(p, what, g, i):
                    if what == "h":
                        k = g * MC + i
                        dve.wait_ge(i_lo, p * BODY * MC + (k + 1))
                        dve.wait_ge(silu_done, p * BODY * MC + (k + 1))
                        dve.tensor_tensor(inter_f[:, k % 2, :], bank[H_BANKS[k % 2][1]][:], sil[:, k % 2, :], ALU.mult)\
                            .then_inc(inter_done, 1)
                    elif what == "o":
                        n = g * TB + i
                        t = (g % NB) * TB + i
                        dve.wait_ge(o_full, p * BODY * TB + (n + 1))
                        dve.scalar_tensor_tensor(x_all[:, t, :], bank[O_BANKS[i]][:, 0:HID],
                                                 comb[:, t, bass.ds(2 * p + g // NB, 1)], x_all[:, t, :],
                                                 ALU.mult, ALU.add).then_inc(o_free, 1)

                passes(dve, run)

            @block.tensor
            def _(pe):
                for q in range(NB):
                    pe.wait_ge(xn_ready, (q + 1) * TB)
                    for c in range(HC):
                        n = q * HC + c
                        if n >= 4:
                            pe.wait_ge(xt_lo, n - 3)
                        for t in range(TB):
                            ins = pe.transpose(bank[O_BANKS[n % 4]][:, t * P:(t + 1) * P],
                                               xn[:, t, c * P:(c + 1) * P], ident[:])
                        ins.then_inc(xt_full, 1)
                pe.wait_ge(gate_lo, 1)
                pe.wait_ge(xt_lo, HC * NB)
                for t in range(NT):
                    for c in range(HC):
                        ins = mm3(pe, bank["q"][:, t * E:(t + 1) * E], xnT[:, c, t * P:(t + 1) * P], gate_w[:, c, :],
                                  c == 0, c == HC - 1)
                ins.then_inc(logits_full, 1)
                pe.wait_ge(routed, 1)
                pe.wait_ge(w_lo, 4)

                def run(p, what, g, i):
                    if what == "h":
                        k = g * MC + i
                        if i == 0 and g == NB:
                            pe.wait_ge(w_lo, p * 8 + 8)
                        elif i == 0 and g == 0:
                            pe.wait_ge(w_lo, p * 8 + 4)
                        pe.wait_ge(inter_done, p * BODY * MC + (k + 1))
                        e, tok = g // NB, slice((g % NB) * BT, (g % NB + 1) * BT)
                        for j, w in enumerate((w0_of, w1_of)):
                            for c in range(HC):
                                ins = mm3(pe, bank[H_BANKS[k % 2][j]][:], w(e, c, i), xnT[:, c, tok],
                                          c == 0, c == HC - 1)
                        ins.then_inc(h_full, 1)
                    elif what == "o":
                        if i == 0:
                            pe.wait_ge(i_lo, p * BODY * MC + (MC * (g + 1) + 2))
                        pe.wait_ge(o_free, p * BODY * TB + (g * TB + i + 1))
                        for m in range(MC):
                            ins = mm3(pe, bank[O_BANKS[i]][:, 0:HID], inter[:, g % 2, m, i * P:(i + 1) * P],
                                      wo_of(g // NB, m), m == 0, m == MC - 1)
                        ins.then_inc(o_full, 1)

                passes(pe, run)


def decoder_layer(nc, x, ctx_in, mask, w_qkv, w_proj, Wq, Wk, Wv, Wo, gate, w0, w1, wo, out):
    cm = Common()
    cm.x = x
    cm.B, cm.S, cm.HID = x.shape
    cm.HC = cm.HID // P
    cm.NT = cm.B * cm.S // P
    cm.PAIRS = cm.B // 2
    cm.TP = 2 * cm.S
    cm.TT = cm.TP // P
    with ExitStack() as ctx:
        cm.sems = ctx
        cm.bank = {n: ctx.enter_context(nc.psum_tensor("bank_" + n, [P, 512], F32))
                   for n in ("q", "t", "s0", "s1", "o0", "o1", "y0", "y1")}
        cm.x_all = ctx.enter_context(nc.sbuf_tensor("x_all", [P, cm.NT, cm.HID], F32))
        cm.ident = ctx.enter_context(nc.sbuf_tensor("ident", [P, P], F32))
        self_attention(nc, cm, w_qkv, w_proj)
        cross_attention(nc, cm, ctx_in, mask, Wq, Wk, Wv, Wo)
        feed_forward(nc, cm, gate, w0, w1, wo)
        stored = ctx.enter_context(nc.semaphore("stored"))
        with nc.Block() as block:
            @block.sync
            def _(sp):
                sp.dma_start(out.rearrange("b (t p) k -> p (b t) k", p=P), cm.x_all[:]).then_inc(stored, 16)
                sp.wait_ge(stored, 16)


_INS = ['x', 'ctx_1024', 'mask_BxS2_bf1', 'L0_attn_weight_qkv', 'L0_attn_weight_proj', 'L0_xattn_Wq', 'L0_xattn_Wk',
        'L0_xattn_Wv', 'L0_xattn_Wo', 'L0_ffn_gate_kernel', 'L0_ffn_w0_kernel', 'L0_ffn_w1_kernel',
        'L0_ffn_wo_kernel']
_OUTS = [((8, 256, 256), 'float32')]


def kernel(**inputs):
    import numpy as _np
    import concourse.bacc as _bacc
    from concourse import mybir as _mybir
    from concourse.bass_utils import run_bass_kernel_spmd as _run

    nc = _bacc.Bacc("TRN2", target_bir_lowering=False, num_devices=1)
    arrays, args = {}, []
    for name in _INS:
        a = _np.ascontiguousarray(inputs[name])
        if a.dtype.kind == "b":
            a = a.view(_np.uint8)
        arrays[f"in_{name}_dram"] = a
        args.append(nc.dram_tensor(f"in_{name}_dram", a.shape, _mybir.dt.from_np(a.dtype), kind="ExternalInput").ap())
    for i, (shape, dtype) in enumerate(_OUTS):
        dt = _mybir.dt.from_np(_np.dtype(dtype))
        args.append(nc.dram_tensor(f"out_{i}_dram", shape, dt, kind="ExternalOutput").ap())
    decoder_layer(nc, *args)
    r = _run(nc, [arrays], core_ids=[0])
    return r.results[0]["out_0_dram"]
```

```python
from contextlib import ExitStack

import concourse.bass as bass
from concourse import mybir

F32 = mybir.dt.float32
F32R = mybir.dt.float32r
BF16 = mybir.dt.bfloat16
I32 = mybir.dt.int32
U8 = mybir.dt.uint8
ALU = mybir.AluOpType
ACT = mybir.ActivationFunctionType
AX_X = mybir.AxisListType.X

P = 128
EPS = 1e-5
NEG = -1e30
BIG = 3e38


class Split:

    def __init__(self, hi, lo):
        self.hi, self.lo = hi, lo

    def __getitem__(self, at):
        return Split(self.hi[at], self.lo[at])

    def view(self, pattern, **sizes):
        return Split(self.hi.rearrange(pattern, **sizes), self.lo.rearrange(pattern, **sizes))


def mm3(pe, out, lhsT, rhs, first, last):
    pe.matmul(out, lhsT.hi, rhs.hi, start=first, stop=False, skip_group_check=True)
    pe.matmul(out, lhsT.hi, rhs.lo, start=False, stop=False, skip_group_check=True)
    return pe.matmul(out, lhsT.lo, rhs.hi, start=False, stop=last, skip_group_check=True)


class Uses:

    def __init__(self, first, body, quiet=()):
        self.full, self.freed, self.before = {}, {}, {}
        n, f, last = {}, {}, {}
        for part, steps in enumerate((first, body)):
            base_n, base_f = dict(n), dict(f)
            for name, bank in steps:
                key = (part, name)
                self.before[key] = last.get(bank)
                n[bank] = n.get(bank, 0) + 1
                f[bank] = f.get(bank, 0) + (name[0] not in quiet)
                self.full[key], self.freed[key] = n[bank], f[bank]
                last[bank] = name
            if part == 1:
                self.per_full = {b: n[b] - base_n.get(b, 0) for b in n}
                self.per_freed = {b: f[b] - base_f.get(b, 0) for b in f}
                self.last = last
        self.bank = {(part, name): bank for part, steps in enumerate((first, body)) for name, bank in steps}

    def count_full(self, p, name):
        if p is None:
            return self.full[0, name]
        return p * self.per_full[self.bank[1, name]] + self.full[1, name]

    def count_freed(self, p, name):
        if p is None:
            return self.freed[0, name]
        return p * self.per_freed[self.bank[1, name]] + self.freed[1, name]

    def bank_of(self, p, name):
        return self.bank[0 if p is None else 1, name]


class Common:
    pass


def self_attention(nc, cm, w_qkv, w_proj):
    B, S, HID, NT, D, HC = cm.B, cm.S, cm.HID, cm.NT, P, cm.HC
    NH = w_proj.shape[1] // D
    NKV = (w_qkv.shape[0] // D - NH) // 2
    QPG = NH // NKV
    NR = NH + 2 * NKV
    PAIRS, TP, TT = cm.PAIRS, cm.TP, cm.TT
    SCALE = float(D) ** -0.5
    UNITS = 2 * NH
    CW = P + 2 * P
    x_all, ident, bank = cm.x_all, cm.ident, cm.bank

    with ExitStack() as ctx:
        def sb(name, shape, dt=F32):
            return ctx.enter_context(nc.sbuf_tensor(name, shape, dt))

        def split(name, shape):
            return Split(sb(name + "_hi", shape, F32R), sb(name + "_lo", shape, F32R))

        def sem(name):
            return cm.sems.enter_context(nc.semaphore("a_" + name))

        causal = sb("causal", [P, CW])
        WqkvT = split("WqkvT", [P, HC, NR * D])
        WprojT = split("WprojT", [P, NH, HID])
        xn = sb("xn", [P, TT, HID])
        xnT = split("xnT", [P, HC, TP])
        kT = split("kT", [P, NKV, TP])
        v = split("v", [P, TT, NKV * D])
        qT = split("qT", [P, 2, TP])
        oT = split("oT", [P, 2, TP])
        pT = split("pT", [P, 2, CW])
        masked = sb("masked", [P, 2, CW])
        prob = sb("prob", [P, 3, CW])
        negmax = sb("negmax", [P, 4, 2])
        rowsum = sb("rowsum", [P, 4, 2])
        rinv = sb("rinv", [P, 4, 2])
        stage = sb("stage", [P, NR * HID])
        ln_stats = sb("ln_stats", [P, NT, 6])
        ln_mv = sb("ln_mv", [P, NT, 2])
        ln_var = sb("ln_var", [P, NT])
        ln_rstd = sb("ln_rstd", [P, NT])
        minus_half = sb("minus_half", [P, NT])

        full = {n: sem("full_" + n) for n in bank}
        half = {n: sem("half_" + n) for n in bank}
        free = {n: sem("free_" + n) for n in bank}
        x_loaded = sem("x_loaded")
        w_loaded = [sem(f"w_loaded{i}") for i in range(2)]
        ident_made = sem("ident_made")
        mask_made = sem("mask_made")
        stats_done = sem("stats_done")
        half_made = sem("half_made")
        var_ready = sem("var_ready")
        rstd_ready = sem("rstd_ready")
        xn_ready = sem("xn_ready")
        masked_ready = sem("masked_ready")
        exp_done = sem("exp_done")
        rinv_ready = sem("rinv_ready")
        prob_ready = sem("prob_ready")
        x_updated = sem("x_updated")

        setup_banks = ("q", "t", "s0", "s1", "o0")
        stage_qkv = stage[:].rearrange("p (r k) -> p r k", k=HID)
        stage_proj = stage[:, 0:2 * NH * D].rearrange("p (j e) -> p j e", j=2)
        fills = []
        for c in range(HC):
            for r in range(0, NR, 4):
                fills.append((WqkvT[:, c, r * P:(r + 4) * P],
                              [stage_qkv[:, r + i, c * P:(c + 1) * P] for i in range(4)]))
        QKV_FILLS = len(fills)
        for h in range(0, NH, 2):
            fills.append((WprojT[:, h:h + 2, :],
                          [stage_proj[:, i % 2, (h + i // 2) * P:(h + i // 2 + 1) * P] for i in range(4)]))
        setup = [(("w", i), setup_banks[i % len(setup_banks)]) for i in range(len(fills))]
        front = ([(("xt", c), "q") for c in range(HC)] + [(("k", g), ("q", "o0")[g % 2]) for g in range(NKV)]
                 + [(("v", t), ("s0", "s1")[t % 2]) for t in range(TT)] + [(("q", 0), "q")])
        body = []
        LAST = UNITS + 6
        for s in range(LAST):
            if s < UNITS:
                body.append((("scores", s), ("s0", "s1")[s % 2]))
                if s % 2 == 0 and s // 2 + 1 < NH:
                    body.append((("q", s // 2 + 1), "q"))
                if s >= 5 and s % 2 == 1 and (s - 5) // 2 < NH - 2:
                    body.append((("o", (s - 5) // 2), ("o0", "o1")[(s - 5) // 2 % 2]))
            if s >= 7 and s % 2 == 1 and (s - 7) // 2 < NH:
                body.append((("proj", (s - 7) // 2), None))
            if 0 <= s - 2 < UNITS:
                body.append((("t", s - 2), "t"))
            if 0 <= s - 3 < UNITS:
                body.append((("pv", s - 3), None))
                h = (s - 3) // 2
                if (s - 3) % 2 == 1 and h >= NH - 2:
                    body.append((("o", h), ("o0", "o1")[h % 2]))
            if 22 <= s < 22 + TT:
                body.append((("next_xn", s - 22), None))
            more = {29: front[0:1], 30: front[1:2], UNITS: front[2:4], UNITS + 1: front[4:6], UNITS + 2: front[6:8],
                    UNITS + 3: front[8:]}
            body += [(("next",) + name, b) for name, b in more.get(s, [])]
        body.append((("residual",), None))
        real = [(n, b) for n, b in body if b]
        uses = Uses(setup + front, [((n[1:] if n[0] == "next" else n), b) for n, b in real], quiet=("scores",))

        w_qkv_v = w_qkv.rearrange("(r p) k -> p r k", p=P)
        w_proj_v = w_proj.rearrange("(j p) e -> p j e", p=P)
        x_v = cm.x.rearrange("b (t p) k -> p (b t) k", p=P)

        def dst_of(name):
            what, i = name
            return {"w": lambda: (fills[i][0], 512), "xt": lambda: (xnT[:, i, :], TP), "k": lambda: (kT[:, i, :], TP),
                    "v": lambda: (v[:, i, :], NKV * D), "q": lambda: (qT[:, i % 2, :], TP),
                    "t": lambda: (pT[:, i % 2, :], CW), "o": lambda: (oT[:, i % 2, :], TP)}[what]()

        def passes(eng, run):
            with eng.Fori(0, PAIRS - 1) as p:
                for name, _ in body:
                    run(p, name)
            for name, _ in body:
                if not name[0].startswith("next"):
                    run(PAIRS - 1, name)

        with nc.Block() as block:

            @block.sync
            def _(sp):
                sp.dma_start(stage_qkv, w_qkv_v).then_inc(w_loaded[0], 16)
                sp.dma_start(x_all[:], x_v).then_inc(x_loaded, 16)
                at = ("w", QKV_FILLS - 1)
                sp.wait_ge(full[uses.bank_of(None, at)], uses.count_full(None, at))
                sp.dma_start(stage_proj, w_proj_v).then_inc(w_loaded[1], 16)

            @block.gpsimd
            def _(pool):
                pool.memset(ident[:], 0.0).then_inc(ident_made, 1)
                pool.memset(causal[:], 0.0).then_inc(mask_made, 1)
                pool.wait_ge(ident_made, 1)
                pool.affine_select(out=ident[:], in_=ident[:], compare_op=ALU.not_equal, fill=1.0, base=0,
                                   pattern=[[-1, P]], channel_multiplier=1).then_inc(ident_made, 1)
                pool.wait_ge(mask_made, 1)
                for at in (0, 2 * P):
                    pool.affine_select(out=causal[:, at:at + P], in_=causal[:, at:at + P], compare_op=ALU.is_ge,
                                       fill=NEG, base=0, pattern=[[-1, P]], channel_multiplier=1)\
                        .then_inc(mask_made, 1)
                pool.memset(minus_half[:], -0.5).then_inc(half_made, 1)
                pool.wait_ge(half_made, 1)
                pool.wait_ge(var_ready, 1)
                pool.tensor_tensor(ln_rstd[:], ln_var[:], minus_half[:], ALU.pow).then_inc(rstd_ready, 1)

                def run(p, name):
                    if name[0] != "scores":
                        return
                    u = name[1]
                    pool.wait_ge(rinv_ready, p * UNITS + (u + 1))
                    for i, (a, b) in enumerate(((0, P), (P, CW))):
                        pool.tensor_tensor(prob[:, u % 3, a:b], prob[:, u % 3, a:b],
                                           rinv[:, u % 4, i:i + 1].to_broadcast([P, b - a]), ALU.mult)\
                            .then_inc(prob_ready, 1)

                passes(pool, run)

            @block.scalar
            def _(act):
                def high(p, name):
                    n = uses.bank_of(p, name)
                    dst, width = dst_of(name)
                    act.wait_ge(full[n], uses.count_full(p, name))
                    act.activation(dst.hi, bank[n][:, 0:width], ACT.Copy).then_inc(half[n], 1)

                for name, _ in setup + front:
                    high(None, name)

                def run(p, name):
                    if name[0] == "next":
                        high(p, name[1:])
                    elif name[0] in ("q", "t") or name[0] == "o" and name[1] >= NH - 2:
                        high(p, name)
                    elif name[0] == "scores":
                        s = name[1]
                        if s >= 5 and s % 2 == 1:
                            high(p, ("o", (s - 5) // 2))
                        act.wait_ge(masked_ready, p * 2 * UNITS + 2 * (s + 1))
                        for i, (a, b) in enumerate(((0, P), (P, CW))):
                            act.activation(prob[:, s % 3, a:b], masked[:, s % 2, a:b], ACT.Exp, scale=-1.0,
                                           bias=negmax[:, s % 4, i:i + 1],
                                           accum_out=rowsum[:, s % 4, i:i + 1]).then_inc(exp_done, 1)

                passes(act, run)

            @block.vector
            def _(dve):
                def low(p, name):
                    n = uses.bank_of(p, name)
                    dst, width = dst_of(name)
                    src = bank[n][:, 0:width]
                    if len(dst.lo.shape) == 3:
                        src = src.rearrange("p (a b) -> p a b", a=dst.lo.shape[1])
                    dve.wait_ge(half[n], uses.count_freed(p, name))
                    dve.tensor_tensor(dst.lo, src, dst.hi.bitcast(F32), ALU.subtract).then_inc(free[n], 1)

                def normalize(p, t):
                    xt = x_all[:, bass.ds(p * TT + t, 1), :].rearrange("p a k -> p (a k)")
                    mu = ln_mv[:, bass.ds(p * TT + t, 1), 0]
                    rs = ln_rstd[:, bass.ds(p * TT + t, 1)]
                    dve.tensor_scalar(xn[:, t, :], xt, mu, rs, ALU.subtract, ALU.mult).then_inc(xn_ready, 1)

                def invert(p, s):
                    dve.wait_ge(exp_done, p * 2 * UNITS + 2 * (s + 1))
                    dve.reciprocal(rinv[:, s % 4, :], rowsum[:, s % 4, :]).then_inc(rinv_ready, 1)

                dve.wait_ge(x_loaded, 16)
                for t in range(NT):
                    dve.bn_stats(ln_stats[:, t, :], x_all[:, t, :]).then_inc(stats_done, 1)
                for t in range(NT):
                    dve.wait_ge(stats_done, t + 1)
                    dve.bn_aggr(ln_mv[:, t, :], ln_stats[:, t, :]).then_inc(stats_done, 1)
                dve.wait_ge(stats_done, 2 * NT)
                dve.tensor_scalar(ln_var[:], ln_mv[:, :, 1], EPS, None, ALU.add).then_inc(var_ready, 1)
                for name, _ in setup:
                    low(None, name)
                dve.wait_ge(rstd_ready, 1)
                for t in range(TT):
                    normalize(0, t)
                for name, _ in front:
                    low(None, name)
                dve.wait_ge(mask_made, 3)

                def run(p, name):
                    if name[0] == "next":
                        low(p, name[1:])
                    elif name[0] == "next_xn":
                        normalize(p + 1, name[1])
                    elif name[0] in ("q", "o"):
                        low(p, name)
                    elif name[0] == "scores":
                        s = name[1]
                        n = uses.bank_of(p, name)
                        dve.wait_ge(full[n], uses.count_full(p, name))
                        if s == 0:
                            dve.tensor_copy(rinv[:, 3, :], ident[:, 0:2])
                        else:
                            invert(p, s - 1)
                        for i, (a, b) in enumerate(((0, P), (P, CW))):
                            dve.tensor_tensor_reduce(masked[:, s % 2, a:b], bank[n][:, a:b], causal[:, a:b],
                                                     -SCALE, BIG, ALU.add, ALU.min, negmax[:, s % 4, i:i + 1])\
                                .then_inc(masked_ready, 1)
                    elif name[0] == "t":
                        low(p, name)
                    elif name[0] == "residual":
                        for j, n in enumerate(("y0", "y1")):
                            dve.wait_ge(full[n], p + 1)
                            xt = x_all[:, bass.ds(p * TT + 2 * j, 2), :]
                            dve.tensor_tensor(xt, bank[n][:].rearrange("p (t k) -> p t k", t=2), xt, ALU.add)\
                                .then_inc(x_updated, 1)
                    if name == ("t", UNITS - 3):
                        invert(p, UNITS - 1)

                passes(dve, run)

            @block.tensor
            def _(pe):
                def wait_free(p, name):
                    n = uses.bank_of(p, name)
                    before = uses.before[0 if p is None else 1, name]
                    if before is None:
                        return
                    if before[0] == "scores":
                        pe.wait_ge(masked_ready, p * 2 * UNITS + 2 * (before[1] + 1))
                    else:
                        pe.wait_ge(free[n], uses.count_freed(p, name) - (name[0] != "scores"))

                def fill(p, name):
                    what, i = name
                    n = uses.bank_of(p, name)
                    wait_free(p, name)
                    if what == "w":
                        for j, src in enumerate(fills[i][1]):
                            ins = pe.transpose(bank[n][:, j * P:(j + 1) * P], src, ident[:])
                    elif what == "xt":
                        for t in range(TT):
                            ins = pe.transpose(bank[n][:, t * P:(t + 1) * P], xn[:, t, i * P:(i + 1) * P], ident[:])
                    elif what == "v":
                        for c in range(HC):
                            wv = WqkvT.view("p c (g i d) -> p c g i d", g=NKV, d=D)[:, c, :, QPG + 1, :]
                            ins = mm3(pe, bank[n][:].rearrange("p (g d) -> p g d", g=NKV),
                                      xnT[:, c, i * P:(i + 1) * P], wv, c == 0, c == HC - 1)
                    else:
                        col = {"k": (i * (QPG + 2) + QPG) * D, "q": ((i // QPG) * (QPG + 2) + i % QPG) * D}[what]
                        for c in range(HC):
                            ins = mm3(pe, bank[n][:], WqkvT[:, c, col:col + D], xnT[:, c, :], c == 0, c == HC - 1)
                    ins.then_inc(full[n], 1)

                def wait_copied(p, name):
                    pe.wait_ge(free[uses.bank_of(p, name)], uses.count_freed(p, name))

                pe.wait_ge(ident_made, 2)
                for name, _ in setup:
                    if name == ("w", 0):
                        pe.wait_ge(w_loaded[0], 16)
                    if name == ("w", QKV_FILLS):
                        pe.wait_ge(w_loaded[1], 16)
                    fill(None, name)
                for name, _ in setup[-len(setup_banks):]:
                    wait_copied(None, name)
                pe.wait_ge(xn_ready, TT)
                for name, _ in front:
                    if name == ("k", 0):
                        wait_copied(None, ("xt", 0))
                        wait_copied(None, ("xt", 1))
                    fill(None, name)
                for name, _ in front[HC:]:
                    wait_copied(None, name)

                def run(p, name):
                    what = name[0]
                    if what == "next":
                        if name == ("next", "xt", 0):
                            pe.wait_ge(xn_ready, p * TT + 2 * TT)
                        if name == ("next", "k", 0):
                            wait_copied(p, ("xt", 0))
                            wait_copied(p, ("xt", 1))
                        fill(p, name[1:])
                        if name == ("next", "q", 0):
                            for other, _ in front[HC:-1]:
                                wait_copied(p, other)
                    elif what == "q":
                        fill(p, name)
                    elif what == "scores":
                        u = name[1]
                        h, b = u // 2, u % 2
                        g = h // QPG
                        n = uses.bank_of(p, name)
                        wait_free(p, name)
                        if b == 0 and h > 0:
                            wait_copied(p, ("q", h))
                        if u == 0:
                            pe.wait_ge(free["q"], uses.count_freed(p, ("q", 1)) - 1)
                        mm3(pe, bank[n][:, 0:P], qT[:, h % 2, b * S:b * S + P], kT[:, g, b * S:b * S + P], True, True)
                        mm3(pe, bank[n][:, P:CW], qT[:, h % 2, b * S + P:b * S + S], kT[:, g, b * S:b * S + S],
                            True, True).then_inc(full[n], 1)
                    elif what == "t":
                        u = name[1]
                        pe.wait_ge(prob_ready, p * 2 * UNITS + 2 * (u + 1))
                        wait_free(p, name)
                        for j in range(3):
                            ins = pe.transpose(bank["t"][:, j * P:(j + 1) * P], prob[:, u % 3, j * P:(j + 1) * P],
                                               ident[:])
                        ins.then_inc(full["t"], 1)
                    elif what == "pv":
                        u = name[1]
                        h, b = u // 2, u % 2
                        g = h // QPG
                        wait_copied(p, ("t", u))
                        if b == 0:
                            wait_free(p, ("o", h))
                        n = uses.bank_of(p, ("o", h))
                        vg = v[:, :, g * D:(g + 1) * D]
                        mm3(pe, bank[n][:, b * S:b * S + S], vg[:, 2 * b, :], pT[:, u % 2, 0:S], True, False)
                        ins = mm3(pe, bank[n][:, b * S + P:b * S + S], vg[:, 2 * b + 1, :], pT[:, u % 2, S:CW],
                                  False, True)
                        if b == 1:
                            ins.then_inc(full[n], 1)
                    elif what == "proj":
                        h = name[1]
                        wait_copied(p, ("o", h))
                        for t in range(TT):
                            y = ("y0", "y1")[t // 2]
                            ins = mm3(pe, bank[y][:, (t % 2) * HID:(t % 2 + 1) * HID],
                                      oT[:, h % 2, t * P:(t + 1) * P], WprojT[:, h, :],
                                      h == 0 and t % 2 == 0, h == NH - 1)
                            if h == NH - 1 and t % 2 == 1:
                                ins.then_inc(full[y], 1)

                passes(pe, run)


class Order:

    def __init__(self, first, body):
        self.at, last, n = {}, {}, {}
        for part, steps in enumerate((first, body)):
            base = {k: tuple(v) for k, v in n.items()}
            for name, bank, who in steps:
                c = n.setdefault(bank, [0, 0, 0])
                c[0] += 1
                c[1] += who == "both"
                c[2] += who != ""
                self.at[part, name] = (bank, tuple(c), last.get(bank), who)
                last[bank] = name
        self.per = {k: tuple(b - a for a, b in zip(base.get(k, (0, 0, 0)), v)) for k, v in n.items()}

    def _count(self, p, name, which):
        bank, c, _, _ = self.at[0 if p is None else 1, name]
        return c[which] if p is None else p * self.per[bank][which] + c[which]

    def bank(self, p, name):
        return self.at[0 if p is None else 1, name][0]

    def who(self, p, name):
        return self.at[0 if p is None else 1, name][3]

    def full(self, p, name):
        return self._count(p, name, 0)

    def half(self, p, name):
        return self._count(p, name, 1)

    def free(self, p, name):
        return self._count(p, name, 2)

    def before(self, p, name):
        return self.at[0 if p is None else 1, name][2]


def cross_attention(nc, cm, ctx_in, mask, Wq, Wk, Wv, Wo):
    HID, NT, HC, PAIRS, TP, TT, S = cm.HID, cm.NT, cm.HC, cm.PAIRS, cm.TP, cm.TT, cm.S
    D = P
    S2, DV = ctx_in.shape[1:]
    NH = Wq.shape[1] // D
    NG = Wk.shape[1] // D
    KP = 2 * S2
    SCALE = float(D) ** -0.5
    HALF = NH // 2 * S2
    NJ = NH * S2 // P
    x_all, ident, bank = cm.x_all, cm.ident, cm.bank

    with ExitStack() as ctx:
        def sb(name, shape, dt=F32, at=ctx):
            return at.enter_context(nc.sbuf_tensor("b_" + name, shape, dt))

        def split(name, shape):
            return Split(sb(name + "_hi", shape, F32R), sb(name + "_lo", shape, F32R))

        def sem(name):
            return cm.sems.enter_context(nc.semaphore("b_" + name))

        WqT = sb("WqT", [P, NH, HID])
        wk = sb("wk", [P, NG * D])
        wv = sb("wv", [P, NG * D])
        wo = sb("wo", [P, NH, HID])
        ctxT = sb("ctxT", [P, PAIRS * KP])
        kT = sb("kT", [P, NG, KP])
        vT = sb("vT", [P, NG, KP])
        xn = sb("xn", [P, TT, HID])
        xnT = split("xnT", [P, HC, TP])
        M = split("M", [P, HC, 2, NH, S2])
        VW = split("VW", [P, NG, 2, HID])
        prob = sb("prob", [P, 2, NH * S2])
        pT = split("pT", [P, 2, NJ, P])
        rowmax = sb("rowmax", [P, 2, NH])
        rowsum = sb("rowsum", [P, 2, NH])
        rinv = sb("rinv", [P, 2, NH])
        ln_stats = sb("ln_stats", [P, TT, 6])
        ln_mv = sb("ln_mv", [P, 2, TT, 2])
        ln_var = sb("ln_var", [P, TT])
        ln_rstd = sb("ln_rstd", [P, 2, TT])
        minus_half = sb("minus_half", [P, TT])
        mask_u8 = sb("mask_u8", [1, PAIRS * KP], U8)
        mask_bf = sb("mask_bf", [1, PAIRS * KP], BF16)
        bias_bf = sb("bias_bf", [1, PAIRS * KP], BF16)
        ones_bf = sb("ones_bf", [1, P], BF16)
        keep = sb("keep", [P, PAIRS])
        with ExitStack() as early:
            stage = sb("stage", [P, HC, NH * D], at=early)
            ctx_sb = sb("ctx", [P, PAIRS, DV], at=early)
        VWs = split("VWs", [P, NG, 2 * HID])

        full = {n: sem("full_" + n) for n in bank}
        half = {n: sem("half_" + n) for n in bank}
        free = {n: sem("free_" + n) for n in bank}
        small_loaded = sem("small_loaded")
        wq_loaded = sem("wq_loaded")
        kv_loaded = sem("kv_loaded")
        wo_loaded = sem("wo_loaded")
        consts = sem("consts")
        mask_ready = sem("mask_ready")
        ctx_masked = sem("ctx_masked")
        stats_done = sem("stats_done")
        var_ready = sem("var_ready")
        rstd_ready = sem("rstd_ready")
        xn_ready = sem("xn_ready")
        max_ready = sem("max_ready")
        shifted = sem("shifted")
        exp_done = sem("exp_done")
        sum_ready = sem("sum_ready")
        rinv_ready = sem("rinv_ready")
        prob_ready = sem("prob_ready")
        VW_moved = sem("VW_moved")
        y_added = sem("y_added")

        setup = [(("keep", 0), "y0", "dve")] + \
                [(("w", i), ("q", "t", "s0", "s1")[i % 4], ("act", "dve")[i % 2]) for i in range(NH * HC // 4)] + \
                [(("ctx", 0), "o0", "act")]
        rot = ("q", "t", "s0", "s1")
        front = [(("xt", c), ("q", "t")[c], "both") for c in range(HC)]
        front += [(("k", i), ("s0", "s1")[i], "act") for i in range(2)]
        front += [(("v", i), ("q", "t")[i], "act") for i in range(2)]
        front += [(("m", i), rot[(i + 2) % 4], "both") for i in range(NH // 4 * HC)]

        def s_step(t):
            return [(("s", t, j), (("q", "t"), ("s0", "s1"))[t % 2][j], "") for j in range(2)]

        def t_step(t):
            return [(("t", t, j), ("o0", "o1")[j], "both") for j in range(2)]

        def vw_step(gs):
            return [(("vw", g), ("y1", "o0", "o1")[g % 3], "both") for g in gs]

        def y_step(t):
            return [(("y", t), "y0", "")]

        def quiet(*name):
            return [(name, None, "")]

        nxt = [(("next",) + n, b, w) for n, b, w in front]
        body = (s_step(0) + vw_step((0, 1)) + s_step(1) + quiet("sum", 0) + vw_step((2, 3)) + quiet("move", 0)
                + vw_step((4, 5)) + quiet("sum", 1) + vw_step((6, 7)) + quiet("move", 1)
                + t_step(0) + s_step(2) + y_step(0) + quiet("next_ln", 0) + quiet("sum", 2) + t_step(1) + s_step(3)
                + y_step(1) + quiet("next_xn", 0) + quiet("sum", 3)
                + t_step(2) + nxt[0:2] + y_step(2) + nxt[2:6] + nxt[6:10] + t_step(3) + nxt[10:] + y_step(3))
        order = Order(setup + front, [((n[1:] if n[0] == "next" else n), b, w) for n, b, w in body if b])

        def dst_of(name):
            what, i = name[0], name[1]
            n = name_bank[name]
            b = bank[n][:]
            if what == "w":
                return WqT[:, 2 * i:2 * i + 2, :], b.rearrange("p (h k) -> p h k", h=2)
            if what == "ctx":
                return ctxT[:], b
            if what == "xt":
                return xnT[:, i, :], b
            if what in ("k", "v"):
                return {"k": kT, "v": vT}[what][:, 4 * i:4 * i + 4, :], b.rearrange("p (g k) -> p g k", g=4)
            if what == "m":
                h, c = 4 * (i // HC), i % HC
                return (M[:, c, :, h:h + 4, :].view("p b h s -> p h b s"),
                        b.rearrange("p (h b s) -> p h b s", h=4, b=2))
            if what == "vw":
                return VWs[:, i, :], b
            if what == "t":
                return (pT[:, i % 2, 4 * name[2]:4 * name[2] + 4, :], b.rearrange("p (j q) -> p j q", j=4))

        name_bank = {name: b for name, b, _ in setup + front}
        name_bank.update({(n[1:] if n[0] == "next" else n): b for n, b, _ in body if b})

        def passes(eng, run):
            with eng.Fori(0, PAIRS - 1) as p:
                for name, _, _ in body:
                    run(p, name)
            for name, _, _ in body:
                if not name[0].startswith("next"):
                    run(PAIRS - 1, name)

        with nc.Block() as block:

            @block.sync
            def _(sp):
                sp.dma_start(mask_u8[:], mask.rearrange("(a b) s -> a (b s)", a=1)).then_inc(small_loaded, 16)
                sp.dma_start(ctx_sb[:], ctx_in.rearrange("(p b) s d -> (b s) p d", b=2)).then_inc(small_loaded, 16)
                sp.dma_start(stage[:], Wq.rearrange("(c p) n -> p c n", p=P)).then_inc(wq_loaded, 16)
                sp.dma_start(wk[:], Wk).then_inc(kv_loaded, 16)
                sp.dma_start(wv[:], Wv).then_inc(kv_loaded, 16)
                sp.dma_start(wo[:], Wo.rearrange("(h p) n -> p h n", p=P)).then_inc(wo_loaded, 16)

                def run(p, name):
                    if name[0] != "move":
                        return
                    g0 = NG // 2 * name[1]
                    at = ("vw", g0 + 3)
                    sp.wait_ge(free[order.bank(p, at)], order.free(p, at))
                    for src, dst in ((VWs.hi, VW.hi), (VWs.lo, VW.lo)):
                        for b in range(2):
                            for h in range(2):
                                sp.dma_start(dst[h * S2:(h + 1) * S2, g0:g0 + 4, b, :].bitcast(F32),
                                             src[b * S2:(b + 1) * S2, g0:g0 + 4, h * HID:(h + 1) * HID].bitcast(F32))\
                                    .then_inc(VW_moved, 16)

                passes(sp, run)

            @block.gpsimd
            def _(pool):
                pool.memset(minus_half[:], -0.5).then_inc(consts, 1)
                pool.memset(ones_bf[:], 1.0).then_inc(consts, 1)

                def power(count, slot):
                    pool.wait_ge(consts, 2)
                    pool.wait_ge(var_ready, count)
                    pool.tensor_tensor(ln_rstd[:, slot, :], ln_var[:], minus_half[:], ALU.pow).then_inc(rstd_ready, 1)

                power(1, 0)

                def run(p, name):
                    if name[0] == "next_ln":
                        power(p + 2, 0)
                    if name[0] == "sum":
                        t = name[1]
                        pool.wait_ge(rinv_ready, p * TT + (t + 1))
                        pr = prob[:, t % 2, :].rearrange("p (h s) -> p h s", s=S2)
                        pool.tensor_tensor(pr, pr, rinv[:, t % 2, :].unsqueeze(2).to_broadcast([P, NH, S2]), ALU.mult)\
                            .then_inc(prob_ready, 1)

                passes(pool, run)

            @block.scalar
            def _(act):
                def copy_out(p, name):
                    who = order.who(p, name)
                    if who in ("both", "act"):
                        n = order.bank(p, name)
                        dst, src = dst_of(name)
                        act.wait_ge(full[n], order.full(p, name))
                        act.activation(dst.hi if who == "both" else dst, src, ACT.Copy)\
                            .then_inc(half[n] if who == "both" else free[n], 1)

                for name, _, _ in setup + front:
                    copy_out(None, name)

                def run(p, name):
                    if name[0] == "next":
                        copy_out(p, name[1:])
                    elif name[0] in ("vw", "t"):
                        copy_out(p, name)
                    elif name[0] == "sum":
                        t = name[1]
                        act.wait_ge(shifted, p * 2 * TT + 2 * (t + 1))
                        act.activation(prob[:, t % 2, :], prob[:, t % 2, :], ACT.Exp, scale=SCALE)\
                            .then_inc(exp_done, 1)

                passes(act, run)

            @block.vector
            def _(dve):
                def copy_out(p, name):
                    who = order.who(p, name)
                    n = order.bank(p, name)
                    if who == "both":
                        dst, src = dst_of(name)
                        dve.wait_ge(half[n], order.half(p, name))
                        dve.tensor_tensor(dst.lo, src, dst.hi.bitcast(F32), ALU.subtract).then_inc(free[n], 1)
                    elif who == "dve":
                        dst, src = dst_of(name)
                        dve.wait_ge(full[n], order.full(p, name))
                        dve.tensor_copy(dst, src).then_inc(free[n], 1)

                def tile(p, t):
                    return x_all[:, bass.ds(p * TT + t, 1), :].rearrange("p a k -> p (a k)")

                def layer_norm_stats(p, q):
                    for t in range(TT):
                        dve.bn_stats(ln_stats[:, t, :], tile(p, t)).then_inc(stats_done, 1)
                    dve.wait_ge(stats_done, q * 2 * TT + TT)
                    dve.tensor_copy(ln_var[:, 0:1], ln_stats[:, 0, 0:1])
                    for t in range(TT):
                        dve.bn_aggr(ln_mv[:, 0, t, :], ln_stats[:, t, :]).then_inc(stats_done, 1)
                    dve.wait_ge(stats_done, q * 2 * TT + 2 * TT)
                    dve.tensor_scalar(ln_var[:], ln_mv[:, 0, :, 1], EPS, None, ALU.add).then_inc(var_ready, 1)

                def normalize(p, q):
                    dve.wait_ge(rstd_ready, q + 1)
                    for t in range(TT):
                        dve.tensor_scalar(xn[:, t, :], tile(p, t), ln_mv[:, 0, t, 0:1], ln_rstd[:, 0, t:t + 1],
                                          ALU.subtract, ALU.mult).then_inc(xn_ready, 1)

                layer_norm_stats(0, 0)
                dve.wait_ge(small_loaded, 32)
                dve.tensor_copy(mask_bf[:], mask_u8[:]).then_inc(mask_ready, 1)
                dve.wait_ge(mask_ready, 1)
                dve.tensor_scalar(bias_bf[:], mask_bf[:], -1.0, -NEG, ALU.add, ALU.mult).then_inc(mask_ready, 1)
                dve.wait_ge(full["y0"], 1)
                dve.tensor_copy(keep[:], bank["y0"][:, 0:PAIRS]).then_inc(free["y0"], 1)
                dve.wait_ge(free["y0"], 1)
                for p in range(PAIRS):
                    dve.tensor_scalar(ctx_sb[:, p, :], ctx_sb[:, p, :], keep[:, p:p + 1], None, ALU.mult)\
                        .then_inc(ctx_masked, 1)
                normalize(0, 0)
                for name, _, _ in setup[1:] + front:
                    copy_out(None, name)

                def run(p, name):
                    if name[0] == "next":
                        copy_out(p, name[1:])
                    elif name[0] in ("vw", "t"):
                        copy_out(p, name)
                    elif name[0] == "next_ln":
                        layer_norm_stats(p + 1, p + 1)
                    elif name[0] == "next_xn":
                        normalize(p + 1, p + 1)
                    elif name[0] == "s" and name[2] == 1:
                        t = name[1]
                        heads = NH // 2
                        banks = [bank[order.bank(p, ("s", t, j))][:].rearrange("p (h s) -> p h s", s=S2)
                                 for j in range(2)]
                        for j in range(2):
                            n = order.bank(p, ("s", t, j))
                            dve.wait_ge(full[n], order.full(p, ("s", t, j)))
                            dve.tensor_reduce(rowmax[:, t % 2, j * heads:(j + 1) * heads], banks[j], AX_X, ALU.max)\
                                .then_inc(max_ready, 1)
                        if t >= 2:
                            for j in range(2):
                                n = order.bank(p, ("t", t - 2, j))
                                dve.wait_ge(full[n], order.full(p, ("t", t - 2, j)))
                        for j in range(2):
                            n = order.bank(p, ("s", t, j))
                            dve.wait_ge(max_ready, p * 2 * TT + (2 * t + j + 1))
                            dve.tensor_tensor(
                                prob[:, t % 2, j * HALF:(j + 1) * HALF].rearrange("p (h s) -> p h s", s=S2), banks[j],
                                rowmax[:, t % 2, j * heads:(j + 1) * heads].unsqueeze(2).to_broadcast([P, heads, S2]),
                                ALU.subtract).then_inc(shifted, 1)
                    elif name[0] == "sum":
                        t = name[1]
                        dve.wait_ge(exp_done, p * TT + (t + 1))
                        dve.tensor_reduce(rowsum[:, t % 2, :], prob[:, t % 2, :].rearrange("p (h s) -> p h s", s=S2),
                                          AX_X, ALU.add).then_inc(sum_ready, 1)
                        dve.wait_ge(sum_ready, p * TT + (t + 1))
                        dve.reciprocal(rinv[:, t % 2, :], rowsum[:, t % 2, :]).then_inc(rinv_ready, 1)
                    elif name[0] == "y":
                        t = name[1]
                        dve.wait_ge(full["y0"], order.full(p, name))
                        dve.tensor_tensor(tile(p, t), bank["y0"][:, 0:HID], tile(p, t), ALU.add)\
                            .then_inc(y_added, 1)

                passes(dve, run)

            @block.tensor
            def _(pe):
                def wait_free(p, name):
                    n = order.bank(p, name)
                    if order.before(p, name) is None:
                        return
                    before = order.before(p, name)
                    if before[0] == "s":
                        pe.wait_ge(shifted, p * 2 * TT + (2 * before[1] + before[2] + 1))
                    elif name[0] == "y":
                        if name[1] > 0:
                            pe.wait_ge(y_added, p * TT + name[1])
                    else:
                        pe.wait_ge(free[n], order.free(p, name) - (order.who(p, name) != ""))

                def wait_copied(p, name):
                    n = order.bank(p, name)
                    pe.wait_ge(free[n], order.free(p, name))

                def fill(p, name):
                    what, i = name[0], name[1]
                    n = order.bank(p, name)
                    wait_free(p, name)
                    if what == "w":
                        for j in range(4):
                            h, c = 2 * i + j // 2, j % 2
                            ins = pe.transpose(bank[n][:, j * P:(j + 1) * P], stage[:, c, h * P:(h + 1) * P], ident[:])
                    elif what == "ctx":
                        for j in range(PAIRS):
                            ins = pe.transpose(bank[n][:, j * P:(j + 1) * P], ctx_sb[:, j, :], ident[:])
                    elif what == "xt":
                        for t in range(TT):
                            ins = pe.transpose(bank[n][:, t * P:(t + 1) * P], xn[:, t, i * P:(i + 1) * P], ident[:])
                    elif what in ("k", "v"):
                        w = {"k": wk, "v": wv}[what]
                        q = 0 if p is None else p + 1
                        for j in range(4):
                            g = 4 * i + j
                            ins = pe.matmul(bank[n][:, j * P:(j + 1) * P], w[:, g * D:(g + 1) * D],
                                            ctxT[:, bass.ds(q * KP, KP)], start=True, stop=True,
                                            skip_group_check=True)
                    elif what == "m":
                        for j in range(4):
                            h, c = 4 * (i // HC) + j, i % HC
                            ins = pe.matmul(bank[n][:, j * P:(j + 1) * P], WqT[:, h, c * P:(c + 1) * P],
                                            kT[:, h // 2, :], start=True, stop=True, skip_group_check=True)
                    elif what == "vw":
                        ins = pe.matmul(bank[n][:], vT[:, i, :], wo[:, 2 * i:2 * i + 2, :].rearrange("p h n -> p (h n)"),
                                        start=True, stop=True, skip_group_check=True)
                    ins.then_inc(full[n], 1)

                pe.wait_ge(mask_ready, 2)
                pe.wait_ge(consts, 2)
                for p in range(PAIRS):
                    ins = pe.matmul(bank["y0"][:, p:p + 1], mask_bf[:, p * KP:(p + 1) * KP], ones_bf[:, 0:1],
                                    start=True, stop=True, skip_group_check=True)
                ins.then_inc(full["y0"], 1)
                pe.wait_ge(wq_loaded, 16)
                for name, _, _ in setup[1:]:
                    if name[0] == "ctx":
                        pe.wait_ge(ctx_masked, PAIRS)
                    fill(None, name)
                for name, _, _ in setup[-5:]:
                    wait_copied(None, name)

                def needs(p, name):
                    q = 0 if p is None else p + 1
                    if name == ("xt", 0):
                        pe.wait_ge(xn_ready, q * TT + TT)
                    if name == ("k", 0) and p is None:
                        pe.wait_ge(kv_loaded, 32)
                    if name == ("m", 0):
                        wait_copied(p, ("k", 0))
                        wait_copied(p, ("k", 1))

                for name, _, _ in front:
                    needs(None, name)
                    fill(None, name)
                pe.wait_ge(wo_loaded, 16)

                def run(p, name):
                    what = name[0]
                    if what == "next":
                        needs(p, name[1:])
                        fill(p, name[1:])
                    elif what == "s":
                        t, j = name[1], name[2]
                        n = order.bank(p, name)
                        if t == 0 and j == 0:
                            for other, b, _ in front[-4:]:
                                pe.wait_ge(free[b], p * order.per[b][2] + order.free(None, other))
                        wait_free(p, name)
                        b = t // 2
                        for c in range(HC):
                            mm3(pe, bank[n][:], xnT[:, c, t * P:(t + 1) * P],
                                M[:, c, b, 8 * j:8 * j + 8, :].view("p h s -> p (h s)"), c == 0, False)
                        bias = bias_bf[:, bass.ds(p * KP + b * S2, S2)].unsqueeze(1).to_broadcast([1, NH // 2, S2])
                        pe.matmul(bank[n][:].rearrange("p (h s) -> p h s", s=S2), ones_bf[:, :], bias,
                                  start=False, stop=True, skip_group_check=True).then_inc(full[n], 1)
                    elif what == "vw":
                        fill(p, name)
                    elif what == "t":
                        t, j = name[1], name[2]
                        n = order.bank(p, name)
                        wait_free(p, name)
                        pe.wait_ge(prob_ready, p * TT + (t + 1))
                        for i in range(4):
                            at = (4 * j + i) * P
                            ins = pe.transpose(bank[n][:, i * P:(i + 1) * P], prob[:, t % 2, at:at + P], ident[:])
                        ins.then_inc(full[n], 1)
                    elif what == "y":
                        t = name[1]
                        b = t // 2
                        wait_free(p, name)
                        for j in range(2):
                            wait_copied(p, ("t", t, j))
                        if t == 0:
                            pe.wait_ge(VW_moved, p * 256 + 256)
                        for j in range(NJ):
                            ins = mm3(pe, bank["y0"][:, 0:HID], pT[:, t % 2, j, :], VW[:, j, b, :],
                                      j == 0, j == NJ - 1)
                        ins.then_inc(full["y0"], 1)

                passes(pe, run)


def feed_forward(nc, cm, gate, w0, w1, wo, rows_in, rows_out, out):
    E, HID, MLP = w0.shape
    NT, HC = cm.NT, cm.HC
    MC = MLP // P
    GT = 4
    NG = NT // GT
    TILES = rows_in.shape[0] // P
    NEVER = -3e38
    WN = HC * MLP
    x_all, ident, bank = cm.x_all, cm.ident, cm.bank
    H0_BANKS, H1_BANKS, XT_BANK, IT_BANK, Y_BANK = ("q", "t"), ("s0", "s1"), "o0", "o1", "y0"
    GATHERED = 6

    def sem(name):
        return cm.sems.enter_context(nc.semaphore("c_" + name))

    with ExitStack() as ctx:
        def sb(name, shape, dt=F32, scope=ctx):
            return scope.enter_context(nc.sbuf_tensor("f_" + name, shape, dt))

        W = Split(sb("W_hi", [P, 2 * E, WN], F32R), sb("W_lo", [P, 2 * E, WN], F32R))
        Wo = sb("Wo", [P, E, MC, HID])
        pos = [sb("pos%d" % k, [P, NT], I32) for k in range(2)]
        weight = [sb("weight%d" % k, [P, NT]) for k in range(2)]
        expert_of = sb("expert_of", [P, TILES], I32)

        with ExitStack() as scope:
            def tmp(name, shape, dt=F32):
                return sb(name, shape, dt, scope)

            xn = tmp("xn", [P, NT, HID])
            xnT = tmp("xnT", [P, HC, GT * P])
            gate_w = tmp("gate", [P, HC, E])
            ln_stats = tmp("ln_stats", [P, NT, 6])
            ln_mv = tmp("ln_mv", [P, NT, 2])
            ln_var = tmp("ln_var", [P, NT])
            ln_rstd = tmp("ln_rstd", [P, NT])
            minus_half = tmp("minus_half", [P, NT])
            experts = tmp("experts", [P, NT, E])
            before = tmp("before", [P, E, E])
            steps_of = tmp("steps_of", [P, E, NT])
            numbers = tmp("numbers", [P, TILES, E])
            logits = tmp("logits", [P, NT, E])
            work = tmp("work", [P, NT, E])
            onehot = [tmp("onehot%d" % k, [P, NT, E]) for k in range(2)]
            taken = tmp("taken", [P, NT, E], BF16)
            earlier = tmp("earlier", [P, P], BF16)
            ones = tmp("ones", [P, P], BF16)
            top = [tmp("top%d" % k, [P, NT]) for k in range(2)]
            chosen = tmp("chosen", [P, NT])
            gap = tmp("gap", [P, NT])
            tiles_cmp = tmp("tiles_cmp", [P, E, NT])
            tiles = tmp("tiles", [P, E])
            tile_sums = tmp("tile_sums", [P, E, E])
            start = tmp("start", [P, E])
            end = tmp("end", [P, E])
            passed = tmp("passed", [P, TILES, E])
            expert_f = tmp("expert_f", [P, TILES])
            slot = tmp("slot", [P, NT, E])
            pos_f = tmp("pos_f", [P, NT])
        with ExitStack() as scope:
            rows = sb("rows", [P, 2, HID], F32, scope)
            xT = Split(sb("xT_hi", [P, 2, HC, P], F32R, scope), sb("xT_lo", [P, 2, HC, P], F32R, scope))
            sil = sb("sil", [P, 2, MLP], F32, scope)
            inter = sb("inter", [P, 2, MLP], F32, scope)
            interT = sb("interT", [P, 2, MC, P], F32, scope)
            y = sb("y", [P, 2, HID], F32, scope)
        with ExitStack() as scope:
            got = sb("got", [P, GATHERED, HID], F32, scope)

        gate_loaded, wo_loaded = sem("gate_loaded"), sem("wo_loaded")
        w_loaded = [sem("w_loaded%d" % i) for i in range(2 * E)]
        consts, stats_done, var_ready, rstd_ready = sem("consts"), sem("stats_done"), sem("var_ready"), sem("rstd_ready")
        xn_ready, xnT_full, xnT_ready = sem("xn_ready"), sem("xnT_full"), sem("xnT_ready")
        gate_done, routed, taken_ready, ranks_full = sem("gate_done"), sem("routed"), sem("taken_ready"), sem("ranks_full")
        gap_ready, gap_exp, pos_ready, expert_ready = sem("gap_ready"), sem("gap_exp"), sem("pos_ready"), sem("expert_ready")
        w_hi, w_lo_pool, w_lo_dve, scattered = sem("w_hi"), sem("w_lo_pool"), sem("w_lo_dve"), sem("scattered")
        rows_loaded = (sem("rows_loaded0"), sem("rows_loaded1"))
        xt_full, xt_hi, xt_lo = sem("xt_full"), sem("xt_hi"), sem("xt_lo")
        h0_full, h1_full, silu_done, inter_done = sem("h0_full"), sem("h1_full"), sem("silu_done"), sem("inter_done")
        it_full, it_copied, y_full, y_copied = sem("it_full"), sem("it_copied"), sem("y_full"), sem("y_copied")
        y_stored = (sem("y_stored0"), sem("y_stored1"))
        gathered = [sem("gathered%d" % i) for i in range(GATHERED)]
        added, stored = sem("added"), sem("stored")

        POOL_SPLITS = 5
        PEEL = 3
        LAST = TILES - 1

        def count(q, j, c=0):
            return j + c if q is None else q * 2 + (j + c)

        def wait(eng, sem, q, j, c):
            if q is not None or j + c > 0:
                eng.wait_ge(sem, count(q, j, c))

        def wait_dma(eng, sems, q, j, c):
            n = (j + c) // 2 + 1
            if q is not None:
                eng.wait_ge(sems[(j + c) % 2], q * 16 + 16 * n)
            elif n > 0:
                eng.wait_ge(sems[(j + c) % 2], 16 * n)

        def all_tiles(eng, run):
            for j in range(PEEL):
                run(None, j)
            with eng.Fori(0, (TILES - PEEL - 2) // 2) as q:
                run(q, PEEL)
                run(q, PEEL + 1)
            for j in range(TILES - 2, TILES):
                run(None, j)

        with nc.Block() as block:
            @block.sync
            def _(sp):
                sp.dma_start(gate_w[:], gate.rearrange("(c p) e -> p c e", p=P)).then_inc(gate_loaded, 16)
                for i in range(2 * E):
                    w = (w0, w1)[i % 2][i // 2]
                    sp.dma_start(W.lo[:, i, :].bitcast(F32).rearrange("p (c n) -> p c n", c=HC),
                                 w.rearrange("(c p) n -> p c n", p=P)).then_inc(w_loaded[i], 16)
                for e in range(E):
                    sp.dma_start(Wo[:, e, :, :], wo[e].rearrange("(c p) n -> p c n", p=P)).then_inc(wo_loaded, 16)

                def load(q, j):
                    sp.dma_start(rows[:, j % 2, :], rows_in[bass.ds(count(q, j) * P, P), :])\
                        .then_inc(rows_loaded[j % 2], 16)

                def store(q, j):
                    sp.wait_ge(y_copied, count(q, j, 1))
                    sp.dma_start(rows_out[bass.ds(count(q, j) * P, P), :], y[:, j % 2, :])\
                        .then_inc(y_stored[j % 2], 16)

                sp.wait_ge(scattered, 16 * 2 * NT)
                load(None, 0)
                load(None, 1)

                def run(q, j):
                    if q is not None or j + 2 <= LAST:
                        sp.wait_ge(xt_full, count(q, j, 1))
                        load(q, j + 2)
                    if q is not None or j > 0:
                        store(q, j - 1)

                all_tiles(sp, run)
                store(None, LAST)
                view = out.rearrange("b (t p) k -> p (b t) k", p=P)
                for t in range(0, NT, GT):
                    sp.wait_ge(added, 2 * (t + GT))
                    sp.dma_start(view[:, t:t + GT, :], x_all[:, t:t + GT, :]).then_inc(stored, 16)
                sp.wait_ge(stored, 16 * NG)

            @block.gpsimd
            def _(pool):
                pool.memset(minus_half[:], -0.5).then_inc(consts, 1)
                for e in range(E):
                    pool.memset(experts[:, :, e:e + 1], float(e)).then_inc(consts, 1)
                pool.memset(ones[:], 1.0).then_inc(consts, 1)
                for t in range(NT):
                    pool.memset(steps_of[:, :, t:t + 1], float(t * P)).then_inc(consts, 1)
                pool.wait_ge(var_ready, 1)
                pool.wait_ge(consts, 1)
                pool.tensor_tensor(ln_rstd[:], ln_var[:], minus_half[:], ALU.pow).then_inc(rstd_ready, 1)
                pool.wait_ge(consts, E + 2 + NT)
                pool.affine_select(earlier[:], ones[:], pattern=[[1, P]], base=-1, channel_multiplier=-1,
                                   compare_op=ALU.is_ge, fill=0.0).then_inc(consts, 1)
                pool.iota(numbers[:], pattern=[[1, TILES], [0, E]], base=0, channel_multiplier=0,
                          allow_small_or_imprecise_dtypes=True).then_inc(consts, 1)
                for i in range(POOL_SPLITS):
                    pool.wait_ge(w_hi, i + 1)
                    pool.tensor_tensor(W.lo[:, i, :], W.lo[:, i, :].bitcast(F32), W.hi[:, i, :].bitcast(F32),
                                       ALU.subtract).then_inc(w_lo_pool, 1)
                cm.wait_zeros(pool)
                for k in range(2):
                    pool.wait_ge(pos_ready, k + 1)
                    for t in range(NT):
                        pool.indirect_dma_start(rows_in[:, :], bass.IndirectOffsetOnAxis(pos[k][:, t:t + 1], 0),
                                                xn[:, t, :], None).then_inc(scattered, 16)
                for i in range(2):
                    j = LAST - i
                    pool.wait_ge(y_stored[j % 2], 16 * (j // 2 + 1))
                for n in range(2 * NT):
                    t, k = n // 2, n % 2
                    if n >= GATHERED:
                        pool.wait_ge(added, n - GATHERED + 1)
                    pool.indirect_dma_start(got[:, n % GATHERED, :], None, rows_out[:, :],
                                            bass.IndirectOffsetOnAxis(pos[k][:, t:t + 1], 0))\
                        .then_inc(gathered[n % GATHERED], 16)

            @block.scalar
            def _(act):
                def split_hi(i):
                    act.wait_ge(w_loaded[i], 16)
                    act.activation(W.hi[:, i, :], W.lo[:, i, :].bitcast(F32), ACT.Copy).then_inc(w_hi, 1)

                for n in range(HC * NG):
                    act.wait_ge(xnT_full, n + 1)
                    act.activation(xnT[:, n % HC, :], bank[H1_BANKS[n % 2]][:], ACT.Copy).then_inc(xnT_ready, 1)
                for i in range(POOL_SPLITS):
                    split_hi(i)
                act.wait_ge(gap_ready, 1)
                act.activation(gap[:], gap[:], ACT.Exp).then_inc(gap_exp, 1)
                for i in range(POOL_SPLITS, 2 * E):
                    split_hi(i)

                def run(q, j):
                    if j == 0 and q is None:
                        copy_hi(None, 0)
                    act.wait_ge(h0_full, count(q, j, 1))
                    act.activation(sil[:, j % 2, :], bank[H0_BANKS[j % 2]][:], ACT.Silu).then_inc(silu_done, 1)
                    if q is not None or j > 0:
                        copy_it(q, j - 1)
                    if q is not None or j < LAST:
                        copy_hi(q, j + 1)

                def copy_it(q, j):
                    act.wait_ge(it_full, count(q, j, 1))
                    act.activation(interT[:, j % 2, :, :].rearrange("p c n -> p (c n)"), bank[IT_BANK][:], ACT.Copy)\
                        .then_inc(it_copied, 1)

                def copy_hi(q, j):
                    act.wait_ge(xt_full, count(q, j, 1))
                    act.activation(xT.hi[:, j % 2, :, :].rearrange("p c n -> p (c n)"), bank[XT_BANK][:, 0:HC * P],
                                   ACT.Copy).then_inc(xt_hi, 1)

                all_tiles(act, run)
                copy_it(None, LAST)

            @block.vector
            def _(dve):
                for t in range(NT):
                    dve.bn_stats(ln_stats[:, t, :], x_all[:, t, :]).then_inc(stats_done, 1)
                dve.wait_ge(stats_done, NT)
                for t in range(NT):
                    dve.bn_aggr(ln_mv[:, t, :], ln_stats[:, t, :]).then_inc(stats_done, 1)
                dve.wait_ge(stats_done, 2 * NT)
                dve.tensor_scalar(ln_var[:], ln_mv[:, :, 1], EPS, None, ALU.add).then_inc(var_ready, 1)
                dve.wait_ge(rstd_ready, 1)
                for t in range(NT):
                    dve.tensor_scalar(xn[:, t, :], x_all[:, t, :], ln_mv[:, t, 0:1], ln_rstd[:, t:t + 1],
                                      ALU.subtract, ALU.mult).then_inc(xn_ready, 1)

                def wide(a):
                    return a[:].unsqueeze(2).to_broadcast([P, NT, E])

                dve.wait_ge(consts, E + 4 + NT)
                dve.tensor_tensor(before[:], experts[:, 0:E, :],
                                  experts[:, 0, :].unsqueeze(2).to_broadcast([P, E, E]), ALU.is_lt).then_inc(routed, 1)
                dve.wait_ge(gate_done, 1)
                dve.tensor_copy(logits[:], bank["q"][:, 0:NT * E].rearrange("p (t e) -> p t e", e=E))\
                    .then_inc(routed, 1)
                for k in range(2):
                    r = 1 + 6 * k
                    dve.wait_ge(routed, r + 1)
                    dve.tensor_reduce(top[k][:], logits[:], AX_X, ALU.max).then_inc(routed, 1)
                    dve.wait_ge(routed, r + 2)
                    dve.tensor_tensor(work[:], logits[:], wide(top[k]), ALU.is_lt).then_inc(routed, 1)
                    dve.wait_ge(routed, r + 3)
                    dve.scalar_tensor_tensor(work[:], work[:], 1000.0, experts[:], ALU.mult, ALU.add)\
                        .then_inc(routed, 1)
                    dve.wait_ge(routed, r + 4)
                    dve.tensor_reduce(chosen[:], work[:], AX_X, ALU.min).then_inc(routed, 1)
                    dve.wait_ge(routed, r + 5)
                    dve.tensor_tensor(onehot[k][:], experts[:], wide(chosen), ALU.is_equal).then_inc(routed, 1)
                    dve.wait_ge(routed, r + 6)
                    if k == 0:
                        dve.scalar_tensor_tensor(logits[:], onehot[0][:], NEVER, logits[:], ALU.mult, ALU.add)\
                            .then_inc(routed, 1)
                dve.tensor_tensor(taken[:], onehot[0][:], onehot[1][:], ALU.add).then_inc(taken_ready, 1)
                dve.tensor_tensor(gap[:], top[1][:], top[0][:], ALU.subtract).then_inc(gap_ready, 1)

                dve.wait_ge(ranks_full, 1)
                dve.tensor_tensor(tiles_cmp[:], bank["t"][:, 0:E].unsqueeze(2).to_broadcast([P, E, NT]), steps_of[:],
                                  ALU.is_gt).then_inc(routed, 1)
                dve.wait_ge(routed, 14)
                dve.tensor_reduce(tiles[:], tiles_cmp[:], AX_X, ALU.add).then_inc(routed, 1)
                dve.wait_ge(routed, 15)
                dve.tensor_tensor(tile_sums[:], tiles[:].unsqueeze(1).to_broadcast([P, E, E]), before[:], ALU.mult)\
                    .then_inc(routed, 1)
                dve.wait_ge(routed, 16)
                dve.tensor_reduce(start[:], tile_sums[:], AX_X, ALU.add).then_inc(routed, 1)
                dve.wait_ge(routed, 17)
                dve.scalar_tensor_tensor(slot[:], start[:].unsqueeze(1).to_broadcast([P, NT, E]), float(P),
                                         bank["s0"][:, 0:NT * E].rearrange("p (t e) -> p t e", e=E),
                                         ALU.mult, ALU.add).then_inc(routed, 1)
                dve.tensor_tensor(end[:], start[:], tiles[:], ALU.add).then_inc(routed, 1)
                for k in range(2):
                    dve.wait_ge(routed, 19 + 2 * k)
                    dve.tensor_tensor(work[:], slot[:], onehot[k][:], ALU.mult).then_inc(routed, 1)
                    dve.wait_ge(routed, 20 + 2 * k)
                    dve.tensor_reduce(pos_f[:], work[:], AX_X, ALU.add).then_inc(routed, 1)
                    dve.wait_ge(routed, 21 + 2 * k)
                    dve.tensor_copy(pos[k][:], pos_f[:]).then_inc(pos_ready, 1)
                    dve.wait_ge(pos_ready, k + 1)
                dve.tensor_tensor(passed[:], end[:].unsqueeze(1).to_broadcast([P, TILES, E]), numbers[:], ALU.is_le)\
                    .then_inc(routed, 1)
                dve.wait_ge(routed, 24)
                dve.tensor_reduce(expert_f[:], passed[:], AX_X, ALU.add).then_inc(routed, 1)
                dve.wait_ge(routed, 25)
                dve.tensor_scalar(expert_f[:], expert_f[:], float(E - 1), None, ALU.min).then_inc(routed, 1)
                dve.wait_ge(routed, 26)
                dve.tensor_copy(expert_of[:], expert_f[:]).then_inc(expert_ready, 1)

                dve.wait_ge(gap_exp, 1)
                dve.tensor_scalar(top[0][:], gap[:], 1.0, None, ALU.add).then_inc(routed, 1)
                dve.wait_ge(routed, 27)
                dve.reciprocal(weight[0][:], top[0][:]).then_inc(routed, 1)
                dve.wait_ge(routed, 28)
                dve.tensor_tensor(weight[1][:], gap[:], weight[0][:], ALU.mult).then_inc(routed, 1)
                dve.wait_ge(routed, 29)
                for i in range(POOL_SPLITS, 2 * E):
                    dve.wait_ge(w_hi, i + 1)
                    dve.tensor_tensor(W.lo[:, i, :], W.lo[:, i, :].bitcast(F32), W.hi[:, i, :].bitcast(F32),
                                      ALU.subtract).then_inc(w_lo_dve, 1)

                def copy_lo(q, j):
                    dve.wait_ge(xt_hi, count(q, j, 1))
                    dve.tensor_tensor(xT.lo[:, j % 2, :, :].rearrange("p c n -> p (c n)"), bank[XT_BANK][:, 0:HC * P],
                                      xT.hi[:, j % 2, :, :].rearrange("p c n -> p (c n)").bitcast(F32),
                                      ALU.subtract).then_inc(xt_lo, 1)

                def copy_y(q, j):
                    dve.wait_ge(y_full, count(q, j, 1))
                    wait_dma(dve, y_stored, q, j, -2)
                    dve.tensor_copy(y[:, j % 2, :], bank[Y_BANK][:, 0:HID]).then_inc(y_copied, 1)

                def run(q, j):
                    if j == 0 and q is None:
                        copy_lo(None, 0)
                    if q is not None or j < LAST:
                        copy_lo(q, j + 1)
                    dve.wait_ge(h1_full, count(q, j, 1))
                    dve.wait_ge(silu_done, count(q, j, 1))
                    dve.tensor_tensor(inter[:, j % 2, :], bank[H1_BANKS[j % 2]][:], sil[:, j % 2, :], ALU.mult)\
                        .then_inc(inter_done, 1)
                    if q is not None or j > 0:
                        copy_y(q, j - 1)

                all_tiles(dve, run)
                copy_y(None, LAST)

                for n in range(2 * NT):
                    t, k = n // 2, n % 2
                    if k == 1:
                        dve.wait_ge(added, n)
                    dve.wait_ge(gathered[n % GATHERED], 16 * (n // GATHERED + 1))
                    dve.scalar_tensor_tensor(x_all[:, t, :], got[:, n % GATHERED, :], weight[k][:, t:t + 1],
                                             x_all[:, t, :], ALU.mult, ALU.add).then_inc(added, 1)

            @block.tensor
            def _(pe):
                pe.wait_ge(gate_loaded, 16)
                for g in range(NG):
                    pe.wait_ge(xn_ready, (g + 1) * GT)
                    for c in range(HC):
                        n = g * HC + c
                        if n >= 2:
                            pe.wait_ge(xnT_ready, n - 1)
                        for t in range(GT):
                            ins = pe.transpose(bank[H1_BANKS[n % 2]][:, t * P:(t + 1) * P],
                                               xn[:, g * GT + t, c * P:(c + 1) * P], ident[:])
                        ins.then_inc(xnT_full, 1)
                    pe.wait_ge(xnT_ready, HC * (g + 1))
                    for t in range(GT):
                        at = (g * GT + t) * E
                        for c in range(HC):
                            ins = pe.matmul(bank["q"][:, at:at + E], xnT[:, c, t * P:(t + 1) * P], gate_w[:, c, :],
                                            start=c == 0, stop=c == HC - 1, skip_group_check=True)
                ins.then_inc(gate_done, 1)
                pe.wait_ge(taken_ready, 1)
                flat = taken[:].rearrange("p t e -> p (t e)")
                pe.matmul(bank["s0"][:, 0:NT * E], earlier[:], flat, start=True, stop=False, skip_group_check=True)
                for s in range(1, NT):
                    pe.matmul(bank["s0"][:, s * E:NT * E], ones[:], flat[:, 0:(NT - s) * E],
                              start=False, stop=s == NT - 1, skip_group_check=True)
                for t in range(NT):
                    ins = pe.matmul(bank["t"][:, 0:E], ones[:], taken[:, t, :], start=t == 0, stop=t == NT - 1,
                                    skip_group_check=True)
                ins.then_inc(ranks_full, 1)

                def xt(q, j):
                    wait_dma(pe, rows_loaded, q, j, 0)
                    wait(pe, xt_lo, q, j, 0)
                    for c in range(HC):
                        ins = pe.transpose(bank[XT_BANK][:, c * P:(c + 1) * P], rows[:, j % 2, c * P:(c + 1) * P],
                                           ident[:])
                    ins.then_inc(xt_full, 1)

                def expert(q, j):
                    return pe.value_load(expert_of[0:1, bass.ds(count(q, j), 1)], min_val=0, max_val=E - 1)

                def hidden(q, j, e, half, banks, full):
                    for c in range(HC):
                        w = Split(*[a[:, bass.ds(e * 2 + half, 1), c * MLP:(c + 1) * MLP]
                                    .rearrange("p a n -> p (a n)") for a in (W.hi, W.lo)])
                        ins = mm3(pe, bank[banks[j % 2]][:], xT[:, j % 2, c, :], w, c == 0, c == HC - 1)
                    ins.then_inc(full, 1)

                def it(q, j):
                    pe.wait_ge(inter_done, count(q, j, 1))
                    for m in range(MC):
                        ins = pe.transpose(bank[IT_BANK][:, m * P:(m + 1) * P], inter[:, j % 2, m * P:(m + 1) * P],
                                           ident[:])
                    ins.then_inc(it_full, 1)

                def outputs(q, j, e):
                    pe.wait_ge(it_copied, count(q, j, 1))
                    wait(pe, y_copied, q, j, 0)
                    for m in range(MC):
                        w = Wo[:, bass.ds(e, 1), m, :].rearrange("p a n -> p (a n)")
                        ins = pe.matmul(bank[Y_BANK][:, 0:HID], interT[:, j % 2, m, :], w,
                                        start=m == 0, stop=m == MC - 1)
                    ins.then_inc(y_full, 1)

                pe.wait_ge(expert_ready, 1)
                xt(None, 0)
                pe.wait_ge(w_lo_pool, POOL_SPLITS)
                pe.wait_ge(w_lo_dve, 2 * E - POOL_SPLITS)
                pe.wait_ge(wo_loaded, 16 * E)

                def run(q, j):
                    e = expert(q, j)
                    pe.wait_ge(xt_lo, count(q, j, 1))
                    wait(pe, inter_done, q, j, -1)
                    hidden(q, j, e, 0, H0_BANKS, h0_full)
                    if q is not None or j > 0:
                        it(q, j - 1)
                    hidden(q, j, e, 1, H1_BANKS, h1_full)
                    if q is not None or j < LAST:
                        xt(q, j + 1)
                    if q is not None or j > 0:
                        outputs(q, j - 1, expert(q, j - 1))

                all_tiles(pe, run)
                it(None, LAST)
                outputs(None, LAST, expert(None, LAST))


def decoder_layer(nc, x, ctx_in, mask, w_qkv, w_proj, Wq, Wk, Wv, Wo, gate, w0, w1, wo, out):
    cm = Common()
    cm.x = x
    cm.B, cm.S, cm.HID = x.shape
    cm.HC = cm.HID // P
    cm.NT = cm.B * cm.S // P
    cm.PAIRS = cm.B // 2
    cm.TP = 2 * cm.S
    cm.TT = cm.TP // P
    with ExitStack() as ctx:
        cm.sems = ctx
        cm.bank = {n: ctx.enter_context(nc.psum_tensor("bank_" + n, [P, 512], F32))
                   for n in ("q", "t", "s0", "s1", "o0", "o1", "y0", "y1")}
        cm.x_all = ctx.enter_context(nc.sbuf_tensor("x_all", [P, cm.NT, cm.HID], F32))
        cm.ident = ctx.enter_context(nc.sbuf_tensor("ident", [P, P], F32))
        E, TOP_K = w0.shape[0], 2
        tiles = TOP_K * cm.NT + E - 1
        rows_in = nc.dram_tensor("rows_in", [tiles * P, cm.HID], F32).ap()
        rows_out = nc.dram_tensor("rows_out", [tiles * P, cm.HID], F32).ap()
        zeros = ctx.enter_context(nc.sbuf_tensor("zeros", [P, 1, cm.HID], F32))
        zeros_ready, zeros_stored = ctx.enter_context(nc.semaphore("zeros_ready")), ctx.enter_context(nc.semaphore("zeros_stored"))
        cm.wait_zeros = lambda eng: eng.wait_ge(zeros_stored, 16)
        with nc.Block() as block:
            @block.gpsimd
            def _(pool):
                pool.memset(zeros[:], 0.0).then_inc(zeros_ready, 1)

            @block.sync
            def _(sp):
                sp.wait_ge(zeros_ready, 1)
                sp.dma_start(rows_in.rearrange("(t p) k -> p t k", p=P),
                             zeros[:].to_broadcast([P, tiles, cm.HID])).then_inc(zeros_stored, 16)

        self_attention(nc, cm, w_qkv, w_proj)
        cross_attention(nc, cm, ctx_in, mask, Wq, Wk, Wv, Wo)
        feed_forward(nc, cm, gate, w0, w1, wo, rows_in, rows_out, out)


_INS = ['x', 'ctx_1024', 'mask_BxS2_bf1', 'L0_attn_weight_qkv', 'L0_attn_weight_proj', 'L0_xattn_Wq', 'L0_xattn_Wk',
        'L0_xattn_Wv', 'L0_xattn_Wo', 'L0_ffn_gate_kernel', 'L0_ffn_w0_kernel', 'L0_ffn_w1_kernel',
        'L0_ffn_wo_kernel']
_OUTS = [((8, 256, 256), 'float32')]


def kernel(**inputs):
    import numpy as _np
    import concourse.bacc as _bacc
    from concourse import mybir as _mybir
    from concourse.bass_utils import run_bass_kernel_spmd as _run

    nc = _bacc.Bacc("TRN2", target_bir_lowering=False, num_devices=1)
    arrays, args = {}, []
    for name in _INS:
        a = _np.ascontiguousarray(inputs[name])
        if a.dtype.kind == "b":
            a = a.view(_np.uint8)
        arrays[f"in_{name}_dram"] = a
        args.append(nc.dram_tensor(f"in_{name}_dram", a.shape, _mybir.dt.from_np(a.dtype), kind="ExternalInput").ap())
    for i, (shape, dtype) in enumerate(_OUTS):
        dt = _mybir.dt.from_np(_np.dtype(dtype))
        args.append(nc.dram_tensor(f"out_{i}_dram", shape, dt, kind="ExternalOutput").ap())
    decoder_layer(nc, *args)
    r = _run(nc, [arrays], core_ids=[0])
    return r.results[0]["out_0_dram"]
```

```python
from contextlib import ExitStack

import concourse.bass as bass
from concourse import mybir

F32 = mybir.dt.float32
F32R = mybir.dt.float32r
BF16 = mybir.dt.bfloat16
I32 = mybir.dt.int32
U8 = mybir.dt.uint8
ALU = mybir.AluOpType
ACT = mybir.ActivationFunctionType
AX_X = mybir.AxisListType.X

P = 128
EPS = 1e-5
NEG = -1e30
BIG = 3e38


class Split:

    def __init__(self, hi, lo):
        self.hi, self.lo = hi, lo

    def __getitem__(self, at):
        return Split(self.hi[at], self.lo[at])

    def view(self, pattern, **sizes):
        return Split(self.hi.rearrange(pattern, **sizes), self.lo.rearrange(pattern, **sizes))


def mm3(pe, out, lhsT, rhs, first, last):
    pe.matmul(out, lhsT.hi, rhs.hi, start=first, stop=False, skip_group_check=True)
    pe.matmul(out, lhsT.hi, rhs.lo, start=False, stop=False, skip_group_check=True)
    return pe.matmul(out, lhsT.lo, rhs.hi, start=False, stop=last, skip_group_check=True)


class Uses:

    def __init__(self, first, body, quiet=()):
        self.full, self.freed, self.before = {}, {}, {}
        n, f, last = {}, {}, {}
        for part, steps in enumerate((first, body)):
            base_n, base_f = dict(n), dict(f)
            for name, bank in steps:
                key = (part, name)
                self.before[key] = last.get(bank)
                n[bank] = n.get(bank, 0) + 1
                f[bank] = f.get(bank, 0) + (name[0] not in quiet)
                self.full[key], self.freed[key] = n[bank], f[bank]
                last[bank] = name
            if part == 1:
                self.per_full = {b: n[b] - base_n.get(b, 0) for b in n}
                self.per_freed = {b: f[b] - base_f.get(b, 0) for b in f}
        self.bank = {(part, name): bank for part, steps in enumerate((first, body)) for name, bank in steps}

    def count_full(self, p, name):
        if p is None:
            return self.full[0, name]
        return p * self.per_full[self.bank[1, name]] + self.full[1, name]

    def count_freed(self, p, name):
        if p is None:
            return self.freed[0, name]
        return p * self.per_freed[self.bank[1, name]] + self.freed[1, name]

    def bank_of(self, p, name):
        return self.bank[0 if p is None else 1, name]


class Common:
    pass


def self_attention(nc, cm, w_qkv, w_proj):
    S, HID, NT, D, HC = cm.S, cm.HID, cm.NT, P, cm.HC
    NH = w_proj.shape[1] // D
    NKV = (w_qkv.shape[0] // D - NH) // 2
    QPG = NH // NKV
    NR = NH + 2 * NKV
    PAIRS, TP, TT = cm.PAIRS, cm.TP, cm.TT
    SCALE = float(D) ** -0.5
    UNITS = 2 * NH
    CW = P + 2 * P
    x_all, ident, bank = cm.x_all, cm.ident, cm.bank

    with ExitStack() as ctx:
        def sb(name, shape, dt=F32):
            return ctx.enter_context(nc.sbuf_tensor(name, shape, dt))

        def split(name, shape):
            return Split(sb(name + "_hi", shape, F32R), sb(name + "_lo", shape, F32R))

        def sem(name):
            return cm.sems.enter_context(nc.semaphore("a_" + name))

        causal = sb("causal", [P, CW])
        WqkvT = split("WqkvT", [P, HC, NR * D])
        WprojT = split("WprojT", [P, NH, HID])
        xn = sb("xn", [P, TT, HID])
        xnT = split("xnT", [P, HC, TP])
        with ExitStack() as early:
            stage_proj = early.enter_context(nc.sbuf_tensor("stage_proj", [P, 2, NH * D], F32))
        kT = split("kT", [P, NKV, TP])
        v = split("v", [P, TT, NKV * D])
        qT = split("qT", [P, 2, TP])
        oT = split("oT", [P, 2, TP])
        pT = split("pT", [P, 2, CW])
        masked = sb("masked", [P, 2, CW])
        prob = sb("prob", [P, 3, CW])
        negmax = sb("negmax", [P, 4, 2])
        rowsum = sb("rowsum", [P, 4, 2])
        rinv = sb("rinv", [P, 4, 2])
        ln_stats = sb("ln_stats", [P, NT, 6])
        ln_mv = sb("ln_mv", [P, NT, 2])
        ln_var = sb("ln_var", [P, NT])
        ln_rstd = sb("ln_rstd", [P, NT])
        minus_half = sb("minus_half", [P, NT])

        W_PARTS = 3
        full = {n: sem("full_" + n) for n in bank}
        half = {n: sem("half_" + n) for n in bank}
        free = {n: sem("free_" + n) for n in bank}
        x_loaded = sem("x_loaded")
        x_rest_loaded = sem("x_rest_loaded")
        w_loaded = [sem(f"w_loaded{i}") for i in range(W_PARTS + 1)]
        ident_made = sem("ident_made")
        mask_made = sem("mask_made")
        stats_done = sem("stats_done")
        half_made = sem("half_made")
        var_ready = sem("var_ready")
        rstd_ready = sem("rstd_ready")
        xn_ready = sem("xn_ready")
        masked_ready = sem("masked_ready")
        exp_done = sem("exp_done")
        rinv_ready = sem("rinv_ready")
        prob_ready = sem("prob_ready")
        x_updated = sem("x_updated")

        setup_banks = ("q", "t", "s0", "s1", "o0")
        stage_qkv = cm.stage[:].rearrange("p (r k) -> p r k", k=HID)
        fills = []
        for r in range(0, NR, 4):
            for c in range(HC):
                fills.append((WqkvT[:, c, r * P:(r + 4) * P],
                              [stage_qkv[:, r + i, c * P:(c + 1) * P] for i in range(4)]))
        QKV_FILLS = len(fills)
        for h in range(0, NH, 2):
            fills.append((WprojT[:, h:h + 2, :],
                          [stage_proj[:, i % 2, (h + i // 2) * P:(h + i // 2 + 1) * P] for i in range(4)]))
        setup = [(("w", i), setup_banks[i % len(setup_banks)]) for i in range(len(fills))]
        front = ([(("xt", c), "q") for c in range(HC)] + [(("k", g), ("q", "o0")[g % 2]) for g in range(NKV)]
                 + [(("q", 0), "q")])
        body = []
        LAST = UNITS + 6
        for s in range(LAST):
            if s < UNITS:
                body.append((("scores", s), ("s0", "s1")[s % 2]))
                if s % 2 == 0 and s // 2 + 1 < NH:
                    body.append((("q", s // 2 + 1), "q"))
                if s < TT:
                    body.append((("v", s), ("o1", "o0", "o1", "o1")[s]))
                if s >= 5 and s % 2 == 1 and (s - 5) // 2 < NH - 2:
                    body.append((("o", (s - 5) // 2), ("o0", "o1")[(s - 5) // 2 % 2]))
            if s >= 7 and s % 2 == 1 and (s - 7) // 2 < NH:
                body.append((("proj", (s - 7) // 2), None))
            if 0 <= s - 2 < UNITS:
                body.append((("t", s - 2), "t"))
            if 0 <= s - 3 < UNITS:
                body.append((("pv", s - 3), None))
                h = (s - 3) // 2
                if (s - 3) % 2 == 1 and h >= NH - 2:
                    body.append((("o", h), ("o0", "o1")[h % 2]))
            if 22 <= s < 22 + TT:
                body.append((("next_xn", s - 22), None))
            more = {29: front[0:1], 30: front[1:2], UNITS: front[2:4], UNITS + 1: front[4:6], UNITS + 2: front[6:]}
            body += [(("next",) + name, b) for name, b in more.get(s, [])]
        body.append((("residual",), None))
        real = [(n, b) for n, b in body if b]
        uses = Uses(setup + front, [((n[1:] if n[0] == "next" else n), b) for n, b in real], quiet=("scores",))

        w_qkv_v = w_qkv.rearrange("(r p) k -> p r k", p=P)
        w_proj_v = w_proj.rearrange("(j p) e -> p j e", p=P)
        x_v = cm.x.rearrange("b (t p) k -> p (b t) k", p=P)

        def dst_of(name):
            what, i = name
            return {"w": lambda: (fills[i][0], 512), "xt": lambda: (xnT[:, i, :], TP), "k": lambda: (kT[:, i, :], TP),
                    "v": lambda: (v[:, i, :], NKV * D), "q": lambda: (qT[:, i % 2, :], TP),
                    "t": lambda: (pT[:, i % 2, :], CW), "o": lambda: (oT[:, i % 2, :], TP)}[what]()

        def passes(eng, run):
            with eng.Fori(0, PAIRS - 1) as p:
                for name, _ in body:
                    run(p, name)
            for name, _ in body:
                if not name[0].startswith("next"):
                    run(PAIRS - 1, name)

        with nc.Block() as block:

            @block.sync
            def _(sp):
                sp.dma_start(x_all[:, 0:TT, :], x_v[:, 0:TT, :]).then_inc(x_loaded, 16)
                part = NR // W_PARTS
                for i in range(W_PARTS):
                    at = slice(i * part, (i + 1) * part)
                    sp.dma_start(stage_qkv[:, at, :], w_qkv_v[:, at, :]).then_inc(w_loaded[i], 16)
                sp.dma_start(stage_proj[:], w_proj_v).then_inc(w_loaded[W_PARTS], 16)
                sp.dma_start(x_all[:, TT:, :], x_v[:, TT:, :]).then_inc(x_rest_loaded, 16)
                at = ("w", QKV_FILLS - 1)
                sp.wait_ge(full[uses.bank_of(None, at)], uses.count_full(None, at))
                cm.load_cross_inputs(sp)

            @block.gpsimd
            def _(pool):
                pool.memset(ident[:], 0.0).then_inc(ident_made, 1)
                pool.memset(causal[:], 0.0).then_inc(mask_made, 1)
                pool.wait_ge(ident_made, 1)
                pool.affine_select(out=ident[:], in_=ident[:], compare_op=ALU.not_equal, fill=1.0, base=0,
                                   pattern=[[-1, P]], channel_multiplier=1).then_inc(ident_made, 1)
                pool.wait_ge(mask_made, 1)
                for at in (0, 2 * P):
                    pool.affine_select(out=causal[:, at:at + P], in_=causal[:, at:at + P], compare_op=ALU.is_ge,
                                       fill=NEG, base=0, pattern=[[-1, P]], channel_multiplier=1)\
                        .then_inc(mask_made, 1)
                pool.memset(minus_half[:], -0.5).then_inc(half_made, 1)
                pool.wait_ge(half_made, 1)
                for i, at in enumerate((slice(0, TT), slice(TT, NT))):
                    pool.wait_ge(var_ready, i + 1)
                    pool.tensor_tensor(ln_rstd[:, at], ln_var[:, at], minus_half[:, at], ALU.pow)\
                        .then_inc(rstd_ready, 1)

                def run(p, name):
                    if name[0] != "scores":
                        return
                    u = name[1]
                    pool.wait_ge(rinv_ready, p * UNITS + (u + 1))
                    for i, (a, b) in enumerate(((0, P), (P, CW))):
                        pool.tensor_tensor(prob[:, u % 3, a:b], prob[:, u % 3, a:b],
                                           rinv[:, u % 4, i:i + 1].to_broadcast([P, b - a]), ALU.mult)\
                            .then_inc(prob_ready, 1)

                passes(pool, run)

            @block.scalar
            def _(act):
                def high(p, name):
                    n = uses.bank_of(p, name)
                    dst, width = dst_of(name)
                    act.wait_ge(full[n], uses.count_full(p, name))
                    act.activation(dst.hi, bank[n][:, 0:width], ACT.Copy).then_inc(half[n], 1)

                for name, _ in setup + front:
                    high(None, name)

                def run(p, name):
                    if name[0] == "next":
                        high(p, name[1:])
                    elif name[0] in ("q", "t", "v") or name[0] == "o" and name[1] >= NH - 2:
                        high(p, name)
                    elif name[0] == "scores":
                        s = name[1]
                        if s >= 5 and s % 2 == 1:
                            high(p, ("o", (s - 5) // 2))
                        act.wait_ge(masked_ready, p * 2 * UNITS + 2 * (s + 1))
                        for i, (a, b) in enumerate(((0, P), (P, CW))):
                            act.activation(prob[:, s % 3, a:b], masked[:, s % 2, a:b], ACT.Exp, scale=-1.0,
                                           bias=negmax[:, s % 4, i:i + 1],
                                           accum_out=rowsum[:, s % 4, i:i + 1]).then_inc(exp_done, 1)

                passes(act, run)

            @block.vector
            def _(dve):
                def low(p, name):
                    n = uses.bank_of(p, name)
                    dst, width = dst_of(name)
                    src = bank[n][:, 0:width]
                    if len(dst.lo.shape) == 3:
                        src = src.rearrange("p (a b) -> p a b", a=dst.lo.shape[1])
                    dve.wait_ge(half[n], uses.count_freed(p, name))
                    dve.tensor_tensor(dst.lo, src, dst.hi.bitcast(F32), ALU.subtract).then_inc(free[n], 1)

                def normalize(p, t):
                    xt = x_all[:, bass.ds(p * TT + t, 1), :].rearrange("p a k -> p (a k)")
                    mu = ln_mv[:, bass.ds(p * TT + t, 1), 0]
                    rs = ln_rstd[:, bass.ds(p * TT + t, 1)]
                    dve.tensor_scalar(xn[:, t, :], xt, mu, rs, ALU.subtract, ALU.mult).then_inc(xn_ready, 1)

                def invert(p, s):
                    dve.wait_ge(exp_done, p * 2 * UNITS + 2 * (s + 1))
                    dve.reciprocal(rinv[:, s % 4, :], rowsum[:, s % 4, :]).then_inc(rinv_ready, 1)

                def stats(t):
                    dve.bn_stats(ln_stats[:, t, :], x_all[:, t, :]).then_inc(stats_done, 1)

                def mean_and_variance(tiles):
                    dve.wait_ge(stats_done, tiles[0] + tiles[-1] + 1)
                    for t in tiles:
                        dve.bn_aggr(ln_mv[:, t, :], ln_stats[:, t, :]).then_inc(stats_done, 1)
                    dve.wait_ge(stats_done, 2 * tiles[-1] + 2)
                    at = slice(tiles[0], tiles[-1] + 1)
                    dve.tensor_scalar(ln_var[:, at], ln_mv[:, at, 1], EPS, None, ALU.add).then_inc(var_ready, 1)

                dve.wait_ge(x_loaded, 16)
                for t in range(TT):
                    stats(t)
                mean_and_variance(range(TT))
                for i, (name, _) in enumerate(setup):
                    low(None, name)
                    if i == 1:
                        dve.wait_ge(rstd_ready, 1)
                        for t in range(TT):
                            normalize(0, t)
                others = list(range(TT, NT))
                for i, (name, _) in enumerate(front):
                    low(None, name)
                    if i >= 1:
                        if i == 1:
                            dve.wait_ge(x_rest_loaded, 16)
                        steps = len(front) - 1
                        for t in others[(i - 1) * len(others) // steps:i * len(others) // steps]:
                            stats(t)
                mean_and_variance(others)
                dve.wait_ge(mask_made, 3)

                def run(p, name):
                    if name[0] == "next":
                        low(p, name[1:])
                    elif name[0] == "next_xn":
                        if name[1] == 0:
                            dve.wait_ge(rstd_ready, 2)
                        normalize(p + 1, name[1])
                    elif name[0] in ("q", "o", "v"):
                        low(p, name)
                    elif name[0] == "scores":
                        s = name[1]
                        n = uses.bank_of(p, name)
                        dve.wait_ge(full[n], uses.count_full(p, name))
                        if s == 0:
                            dve.tensor_copy(rinv[:, 3, :], ident[:, 0:2])
                        else:
                            invert(p, s - 1)
                        for i, (a, b) in enumerate(((0, P), (P, CW))):
                            dve.tensor_tensor_reduce(masked[:, s % 2, a:b], bank[n][:, a:b], causal[:, a:b],
                                                     -SCALE, BIG, ALU.add, ALU.min, negmax[:, s % 4, i:i + 1])\
                                .then_inc(masked_ready, 1)
                    elif name[0] == "t":
                        low(p, name)
                    elif name[0] == "residual":
                        for j, n in enumerate(("y0", "y1")):
                            dve.wait_ge(full[n], p + 1)
                            xt = x_all[:, bass.ds(p * TT + 2 * j, 2), :]
                            dve.tensor_tensor(xt, bank[n][:].rearrange("p (t k) -> p t k", t=2), xt, ALU.add)\
                                .then_inc(x_updated, 1)
                    if name == ("t", UNITS - 3):
                        invert(p, UNITS - 1)

                passes(dve, run)

            @block.tensor
            def _(pe):
                def wait_free(p, name):
                    n = uses.bank_of(p, name)
                    before = uses.before[0 if p is None else 1, name]
                    if before is None:
                        return
                    if before[0] == "scores":
                        pe.wait_ge(masked_ready, p * 2 * UNITS + 2 * (before[1] + 1))
                    else:
                        pe.wait_ge(free[n], uses.count_freed(p, name) - (name[0] != "scores"))

                def fill(p, name):
                    what, i = name
                    n = uses.bank_of(p, name)
                    wait_free(p, name)
                    if what == "w":
                        for j, src in enumerate(fills[i][1]):
                            ins = pe.transpose(bank[n][:, j * P:(j + 1) * P], src, ident[:])
                    elif what == "xt":
                        for t in range(TT):
                            ins = pe.transpose(bank[n][:, t * P:(t + 1) * P], xn[:, t, i * P:(i + 1) * P], ident[:])
                    elif what == "v":
                        for c in range(HC):
                            wv = WqkvT.view("p c (g i d) -> p c g i d", g=NKV, d=D)[:, c, :, QPG + 1, :]
                            ins = mm3(pe, bank[n][:].rearrange("p (g d) -> p g d", g=NKV),
                                      xnT[:, c, i * P:(i + 1) * P], wv, c == 0, c == HC - 1)
                    else:
                        col = {"k": (i * (QPG + 2) + QPG) * D, "q": ((i // QPG) * (QPG + 2) + i % QPG) * D}[what]
                        for c in range(HC):
                            ins = mm3(pe, bank[n][:], WqkvT[:, c, col:col + D], xnT[:, c, :], c == 0, c == HC - 1)
                    ins.then_inc(full[n], 1)

                def wait_copied(p, name):
                    pe.wait_ge(free[uses.bank_of(p, name)], uses.count_freed(p, name))

                pe.wait_ge(ident_made, 2)
                for name, _ in setup:
                    i = name[1]
                    if i == QKV_FILLS:
                        pe.wait_ge(w_loaded[W_PARTS], 16)
                    elif i < QKV_FILLS and i % (QKV_FILLS // W_PARTS) == 0:
                        pe.wait_ge(w_loaded[i // (QKV_FILLS // W_PARTS)], 16)
                    fill(None, name)
                for name, _ in setup[-len(setup_banks):]:
                    wait_copied(None, name)
                pe.wait_ge(xn_ready, TT)
                for name, _ in front:
                    if name == ("k", 0):
                        wait_copied(None, ("xt", 0))
                        wait_copied(None, ("xt", 1))
                    fill(None, name)
                for name, _ in front[HC:]:
                    wait_copied(None, name)

                def run(p, name):
                    what = name[0]
                    if what == "next":
                        if name == ("next", "xt", 0):
                            pe.wait_ge(xn_ready, p * TT + 2 * TT)
                        if name == ("next", "k", 0):
                            wait_copied(p, ("xt", 0))
                            wait_copied(p, ("xt", 1))
                        fill(p, name[1:])
                        if name == ("next", "q", 0):
                            for other, _ in front[HC:-1]:
                                wait_copied(p, other)
                    elif what in ("q", "v"):
                        fill(p, name)
                    elif what == "scores":
                        u = name[1]
                        h, b = u // 2, u % 2
                        g = h // QPG
                        n = uses.bank_of(p, name)
                        wait_free(p, name)
                        if b == 0 and h > 0:
                            wait_copied(p, ("q", h))
                        if u == 0:
                            pe.wait_ge(free["q"], uses.count_freed(p, ("q", 1)) - 1)
                        mm3(pe, bank[n][:, 0:P], qT[:, h % 2, b * S:b * S + P], kT[:, g, b * S:b * S + P], True, True)
                        mm3(pe, bank[n][:, P:CW], qT[:, h % 2, b * S + P:b * S + S], kT[:, g, b * S:b * S + S],
                            True, True).then_inc(full[n], 1)
                    elif what == "t":
                        u = name[1]
                        pe.wait_ge(prob_ready, p * 2 * UNITS + 2 * (u + 1))
                        wait_free(p, name)
                        for j in range(3):
                            ins = pe.transpose(bank["t"][:, j * P:(j + 1) * P], prob[:, u % 3, j * P:(j + 1) * P],
                                               ident[:])
                        ins.then_inc(full["t"], 1)
                    elif what == "pv":
                        u = name[1]
                        h, b = u // 2, u % 2
                        g = h // QPG
                        wait_copied(p, ("t", u))
                        if u < 2:
                            for t in ((0, 1), (3,))[b]:
                                wait_copied(p, ("v", t))
                        if b == 0:
                            wait_free(p, ("o", h))
                        n = uses.bank_of(p, ("o", h))
                        vg = v[:, :, g * D:(g + 1) * D]
                        mm3(pe, bank[n][:, b * S:b * S + S], vg[:, 2 * b, :], pT[:, u % 2, 0:S], True, False)
                        ins = mm3(pe, bank[n][:, b * S + P:b * S + S], vg[:, 2 * b + 1, :], pT[:, u % 2, S:CW],
                                  False, True)
                        if b == 1:
                            ins.then_inc(full[n], 1)
                    elif what == "proj":
                        h = name[1]
                        wait_copied(p, ("o", h))
                        for t in range(TT):
                            y = ("y0", "y1")[t // 2]
                            ins = mm3(pe, bank[y][:, (t % 2) * HID:(t % 2 + 1) * HID],
                                      oT[:, h % 2, t * P:(t + 1) * P], WprojT[:, h, :],
                                      h == 0 and t % 2 == 0, h == NH - 1)
                            if h == NH - 1 and t % 2 == 1:
                                ins.then_inc(full[y], 1)

                passes(pe, run)


class Order:

    def __init__(self, first, body, final, passes):
        self.at, self.per = {}, {}
        count, last = self._number(0, first, {}, {})
        after, _ = self._number(1, body, count, last)
        for bank, c in after.items():
            self.per[bank] = tuple(b - a for a, b in zip(count.get(bank, (0, 0, 0)), c))
        start = {bank: tuple(a + passes * b for a, b in zip(count.get(bank, (0, 0, 0)), self.per[bank]))
                 for bank in after}
        self._number(2, final, start, last)

    def _number(self, part, steps, count, last):
        count, last = dict(count), dict(last)
        for name, bank, who in steps:
            a, b, c = count.get(bank, (0, 0, 0))
            count[bank] = (a + 1, b + (who == "both"), c + (who != ""))
            self.at[part, name] = (bank, count[bank], last.get(bank), who)
            last[bank] = name
        return count, last

    def _of(self, p, name):
        return self.at[0 if p is None else 2 if isinstance(p, int) else 1, name]

    def _count(self, p, name, which):
        bank, c, _, _ = self._of(p, name)
        return c[which] if p is None or isinstance(p, int) else p * self.per[bank][which] + c[which]

    def bank(self, p, name):
        return self._of(p, name)[0]

    def who(self, p, name):
        return self._of(p, name)[3]

    def full(self, p, name):
        return self._count(p, name, 0)

    def half(self, p, name):
        return self._count(p, name, 1)

    def free(self, p, name):
        return self._count(p, name, 2)

    def before(self, p, name):
        return self._of(p, name)[2]


def cross_attention(nc, cm, ctx_in, mask, Wq, Wk, Wv, Wo):
    HID, HC, PAIRS, TP, TT = cm.HID, cm.HC, cm.PAIRS, cm.TP, cm.TT
    D = P
    S2 = ctx_in.shape[1]
    NH = Wq.shape[1] // D
    NG = Wk.shape[1] // D
    KP = 2 * S2
    SCALE = float(D) ** -0.5
    HALF = NH // 2 * S2
    NJ = NH * S2 // P
    x_all, ident, bank = cm.x_all, cm.ident, cm.bank

    with ExitStack() as ctx:
        def sb(name, shape, dt=F32, at=ctx):
            return at.enter_context(nc.sbuf_tensor("b_" + name, shape, dt))

        def split(name, shape):
            return Split(sb(name + "_hi", shape, F32R), sb(name + "_lo", shape, F32R))

        def sem(name):
            return cm.sems.enter_context(nc.semaphore("b_" + name))

        VWs = split("VWs", [P, NG, 2 * HID])
        WqT = sb("WqT", [P, NH, HID])
        wk = sb("wk", [P, NG * D])
        wv = sb("wv", [P, NG * D])
        wo = sb("wo", [P, NH, HID])
        ctxT = sb("ctxT", [P, PAIRS * KP])
        kT = sb("kT", [P, NG, KP])
        vT = sb("vT", [P, NG, KP])
        xn = sb("xn", [P, TT, HID])
        xnT = split("xnT", [P, HC, TP])
        M = split("M", [P, HC, 2, NH, S2])
        VW = split("VW", [P, NG, 2, HID])
        prob = sb("prob", [P, 2, NH * S2])
        pT = split("pT", [P, 2, NJ, P])
        rowmax = sb("rowmax", [P, 2, NH])
        rowsum = sb("rowsum", [P, 2, NH])
        rinv = sb("rinv", [P, 2, NH])
        ln_stats = sb("ln_stats", [P, TT, 6])
        ln_mv = sb("ln_mv", [P, 2, TT, 2])
        ln_var = sb("ln_var", [P, TT])
        ln_rstd = sb("ln_rstd", [P, 2, TT])
        minus_half = sb("minus_half", [P, TT])
        mask_u8 = sb("mask_u8", [1, PAIRS * KP], U8)
        mask_bf = sb("mask_bf", [1, PAIRS * KP], BF16)
        bias_bf = sb("bias_bf", [1, PAIRS * KP], BF16)
        ones_bf = sb("ones_bf", [1, P], BF16)
        keep = sb("keep", [P, PAIRS])
        stage, ctx_sb = cm.Wq_staged, cm.ctx_staged

        full = {n: sem("full_" + n) for n in bank}
        half = {n: sem("half_" + n) for n in bank}
        free = {n: sem("free_" + n) for n in bank}
        small_loaded = sem("small_loaded")
        kv_loaded = sem("kv_loaded")
        wo_loaded = sem("wo_loaded")
        consts = sem("consts")
        mask_ready = sem("mask_ready")
        ctx_masked = sem("ctx_masked")
        stats_done = sem("stats_done")
        var_ready = sem("var_ready")
        rstd_ready = sem("rstd_ready")
        xn_ready = sem("xn_ready")
        max_ready = sem("max_ready")
        shifted = sem("shifted")
        exp_done = sem("exp_done")
        sum_ready = sem("sum_ready")
        rinv_ready = sem("rinv_ready")
        prob_ready = sem("prob_ready")
        VW_moved = sem("VW_moved")
        y_added = sem("y_added")

        setup = [(("keep", 0), "y0", "dve")] + \
                [(("w", i), ("q", "t", "s0", "s1")[i % 4], ("act", "dve")[i % 2]) for i in range(NH * HC // 4)] + \
                [(("ctx", 0), "o0", "act")]
        rot = ("q", "t", "s0", "s1")
        front = [(("xt", c), ("q", "t")[c], "both") for c in range(HC)]
        front += [(("k", i), ("q", "t")[i], "act") for i in range(2)]
        front += [(("v", i), ("s0", "s1")[i], "act") for i in range(2)]
        front += [(("m", i), rot[(i + 2) % 4], "both") for i in range(NH // 4 * HC)]

        def s_step(t):
            return [(("s", t, j), (("q", "t"), ("s0", "s1"))[t % 2][j], "") for j in range(2)]

        def t_step(t):
            return [(("t", t, j), ("o0", "o1")[j], "both") for j in range(2)]

        def vw_step(gs):
            return [(("vw", g), ("y1", "o0", "o1")[g % 3], "both") for g in gs]

        def y_step(t):
            return [(("y", t), "y1" if t == 1 else "y0", "")]

        def quiet(*name):
            return [(name, None, "")]

        nxt = [(("next",) + n, b, w) for n, b, w in front]
        body = (s_step(0) + vw_step((0, 1)) + s_step(1) + nxt[2:4] + quiet("next_ln", 0) + quiet("sum", 0)
                + vw_step((2, 3)) + quiet("move", 0) + vw_step((4, 5)) + quiet("sum", 1) + vw_step((6, 7))
                + quiet("move", 1) + nxt[4:6] + quiet("next_xn", 0) + t_step(0) + s_step(2) + t_step(1) + s_step(3)
                + quiet("sum", 2) + y_step(0) + y_step(1) + nxt[0:2] + quiet("sum", 3)
                + t_step(2) + nxt[6:8] + y_step(2) + nxt[8:11] + t_step(3) + nxt[11:] + y_step(3))
        order = Order(setup + front, [((n[1:] if n[0] == "next" else n), b, w) for n, b, w in body if b],
                      [(n, b, w) for n, b, w in body if b and n[0] != "next"], PAIRS - 1)

        def dst_of(name):
            what, i = name[0], name[1]
            n = name_bank[name]
            b = bank[n][:]
            if what == "w":
                return WqT[:, 2 * i:2 * i + 2, :], b.rearrange("p (h k) -> p h k", h=2)
            if what == "ctx":
                return ctxT[:], b
            if what == "xt":
                return xnT[:, i, :], b
            if what in ("k", "v"):
                return {"k": kT, "v": vT}[what][:, 4 * i:4 * i + 4, :], b.rearrange("p (g k) -> p g k", g=4)
            if what == "m":
                h, c = 4 * (i // HC), i % HC
                return (M[:, c, :, h:h + 4, :].view("p b h s -> p h b s"),
                        b.rearrange("p (h b s) -> p h b s", h=4, b=2))
            if what == "vw":
                return VWs[:, i, :], b
            if what == "t":
                return (pT[:, i % 2, 4 * name[2]:4 * name[2] + 4, :], b.rearrange("p (j q) -> p j q", j=4))

        name_bank = {name: b for name, b, _ in setup + front}
        name_bank.update({(n[1:] if n[0] == "next" else n): b for n, b, _ in body if b})

        def passes(eng, run):
            with eng.Fori(0, PAIRS - 1) as p:
                for name, _, _ in body:
                    run(p, name)
            for name, _, _ in body:
                if not name[0].startswith("next"):
                    run(PAIRS - 1, name)

        with nc.Block() as block:

            @block.sync
            def _(sp):
                sp.dma_start(mask_u8[:], mask.rearrange("(a b) s -> a (b s)", a=1)).then_inc(small_loaded, 16)
                sp.dma_start(wk[:], Wk).then_inc(kv_loaded, 16)
                sp.dma_start(wv[:], Wv).then_inc(kv_loaded, 16)
                sp.dma_start(wo[:], Wo.rearrange("(h p) n -> p h n", p=P)).then_inc(wo_loaded, 16)

                def run(p, name):
                    if name[0] != "move":
                        return
                    g0 = NG // 2 * name[1]
                    at = ("vw", g0 + 3)
                    sp.wait_ge(free[order.bank(p, at)], order.free(p, at))
                    for src, dst in ((VWs.hi, VW.hi), (VWs.lo, VW.lo)):
                        for b in range(2):
                            for h in range(2):
                                sp.dma_start(dst[h * S2:(h + 1) * S2, g0:g0 + 4, b, :].bitcast(F32),
                                             src[b * S2:(b + 1) * S2, g0:g0 + 4, h * HID:(h + 1) * HID].bitcast(F32))\
                                    .then_inc(VW_moved, 16)

                passes(sp, run)

            @block.gpsimd
            def _(pool):
                pool.memset(minus_half[:], -0.5).then_inc(consts, 1)
                pool.memset(ones_bf[:], 1.0).then_inc(consts, 1)

                def power(count, slot):
                    pool.wait_ge(consts, 2)
                    pool.wait_ge(var_ready, count)
                    pool.tensor_tensor(ln_rstd[:, slot, :], ln_var[:], minus_half[:], ALU.pow).then_inc(rstd_ready, 1)

                power(1, 0)

                def run(p, name):
                    if name[0] == "next_ln":
                        power(p + 2, 0)
                    if name[0] == "sum":
                        t = name[1]
                        pool.wait_ge(rinv_ready, p * TT + (t + 1))
                        pr = prob[:, t % 2, :].rearrange("p (h s) -> p h s", s=S2)
                        pool.tensor_tensor(pr, pr, rinv[:, t % 2, :].unsqueeze(2).to_broadcast([P, NH, S2]), ALU.mult)\
                            .then_inc(prob_ready, 1)

                passes(pool, run)

            @block.scalar
            def _(act):
                def copy_out(p, name):
                    who = order.who(p, name)
                    if who in ("both", "act"):
                        n = order.bank(p, name)
                        dst, src = dst_of(name)
                        act.wait_ge(full[n], order.full(p, name))
                        act.activation(dst.hi if who == "both" else dst, src, ACT.Copy)\
                            .then_inc(half[n] if who == "both" else free[n], 1)

                for name, _, _ in setup + front:
                    copy_out(None, name)

                def run(p, name):
                    if name[0] == "next":
                        copy_out(p, name[1:])
                    elif name[0] in ("vw", "t"):
                        copy_out(p, name)
                    elif name[0] == "sum":
                        t = name[1]
                        act.wait_ge(shifted, p * 2 * TT + 2 * (t + 1))
                        act.activation(prob[:, t % 2, :], prob[:, t % 2, :], ACT.Exp, scale=SCALE)\
                            .then_inc(exp_done, 1)

                passes(act, run)

            @block.vector
            def _(dve):
                def copy_out(p, name):
                    who = order.who(p, name)
                    n = order.bank(p, name)
                    if who == "both":
                        dst, src = dst_of(name)
                        dve.wait_ge(half[n], order.half(p, name))
                        dve.tensor_tensor(dst.lo, src, dst.hi.bitcast(F32), ALU.subtract).then_inc(free[n], 1)
                    elif who == "dve":
                        dst, src = dst_of(name)
                        dve.wait_ge(full[n], order.full(p, name))
                        dve.tensor_copy(dst, src).then_inc(free[n], 1)

                def tile(p, t):
                    return x_all[:, bass.ds(p * TT + t, 1), :].rearrange("p a k -> p (a k)")

                def layer_norm_stats(p, q):
                    for t in range(TT):
                        dve.bn_stats(ln_stats[:, t, :], tile(p, t)).then_inc(stats_done, 1)
                    dve.wait_ge(stats_done, q * 2 * TT + TT)
                    dve.tensor_copy(ln_var[:, 0:1], ln_stats[:, 0, 0:1])
                    for t in range(TT):
                        dve.bn_aggr(ln_mv[:, 0, t, :], ln_stats[:, t, :]).then_inc(stats_done, 1)
                    dve.wait_ge(stats_done, q * 2 * TT + 2 * TT)
                    dve.tensor_scalar(ln_var[:], ln_mv[:, 0, :, 1], EPS, None, ALU.add).then_inc(var_ready, 1)

                def normalize(p, q):
                    dve.wait_ge(rstd_ready, q + 1)
                    for t in range(TT):
                        dve.tensor_scalar(xn[:, t, :], tile(p, t), ln_mv[:, 0, t, 0:1], ln_rstd[:, 0, t:t + 1],
                                          ALU.subtract, ALU.mult).then_inc(xn_ready, 1)

                layer_norm_stats(0, 0)
                dve.wait_ge(small_loaded, 16)
                dve.wait_ge(cm.ctx_loaded, 16)
                dve.tensor_copy(mask_bf[:], mask_u8[:]).then_inc(mask_ready, 1)
                dve.wait_ge(mask_ready, 1)
                dve.tensor_scalar(bias_bf[:], mask_bf[:], -1.0, -NEG, ALU.add, ALU.mult).then_inc(mask_ready, 1)
                dve.wait_ge(full["y0"], 1)
                dve.tensor_copy(keep[:], bank["y0"][:, 0:PAIRS]).then_inc(free["y0"], 1)
                dve.wait_ge(free["y0"], 1)
                for p in range(PAIRS):
                    dve.tensor_scalar(ctx_sb[:, p, :], ctx_sb[:, p, :], keep[:, p:p + 1], None, ALU.mult)\
                        .then_inc(ctx_masked, 1)
                normalize(0, 0)
                for name, _, _ in setup[1:] + front:
                    copy_out(None, name)

                def run(p, name):
                    if name[0] == "next":
                        copy_out(p, name[1:])
                    elif name[0] in ("vw", "t"):
                        copy_out(p, name)
                    elif name[0] == "next_ln":
                        layer_norm_stats(p + 1, p + 1)
                    elif name[0] == "next_xn":
                        normalize(p + 1, p + 1)
                    elif name[0] == "s" and name[2] == 1:
                        t = name[1]
                        heads = NH // 2
                        banks = [bank[order.bank(p, ("s", t, j))][:].rearrange("p (h s) -> p h s", s=S2)
                                 for j in range(2)]
                        for j in range(2):
                            n = order.bank(p, ("s", t, j))
                            dve.wait_ge(full[n], order.full(p, ("s", t, j)))
                            dve.tensor_reduce(rowmax[:, t % 2, j * heads:(j + 1) * heads], banks[j], AX_X, ALU.max)\
                                .then_inc(max_ready, 1)
                        if t >= 2:
                            for j in range(2):
                                n = order.bank(p, ("t", t - 2, j))
                                dve.wait_ge(full[n], order.full(p, ("t", t - 2, j)))
                        for j in range(2):
                            n = order.bank(p, ("s", t, j))
                            dve.wait_ge(max_ready, p * 2 * TT + (2 * t + j + 1))
                            dve.tensor_tensor(
                                prob[:, t % 2, j * HALF:(j + 1) * HALF].rearrange("p (h s) -> p h s", s=S2), banks[j],
                                rowmax[:, t % 2, j * heads:(j + 1) * heads].unsqueeze(2).to_broadcast([P, heads, S2]),
                                ALU.subtract).then_inc(shifted, 1)
                    elif name[0] == "sum":
                        t = name[1]
                        dve.wait_ge(exp_done, p * TT + (t + 1))
                        dve.tensor_reduce(rowsum[:, t % 2, :], prob[:, t % 2, :].rearrange("p (h s) -> p h s", s=S2),
                                          AX_X, ALU.add).then_inc(sum_ready, 1)
                        dve.wait_ge(sum_ready, p * TT + (t + 1))
                        dve.reciprocal(rinv[:, t % 2, :], rowsum[:, t % 2, :]).then_inc(rinv_ready, 1)
                    elif name[0] == "y":
                        t = name[1]
                        n = order.bank(p, name)
                        dve.wait_ge(full[n], order.full(p, name))
                        dve.tensor_tensor(tile(p, t), bank[n][:, 0:HID], tile(p, t), ALU.add)\
                            .then_inc(y_added, 1)

                passes(dve, run)

            @block.tensor
            def _(pe):
                def wait_free(p, name):
                    n = order.bank(p, name)
                    if order.before(p, name) is None:
                        return
                    before = order.before(p, name)
                    if before[0] == "s":
                        pe.wait_ge(shifted, p * 2 * TT + (2 * before[1] + before[2] + 1))
                    elif before[0] == "y":
                        pe.wait_ge(y_added, p * TT + (before[1] + 1))
                    elif name == ("y", 0):
                        return
                    else:
                        pe.wait_ge(free[n], order.free(p, name) - (order.who(p, name) != ""))

                def wait_copied(p, name):
                    n = order.bank(p, name)
                    pe.wait_ge(free[n], order.free(p, name))

                def fill(p, name):
                    what, i = name[0], name[1]
                    n = order.bank(p, name)
                    wait_free(p, name)
                    if what == "w":
                        for j in range(4):
                            h, c = 2 * i + j // 2, j % 2
                            ins = pe.transpose(bank[n][:, j * P:(j + 1) * P], stage[:, c, h * P:(h + 1) * P], ident[:])
                    elif what == "ctx":
                        for j in range(PAIRS):
                            ins = pe.transpose(bank[n][:, j * P:(j + 1) * P], ctx_sb[:, j, :], ident[:])
                    elif what == "xt":
                        for t in range(TT):
                            ins = pe.transpose(bank[n][:, t * P:(t + 1) * P], xn[:, t, i * P:(i + 1) * P], ident[:])
                    elif what in ("k", "v"):
                        w = {"k": wk, "v": wv}[what]
                        q = 0 if p is None else p + 1
                        for j in range(4):
                            g = 4 * i + j
                            ins = pe.matmul(bank[n][:, j * P:(j + 1) * P], w[:, g * D:(g + 1) * D],
                                            ctxT[:, bass.ds(q * KP, KP)], start=True, stop=True,
                                            skip_group_check=True)
                    elif what == "m":
                        for j in range(4):
                            h, c = 4 * (i // HC) + j, i % HC
                            ins = pe.matmul(bank[n][:, j * P:(j + 1) * P], WqT[:, h, c * P:(c + 1) * P],
                                            kT[:, h // 2, :], start=True, stop=True, skip_group_check=True)
                    elif what == "vw":
                        w = wo[:, 2 * i:2 * i + 2, :].rearrange("p h n -> p (h n)")
                        ins = pe.matmul(bank[n][:], vT[:, i, :], w, start=True, stop=True, skip_group_check=True)
                    ins.then_inc(full[n], 1)

                pe.wait_ge(mask_ready, 2)
                pe.wait_ge(consts, 2)
                for p in range(PAIRS):
                    ins = pe.matmul(bank["y0"][:, p:p + 1], mask_bf[:, p * KP:(p + 1) * KP], ones_bf[:, 0:1],
                                    start=True, stop=True, skip_group_check=True)
                ins.then_inc(full["y0"], 1)
                pe.wait_ge(cm.wq_loaded, 16)
                for name, _, _ in setup[1:]:
                    if name[0] == "ctx":
                        pe.wait_ge(ctx_masked, PAIRS)
                    fill(None, name)
                for name, _, _ in setup[-5:]:
                    wait_copied(None, name)

                def needs(p, name):
                    q = 0 if p is None else p + 1
                    if name == ("xt", 0):
                        pe.wait_ge(xn_ready, q * TT + TT)
                    if name == ("k", 0) and p is None:
                        pe.wait_ge(kv_loaded, 32)
                    if name == ("m", 0):
                        wait_copied(p, ("k", 0))
                        wait_copied(p, ("k", 1))

                for name, _, _ in front:
                    needs(None, name)
                    fill(None, name)
                pe.wait_ge(wo_loaded, 16)

                def run(p, name):
                    what = name[0]
                    if what == "next":
                        needs(p, name[1:])
                        fill(p, name[1:])
                    elif what == "s":
                        t, j = name[1], name[2]
                        n = order.bank(p, name)
                        if t == 0 and j == 0:
                            for other, b, _ in front[-4:]:
                                pe.wait_ge(free[b], p * order.per[b][2] + order.free(None, other))
                        wait_free(p, name)
                        b = t // 2
                        for c in range(HC):
                            mm3(pe, bank[n][:], xnT[:, c, t * P:(t + 1) * P],
                                M[:, c, b, 8 * j:8 * j + 8, :].view("p h s -> p (h s)"), c == 0, False)
                        bias = bias_bf[:, bass.ds(p * KP + b * S2, S2)].unsqueeze(1).to_broadcast([1, NH // 2, S2])
                        pe.matmul(bank[n][:].rearrange("p (h s) -> p h s", s=S2), ones_bf[:, :], bias,
                                  start=False, stop=True, skip_group_check=True).then_inc(full[n], 1)
                    elif what == "vw":
                        fill(p, name)
                    elif what == "t":
                        t, j = name[1], name[2]
                        n = order.bank(p, name)
                        wait_free(p, name)
                        pe.wait_ge(prob_ready, p * TT + (t + 1))
                        for i in range(4):
                            at = (4 * j + i) * P
                            ins = pe.transpose(bank[n][:, i * P:(i + 1) * P], prob[:, t % 2, at:at + P], ident[:])
                        ins.then_inc(full[n], 1)
                    elif what == "y":
                        t = name[1]
                        b = t // 2
                        n = order.bank(p, name)
                        wait_free(p, name)
                        for j in range(2):
                            wait_copied(p, ("t", t, j))
                        if t == 0:
                            pe.wait_ge(VW_moved, p * 256 + 256)
                        for j in range(NJ):
                            ins = mm3(pe, bank[n][:, 0:HID], pT[:, t % 2, j, :], VW[:, j, b, :],
                                      j == 0, j == NJ - 1)
                        ins.then_inc(full[n], 1)

                passes(pe, run)


def feed_forward(nc, cm, gate, w0, w1, wo, xn_rows, y_rows, out):
    E, HID, MLP = w0.shape
    NT, HC = cm.NT, cm.HC
    MC = MLP // P
    GT = 4
    NG = NT // GT
    TOKENS = NT * P
    TILES = (y_rows.shape[0] - 2 * TOKENS) // P
    NEVER = -3e38
    WN = HC * MLP
    x_all, ident, bank = cm.x_all, cm.ident, cm.bank
    H0_BANKS, H1_BANKS, XT_BANK, IT_BANK, Y_BANK = ("q", "t"), ("s0", "s1"), "o0", "o1", "y0"
    XN_BANKS, GATE_BANKS = ("s0", "s1", "o0", "o1"), ("y0", "y1")

    def sem(name):
        return cm.sems.enter_context(nc.semaphore("c_" + name))

    with ExitStack() as ctx:
        def sb(name, shape, dt=F32, scope=ctx):
            return scope.enter_context(nc.sbuf_tensor("f_" + name, shape, dt))

        weight = [sb("weight%d" % k, [P, NT]) for k in range(2)]
        expert_of = sb("expert_of", [P, TILES], I32)
        move = sb("move", [P, TILES + 2, 2], I32)
        carrier, zero = sb("carrier", [P, 2]), sb("zero", [P, 1])
        move_now = sb("move_now", [P, 2, 2], I32)

        with ExitStack() as scope:
            got = sb("got", [P, 2, NT, HID], F32, scope)
        W = Split(sb("W_hi", [P, 2 * E, WN], F32R), sb("W_lo", [P, 2 * E, WN], F32R))
        with ExitStack() as scope:
            xnT = sb("xnT", [P, 2, HC, GT * P], F32, scope)
            logitsT = sb("logitsT", [E, 2, GT * P], F32, scope)
        Wo = sb("Wo", [P, E, MC, HID])

        with ExitStack() as scope:
            def tmp(name, shape, dt=F32):
                return sb(name, shape, dt, scope)

            gate_w = tmp("gate", [P, HC, E])
            ln_stats = tmp("ln_stats", [P, NT, 6])
            ln_mv = tmp("ln_mv", [P, NT, 2])
            ln_var = tmp("ln_var", [P, NT])
            ln_rstd = tmp("ln_rstd", [P, NT])
            minus_half = tmp("minus_half", [P, NT])
            experts = tmp("experts", [P, NT, E])
            before = tmp("before", [P, E, E])
            steps_of = tmp("steps_of", [P, E, NT])
            numbers = tmp("numbers", [P, TILES])
            lanes = tmp("lanes", [P, P])
            tile_no = tmp("tile_no", [P, 2, NT])
            lane = tmp("lane", [P, 1])
            spare = tmp("spare", [P, TILES])
            logits = tmp("logits", [P, NT, E])
            work = tmp("work", [P, NT, E])
            onehot = [tmp("onehot%d" % k, [P, NT, E]) for k in range(2)]
            taken = tmp("taken", [P, NT, E], BF16)
            earlier = tmp("earlier", [P, P], BF16)
            ones = tmp("ones", [P, P], BF16)
            top = [tmp("top%d" % k, [P, NT]) for k in range(2)]
            chosen = tmp("chosen", [P, NT])
            gap = tmp("gap", [P, NT])
            tiles_cmp = tmp("tiles_cmp", [P, E, NT])
            tiles = tmp("tiles", [P, E])
            tile_sums = tmp("tile_sums", [P, E, E])
            start = tmp("start", [P, E])
            end = tmp("end", [P, E])
            passed = tmp("passed", [P, TILES, E])
            expert_f = tmp("expert_f", [P, TILES])
            slot = tmp("slot", [P, NT, E])
            pos = tmp("pos", [P, 2, NT])
            pos_i = tmp("pos_i", [P, 3, 2 * NT], I32)
            pos_tile = tmp("pos_tile", [P, 2 * NT])
            pos_lane = tmp("pos_lane", [P, 2 * NT])
            found = tmp("found", [P, 4, TILES])
            token = tmp("token", [P, TILES])
            target = tmp("target", [P, TILES])
            with ExitStack() as inner:
                xn = sb("xn", [P, NT, HID], F32, inner)
            with ExitStack() as inner:
                lane_hot = sb("lane_hot", [P, 2 * NT, P], BF16, inner)
                tile_hot = sb("tile_hot", [P, 2 * NT, 3, TILES], BF16, inner)
        with ExitStack() as scope:
            rows = sb("rows", [P, 2, HID], F32, scope)
            xT = Split(sb("xT_hi", [P, 2, HC, P], F32R, scope), sb("xT_lo", [P, 2, HC, P], F32R, scope))
            sil = sb("sil", [P, 2, MLP], F32, scope)
            inter = sb("inter", [P, 2, MLP], F32, scope)
            interT = sb("interT", [P, 2, MC, P], F32, scope)
            y = sb("y", [P, 2, HID], F32, scope)

        gate_loaded, wo_loaded = sem("gate_loaded"), sem("wo_loaded")
        w_loaded = [sem("w_loaded%d" % i) for i in range(2 * E)]
        consts, stats_done, var_ready, rstd_ready = sem("consts"), sem("stats_done"), sem("var_ready"), sem("rstd_ready")
        xn_ready, xnT_full, xnT_ready = sem("xn_ready"), sem("xnT_full"), sem("xnT_ready")
        gate_full, gate_copied = sem("gate_full"), sem("gate_copied")
        gate_done, routed, taken_ready, ranks_full = sem("gate_done"), sem("routed"), sem("taken_ready"), sem("ranks_full")
        gap_ready, gap_exp, expert_ready = sem("gap_ready"), sem("gap_exp"), sem("expert_ready")
        hot_ready, found_full, move_ready = sem("hot_ready"), sem("found_full"), sem("move_ready")
        carried = sem("carried")
        w_hi, w_lo_pool, w_lo_dve, xn_stored = sem("w_hi"), sem("w_lo_pool"), sem("w_lo_dve"), sem("xn_stored")
        rows_loaded = (sem("rows_loaded0"), sem("rows_loaded1"))
        xt_full, xt_hi, xt_lo = sem("xt_full"), sem("xt_hi"), sem("xt_lo")
        h0_full, h1_full, silu_done, inter_done = sem("h0_full"), sem("h1_full"), sem("silu_done"), sem("inter_done")
        it_full, it_copied, y_full, y_copied = sem("it_full"), sem("it_copied"), sem("y_full"), sem("y_copied")
        y_stored = (sem("y_stored0"), sem("y_stored1"))
        got_loaded = [sem("got_loaded%d" % i) for i in range(NG)]
        added, stored = sem("added"), sem("stored")

        DVE_SPLITS = ((0, 3), (12, 13, 14, 15))
        POOL_SPLITS = [i for i in range(2 * E) if i not in DVE_SPLITS[0] + DVE_SPLITS[1]]
        PEEL = 3
        LAST = TILES - 1

        def count(q, j, c=0):
            return j + c if q is None else q * 2 + (j + c)

        def wait(eng, sem, q, j, c):
            if q is not None or j + c > 0:
                eng.wait_ge(sem, count(q, j, c))

        def wait_dma(eng, sems, q, j, c):
            n = (j + c) // 2 + 1
            if q is not None:
                eng.wait_ge(sems[(j + c) % 2], q * 16 + 16 * n)
            elif n > 0:
                eng.wait_ge(sems[(j + c) % 2], 16 * n)

        def all_tiles(eng, run):
            for j in range(PEEL):
                run(None, j)
            with eng.Fori(0, (TILES - PEEL - 2) // 2) as q:
                run(q, PEEL)
                run(q, PEEL + 1)
            for j in range(TILES - 2, TILES):
                run(None, j)

        def split_lo(eng, i, signal):
            eng.wait_ge(w_hi, i + 1)
            eng.tensor_tensor(W.lo[:, i, :], W.lo[:, i, :].bitcast(F32), W.hi[:, i, :].bitcast(F32), ALU.subtract)\
                .then_inc(signal, 1)

        def load_results(eng, k):
            for j in (LAST - 1, LAST):
                eng.wait_ge(y_stored[j % 2], 16 * (j // 2 + 1))
            view = y_rows[k * TOKENS:(k + 1) * TOKENS, :].rearrange("(t p) k -> p t k", p=P)
            for g in range(NG):
                eng.dma_start(got[:, k, GT * g:GT * (g + 1), :], view[:, GT * g:GT * (g + 1), :])\
                    .then_inc(got_loaded[g], 16)

        with nc.Block() as block:
            @block.sync
            def _(sp):
                sp.dma_start(gate_w[:], gate.rearrange("(c p) e -> p c e", p=P)).then_inc(gate_loaded, 16)
                def load_w(i):
                    w = (w0, w1)[i % 2][i // 2]
                    sp.dma_start(W.lo[:, i, :].bitcast(F32).rearrange("p (c n) -> p c n", c=HC),
                                 w.rearrange("(c p) n -> p c n", p=P)).then_inc(w_loaded[i], 16)

                view = xn_rows.rearrange("(t p) k -> p t k", p=P)
                for i in range(6):
                    load_w(i)
                for g in range(NG):
                    sp.wait_ge(xn_ready, GT * (g + 1))
                    sp.dma_start(view[:, GT * g:GT * (g + 1), :], xn[:, GT * g:GT * (g + 1), :])\
                        .then_inc(xn_stored, 16)
                    for i in (6 + 2 * g, 7 + 2 * g):
                        load_w(i)
                for i in (2 * E - 2, 2 * E - 1):
                    load_w(i)
                sp.wait_ge(gate_done, 1)
                for e in range(E):
                    sp.dma_start(Wo[:, e, :, :], wo[e].rearrange("(c p) n -> p c n", p=P)).then_inc(wo_loaded, 16)

                load_results(sp, 0)
                view = out.rearrange("b (t p) k -> p (b t) k", p=P)
                for g in range(NG):
                    sp.wait_ge(added, 2 * GT * (g + 1))
                    sp.dma_start(view[:, GT * g:GT * (g + 1), :], x_all[:, GT * g:GT * (g + 1), :])\
                        .then_inc(stored, 16)
                sp.wait_ge(stored, 16 * NG)

            @block.gpsimd
            def _(pool):
                pool.memset(minus_half[:], -0.5).then_inc(consts, 1)
                for g in range(NG):
                    if g == 0:
                        pool.wait_ge(consts, 1)
                    pool.wait_ge(var_ready, g + 1)
                    at = slice(GT * g, GT * (g + 1))
                    pool.tensor_tensor(ln_rstd[:, at], ln_var[:, at], minus_half[:, at], ALU.pow)\
                        .then_inc(rstd_ready, 1)
                pool.memset(zero[:], 0.0).then_inc(consts, 1)
                pool.memset(move[:], 0).then_inc(consts, 1)
                for e in range(E):
                    pool.memset(experts[:, :, e:e + 1], float(e)).then_inc(consts, 1)
                pool.memset(ones[:], 1.0).then_inc(consts, 1)
                for t in range(NT):
                    pool.memset(steps_of[:, :, t:t + 1], float(t * P)).then_inc(consts, 1)
                pool.wait_ge(consts, E + 4 + NT)
                pool.affine_select(earlier[:], ones[:], pattern=[[1, P]], base=-1, channel_multiplier=-1,
                                   compare_op=ALU.is_ge, fill=0.0).then_inc(consts, 1)
                pool.iota(numbers[:], pattern=[[1, TILES]], base=0, channel_multiplier=0,
                          allow_small_or_imprecise_dtypes=True).then_inc(consts, 1)
                pool.iota(lanes[:], pattern=[[1, P]], base=0, channel_multiplier=0,
                          allow_small_or_imprecise_dtypes=True).then_inc(consts, 1)
                pool.iota(tile_no[:], pattern=[[0, 2], [1, NT]], base=0, channel_multiplier=0,
                          allow_small_or_imprecise_dtypes=True).then_inc(consts, 1)
                pool.iota(lane[:], pattern=[[0, 1]], base=0, channel_multiplier=1,
                          allow_small_or_imprecise_dtypes=True).then_inc(consts, 1)
                pool.iota(spare[:], pattern=[[P, TILES]], base=2 * TOKENS, channel_multiplier=1,
                          allow_small_or_imprecise_dtypes=True).then_inc(consts, 1)
                for i in POOL_SPLITS[:-2]:
                    split_lo(pool, i, w_lo_pool)

                pool.wait_ge(routed, 29)
                pool.tensor_tensor(tile_hot[:, :, 1, :], tile_hot[:, :, 0, :],
                                   tile_no[:].rearrange("p k t -> p (k t)").unsqueeze(2)
                                   .to_broadcast([P, 2 * NT, TILES]), ALU.mult).then_inc(hot_ready, 1)
                for i in POOL_SPLITS[-2:]:
                    split_lo(pool, i, w_lo_pool)

                def gather(j, n):
                    pool.indirect_dma_start(rows[:, j % 2, :], None, xn_rows[:, :],
                                            bass.IndirectOffsetOnAxis(move_now[:, n, 0:1], 0))\
                        .then_inc(rows_loaded[j % 2], 16)

                def scatter(j, n):
                    pool.indirect_dma_start(y_rows[:, :], bass.IndirectOffsetOnAxis(move_now[:, n, 1:2], 0),
                                            y[:, j % 2, :], None).then_inc(y_stored[j % 2], 16)

                pool.wait_ge(xn_stored, 16 * NG)
                pool.wait_ge(move_ready, 2)
                for j in range(2):
                    gather(j, j)

                def run(q, j):
                    pool.wait_ge(move_ready, count(q, j, 3))
                    pool.tensor_tensor(carrier[:, j % 2:j % 2 + 1], zero[:], zero[:], ALU.add)\
                        .then_inc(carried, 1)
                    if q is not None or j + 2 <= LAST:
                        gather(j + 2, j % 2)
                    if q is not None or j >= 2:
                        scatter(j - 2, j % 2)

                all_tiles(pool, run)
                for j in (LAST + 1, LAST + 2):
                    run(None, j)

            @block.scalar
            def _(act):
                def split_hi(i):
                    act.wait_ge(w_loaded[i], 16)
                    act.activation(W.hi[:, i, :], W.lo[:, i, :].bitcast(F32), ACT.Copy).then_inc(w_hi, 1)

                def copy_xnT(g):
                    for c in range(HC):
                        n = g * HC + c
                        act.wait_ge(xnT_full, n + 1)
                        act.activation(xnT[:, g % 2, c, :], bank[XN_BANKS[n % 4]][:], ACT.Copy).then_inc(xnT_ready, 1)

                def copy_gate(g):
                    act.wait_ge(gate_full, g + 1)
                    act.activation(logitsT[:, g % 2, :], bank[GATE_BANKS[g % 2]][0:E, :], ACT.Copy)\
                        .then_inc(gate_copied, 1)

                copy_xnT(0)
                split_hi(0)
                copy_xnT(1)
                split_hi(1)
                copy_gate(0)
                copy_xnT(2)
                split_hi(2)
                copy_gate(1)
                copy_xnT(3)
                split_hi(3)
                copy_gate(2)
                copy_gate(3)
                for i in range(4, 2 * E):
                    split_hi(i)
                act.wait_ge(gap_ready, 1)
                act.activation(gap[:], gap[:], ACT.Exp).then_inc(gap_exp, 1)

                def run(q, j):
                    if j == 0 and q is None:
                        copy_hi(None, 0)
                    act.wait_ge(h0_full, count(q, j, 1))
                    act.activation(sil[:, j % 2, :], bank[H0_BANKS[j % 2]][:], ACT.Silu).then_inc(silu_done, 1)
                    if q is not None or j > 0:
                        copy_it(q, j - 1)
                    if q is not None or j < LAST:
                        copy_hi(q, j + 1)

                def copy_it(q, j):
                    act.wait_ge(it_full, count(q, j, 1))
                    act.activation(interT[:, j % 2, :, :].rearrange("p c n -> p (c n)"), bank[IT_BANK][:], ACT.Copy)\
                        .then_inc(it_copied, 1)

                def copy_hi(q, j):
                    act.wait_ge(xt_full, count(q, j, 1))
                    act.activation(xT.hi[:, j % 2, :, :].rearrange("p c n -> p (c n)"), bank[XT_BANK][:, 0:HC * P],
                                   ACT.Copy).then_inc(xt_hi, 1)

                all_tiles(act, run)
                copy_it(None, LAST)
                load_results(act, 1)

            @block.vector
            def _(dve):
                def layer_norm_stats(g):
                    for t in range(GT * g, GT * (g + 1)):
                        dve.bn_stats(ln_stats[:, t, :], x_all[:, t, :]).then_inc(stats_done, 1)
                    dve.wait_ge(stats_done, 2 * GT * g + GT)
                    for t in range(GT * g, GT * (g + 1)):
                        dve.bn_aggr(ln_mv[:, t, :], ln_stats[:, t, :]).then_inc(stats_done, 1)
                    dve.wait_ge(stats_done, 2 * GT * (g + 1))
                    at = slice(GT * g, GT * (g + 1))
                    dve.tensor_scalar(ln_var[:, at], ln_mv[:, at, 1], EPS, None, ALU.add).then_inc(var_ready, 1)

                def normalize(g):
                    dve.wait_ge(rstd_ready, g + 1)
                    for t in range(GT * g, GT * (g + 1)):
                        dve.tensor_scalar(xn[:, t, :], x_all[:, t, :], ln_mv[:, t, 0:1], ln_rstd[:, t:t + 1],
                                          ALU.subtract, ALU.mult).then_inc(xn_ready, 1)

                layer_norm_stats(0)
                for g in range(1, NG):
                    layer_norm_stats(g)
                    normalize(g - 1)
                normalize(NG - 1)
                for i in DVE_SPLITS[0]:
                    split_lo(dve, i, w_lo_dve)

                def wide(a):
                    return a[:].unsqueeze(2).to_broadcast([P, NT, E])

                dve.wait_ge(consts, E + 10 + NT)
                dve.tensor_tensor(before[:], experts[:, 0:E, :],
                                  experts[:, 0, :].unsqueeze(2).to_broadcast([P, E, E]), ALU.is_lt).then_inc(routed, 1)
                dve.wait_ge(gate_done, 1)
                dve.tensor_copy(logits[:], bank["q"][:, 0:NT * E].rearrange("p (t e) -> p t e", e=E))\
                    .then_inc(routed, 1)
                for k in range(2):
                    r = 1 + 6 * k
                    dve.wait_ge(routed, r + 1)
                    dve.tensor_reduce(top[k][:], logits[:], AX_X, ALU.max).then_inc(routed, 1)
                    dve.wait_ge(routed, r + 2)
                    dve.tensor_tensor(work[:], logits[:], wide(top[k]), ALU.is_lt).then_inc(routed, 1)
                    dve.wait_ge(routed, r + 3)
                    dve.scalar_tensor_tensor(work[:], work[:], 1000.0, experts[:], ALU.mult, ALU.add)\
                        .then_inc(routed, 1)
                    dve.wait_ge(routed, r + 4)
                    dve.tensor_reduce(chosen[:], work[:], AX_X, ALU.min).then_inc(routed, 1)
                    dve.wait_ge(routed, r + 5)
                    dve.tensor_tensor(onehot[k][:], experts[:], wide(chosen), ALU.is_equal).then_inc(routed, 1)
                    dve.wait_ge(routed, r + 6)
                    if k == 0:
                        dve.scalar_tensor_tensor(logits[:], onehot[0][:], NEVER, logits[:], ALU.mult, ALU.add)\
                            .then_inc(routed, 1)
                dve.tensor_tensor(taken[:], onehot[0][:], onehot[1][:], ALU.add).then_inc(taken_ready, 1)
                dve.tensor_tensor(gap[:], top[1][:], top[0][:], ALU.subtract).then_inc(gap_ready, 1)

                dve.wait_ge(ranks_full, 1)
                dve.tensor_tensor(tiles_cmp[:], bank["t"][:, 0:E].unsqueeze(2).to_broadcast([P, E, NT]), steps_of[:],
                                  ALU.is_gt).then_inc(routed, 1)
                dve.wait_ge(routed, 14)
                dve.tensor_reduce(tiles[:], tiles_cmp[:], AX_X, ALU.add).then_inc(routed, 1)
                dve.wait_ge(routed, 15)
                dve.tensor_tensor(tile_sums[:], tiles[:].unsqueeze(1).to_broadcast([P, E, E]), before[:], ALU.mult)\
                    .then_inc(routed, 1)
                dve.wait_ge(routed, 16)
                dve.tensor_reduce(start[:], tile_sums[:], AX_X, ALU.add).then_inc(routed, 1)
                dve.wait_ge(routed, 17)
                dve.scalar_tensor_tensor(slot[:], start[:].unsqueeze(1).to_broadcast([P, NT, E]), float(P),
                                         bank["s0"][:, 0:NT * E].rearrange("p (t e) -> p t e", e=E),
                                         ALU.mult, ALU.add).then_inc(routed, 1)
                dve.tensor_tensor(end[:], start[:], tiles[:], ALU.add).then_inc(routed, 1)
                for k in range(2):
                    dve.wait_ge(routed, 19 + 2 * k)
                    dve.tensor_tensor(work[:], slot[:], onehot[k][:], ALU.mult).then_inc(routed, 1)
                    dve.wait_ge(routed, 20 + 2 * k)
                    dve.tensor_reduce(pos[:, k, :], work[:], AX_X, ALU.add).then_inc(routed, 1)
                dve.wait_ge(routed, 23)
                dve.tensor_copy(pos_i[:, 0, :], pos[:].rearrange("p k t -> p (k t)")).then_inc(routed, 1)
                dve.wait_ge(routed, 24)
                dve.tensor_scalar(pos_i[:, 1, :], pos_i[:, 0, :], 7, None, ALU.arith_shift_right).then_inc(routed, 1)
                dve.tensor_scalar(pos_i[:, 2, :], pos_i[:, 0, :], P - 1, None, ALU.bitwise_and).then_inc(routed, 1)
                dve.wait_ge(routed, 26)
                dve.wait_ge(xn_stored, 16 * NG)
                dve.tensor_copy(pos_tile[:], pos_i[:, 1, :]).then_inc(routed, 1)
                dve.tensor_copy(pos_lane[:], pos_i[:, 2, :]).then_inc(routed, 1)
                dve.wait_ge(routed, 28)
                dve.tensor_tensor(tile_hot[:, :, 0, :], pos_tile[:].unsqueeze(2).to_broadcast([P, 2 * NT, TILES]),
                                  numbers[:].unsqueeze(1).to_broadcast([P, 2 * NT, TILES]), ALU.is_equal)\
                    .then_inc(routed, 1)
                for k in range(2):
                    at = slice(k * NT, (k + 1) * NT)
                    dve.tensor_tensor(lane_hot[:, at, :], pos_lane[:, at].unsqueeze(2).to_broadcast([P, NT, P]),
                                      lanes[:].unsqueeze(1).to_broadcast([P, NT, P]), ALU.is_equal)\
                        .then_inc(routed, 1)
                    if k == 0:
                        dve.wait_ge(routed, 30)
                        dve.tensor_scalar(tile_hot[:, :, 2, :], tile_hot[:, :, 0, :], lane[:, 0:1], None, ALU.mult)\
                            .then_inc(routed, 1)
                dve.tensor_tensor(passed[:], end[:].unsqueeze(1).to_broadcast([P, TILES, E]),
                                  numbers[:].unsqueeze(2).to_broadcast([P, TILES, E]), ALU.is_le).then_inc(routed, 1)
                dve.wait_ge(routed, 33)
                dve.tensor_reduce(expert_f[:], passed[:], AX_X, ALU.add).then_inc(routed, 1)
                dve.wait_ge(routed, 34)
                dve.tensor_scalar(expert_f[:], expert_f[:], float(E - 1), None, ALU.min).then_inc(routed, 1)
                dve.wait_ge(routed, 35)
                dve.tensor_copy(expert_of[:], expert_f[:]).then_inc(expert_ready, 1)

                for i in DVE_SPLITS[1]:
                    split_lo(dve, i, w_lo_dve)
                dve.wait_ge(found_full, 1)
                dve.tensor_copy(found[:, 0:3, :], bank["s1"][:, 0:3 * TILES].rearrange("p (a j) -> p a j", a=3))\
                    .then_inc(routed, 1)
                dve.tensor_copy(found[:, 3, :], bank["q"][:, 0:TILES]).then_inc(routed, 1)
                dve.wait_ge(routed, 37)
                dve.scalar_tensor_tensor(token[:], found[:, 1, :], float(P), found[:, 2, :], ALU.mult, ALU.add)\
                    .then_inc(routed, 1)
                dve.tensor_tensor(target[:], found[:, 0, :], spare[:], ALU.mult).then_inc(routed, 1)
                dve.wait_ge(routed, 38)
                dve.tensor_copy(move_now[:, :, 0], token[:, 0:2]).then_inc(move_ready, 2)
                dve.wait_ge(routed, 39)
                dve.tensor_tensor(target[:], spare[:], target[:], ALU.subtract).then_inc(routed, 1)
                dve.scalar_tensor_tensor(found[:, 3, :], found[:, 3, :], float(TOKENS), token[:], ALU.mult, ALU.add)\
                    .then_inc(routed, 1)
                dve.wait_ge(routed, 41)
                dve.tensor_tensor(target[:], target[:], found[:, 3, :], ALU.add).then_inc(routed, 1)
                dve.tensor_copy(move[:, 0:TILES - 2, 0], token[:, 2:TILES]).then_inc(routed, 1)
                dve.wait_ge(routed, 43)
                dve.tensor_copy(move[:, 2:TILES + 2, 1], target[:]).then_inc(routed, 1)

                dve.wait_ge(gap_exp, 1)
                dve.tensor_scalar(top[0][:], gap[:], 1.0, None, ALU.add).then_inc(routed, 1)
                dve.wait_ge(routed, 45)
                dve.reciprocal(weight[0][:], top[0][:]).then_inc(routed, 1)
                dve.wait_ge(routed, 46)
                dve.tensor_tensor(weight[1][:], gap[:], weight[0][:], ALU.mult).then_inc(routed, 1)
                dve.wait_ge(routed, 47)

                def copy_lo(q, j):
                    dve.wait_ge(xt_hi, count(q, j, 1))
                    dve.tensor_tensor(xT.lo[:, j % 2, :, :].rearrange("p c n -> p (c n)"), bank[XT_BANK][:, 0:HC * P],
                                      xT.hi[:, j % 2, :, :].rearrange("p c n -> p (c n)").bitcast(F32),
                                      ALU.subtract).then_inc(xt_lo, 1)

                def copy_y(q, j):
                    dve.wait_ge(y_full, count(q, j, 1))
                    wait_dma(dve, y_stored, q, j, -2)
                    dve.tensor_copy(y[:, j % 2, :], bank[Y_BANK][:, 0:HID]).then_inc(y_copied, 1)

                def next_move(q, j):
                    if q is not None or j <= LAST:
                        dve.wait_ge(xt_full, count(q, j, 1))
                    wait(dve, carried, q, j, -1)
                    dve.tensor_copy(move_now[:, j % 2, :], move[:, bass.ds(count(q, j), 1), :]
                                    .rearrange("p a k -> p (a k)")).then_inc(move_ready, 1)

                def run(q, j):
                    if j == 0 and q is None:
                        copy_lo(None, 0)
                    next_move(q, j)
                    if q is not None or j < LAST:
                        copy_lo(q, j + 1)
                    dve.wait_ge(h1_full, count(q, j, 1))
                    dve.wait_ge(silu_done, count(q, j, 1))
                    dve.tensor_tensor(inter[:, j % 2, :], bank[H1_BANKS[j % 2]][:], sil[:, j % 2, :], ALU.mult)\
                        .then_inc(inter_done, 1)
                    if q is not None or j > 0:
                        copy_y(q, j - 1)

                all_tiles(dve, run)
                next_move(None, LAST + 1)
                copy_y(None, LAST)
                next_move(None, LAST + 2)

                for g in range(NG):
                    dve.wait_ge(got_loaded[g], 32)
                    for k in range(2):
                        if k == 1:
                            dve.wait_ge(added, (2 * g + 1) * GT)
                        for t in range(g * GT, (g + 1) * GT):
                            dve.scalar_tensor_tensor(x_all[:, t, :], got[:, k, t, :], weight[k][:, t:t + 1],
                                                     x_all[:, t, :], ALU.mult, ALU.add).then_inc(added, 1)

            @block.tensor
            def _(pe):
                pe.wait_ge(gate_loaded, 16)
                def transpose_xn(g):
                    pe.wait_ge(xn_ready, (g + 1) * GT)
                    for c in range(HC):
                        n = g * HC + c
                        if n >= 4:
                            pe.wait_ge(xnT_ready, n - 3)
                        for t in range(GT):
                            ins = pe.transpose(bank[XN_BANKS[n % 4]][:, t * P:(t + 1) * P],
                                               xn[:, g * GT + t, c * P:(c + 1) * P], ident[:])
                        ins.then_inc(xnT_full, 1)

                def gate_logits(g):
                    pe.wait_ge(xnT_ready, HC * (g + 1))
                    if g >= 2:
                        pe.wait_ge(gate_copied, g - 1)
                    for c in range(HC):
                        ins = pe.matmul(bank[GATE_BANKS[g % 2]][0:E, :], gate_w[:, c, :], xnT[:, g % 2, c, :],
                                        start=c == 0, stop=c == HC - 1, skip_group_check=True)
                    ins.then_inc(gate_full, 1)

                def transpose_logits(g):
                    pe.wait_ge(gate_copied, g + 1)
                    for t in range(GT):
                        at = (g * GT + t) * E
                        ins = pe.transpose(bank["q"][:, at:at + E], logitsT[:, g % 2, t * P:(t + 1) * P],
                                           ident[0:E, 0:E])
                    return ins

                transpose_xn(0)
                transpose_xn(1)
                gate_logits(0)
                transpose_xn(2)
                gate_logits(1)
                transpose_logits(0)
                transpose_xn(3)
                gate_logits(2)
                transpose_logits(1)
                gate_logits(3)
                transpose_logits(2)
                ins = transpose_logits(3)
                ins.then_inc(gate_done, 1)
                pe.wait_ge(taken_ready, 1)
                flat = taken[:].rearrange("p t e -> p (t e)")
                pe.matmul(bank["s0"][:, 0:NT * E], earlier[:], flat, start=True, stop=False, skip_group_check=True)
                for s in range(1, NT):
                    pe.matmul(bank["s0"][:, s * E:NT * E], ones[:], flat[:, 0:(NT - s) * E],
                              start=False, stop=s == NT - 1, skip_group_check=True)
                for t in range(NT):
                    ins = pe.matmul(bank["t"][:, 0:E], ones[:], taken[:, t, :], start=t == 0, stop=t == NT - 1,
                                    skip_group_check=True)
                ins.then_inc(ranks_full, 1)
                pe.wait_ge(routed, 32)
                pe.wait_ge(hot_ready, 1)
                for n in range(2 * NT):
                    pe.matmul(bank["s1"][:, 0:3 * TILES], lane_hot[:, n, :],
                              tile_hot[:, n, :, :].rearrange("p a j -> p (a j)"), start=n == 0, stop=n == 2 * NT - 1,
                              skip_group_check=True)
                for n in range(NT, 2 * NT):
                    ins = pe.matmul(bank["q"][:, 0:TILES], lane_hot[:, n, :], tile_hot[:, n, 0, :],
                                    start=n == NT, stop=n == 2 * NT - 1, skip_group_check=True)
                ins.then_inc(found_full, 1)

                def xt(q, j):
                    wait_dma(pe, rows_loaded, q, j, 0)
                    wait(pe, xt_lo, q, j, 0)
                    for c in range(HC):
                        ins = pe.transpose(bank[XT_BANK][:, c * P:(c + 1) * P], rows[:, j % 2, c * P:(c + 1) * P],
                                           ident[:])
                    ins.then_inc(xt_full, 1)

                def expert(q, j):
                    return pe.value_load(expert_of[0:1, bass.ds(count(q, j), 1)], min_val=0, max_val=E - 1)

                def hidden(q, j, e, half, banks, full):
                    for c in range(HC):
                        w = Split(*[a[:, bass.ds(e * 2 + half, 1), c * MLP:(c + 1) * MLP]
                                    .rearrange("p a n -> p (a n)") for a in (W.hi, W.lo)])
                        ins = mm3(pe, bank[banks[j % 2]][:], xT[:, j % 2, c, :], w, c == 0, c == HC - 1)
                    ins.then_inc(full, 1)

                def it(q, j):
                    pe.wait_ge(inter_done, count(q, j, 1))
                    for m in range(MC):
                        ins = pe.transpose(bank[IT_BANK][:, m * P:(m + 1) * P], inter[:, j % 2, m * P:(m + 1) * P],
                                           ident[:])
                    ins.then_inc(it_full, 1)

                def outputs(q, j, e):
                    pe.wait_ge(it_copied, count(q, j, 1))
                    wait(pe, y_copied, q, j, 0)
                    for m in range(MC):
                        w = Wo[:, bass.ds(e, 1), m, :].rearrange("p a n -> p (a n)")
                        ins = pe.matmul(bank[Y_BANK][:, 0:HID], interT[:, j % 2, m, :], w,
                                        start=m == 0, stop=m == MC - 1)
                    ins.then_inc(y_full, 1)

                pe.wait_ge(expert_ready, 1)
                pe.wait_ge(routed, 47)
                xt(None, 0)
                pe.wait_ge(w_lo_pool, len(POOL_SPLITS))
                pe.wait_ge(w_lo_dve, 2 * E - len(POOL_SPLITS))
                pe.wait_ge(wo_loaded, 16 * E)

                def run(q, j):
                    e = expert(q, j)
                    pe.wait_ge(xt_lo, count(q, j, 1))
                    wait(pe, inter_done, q, j, -1)
                    hidden(q, j, e, 0, H0_BANKS, h0_full)
                    if q is not None or j > 0:
                        it(q, j - 1)
                    hidden(q, j, e, 1, H1_BANKS, h1_full)
                    if q is not None or j < LAST:
                        xt(q, j + 1)
                    if q is not None or j > 0:
                        outputs(q, j - 1, expert(q, j - 1))

                all_tiles(pe, run)
                it(None, LAST)
                outputs(None, LAST, expert(None, LAST))


def decoder_layer(nc, x, ctx_in, mask, w_qkv, w_proj, Wq, Wk, Wv, Wo, gate, w0, w1, wo, out):
    cm = Common()
    cm.x = x
    cm.B, cm.S, cm.HID = x.shape
    cm.HC = cm.HID // P
    cm.NT = cm.B * cm.S // P
    cm.PAIRS = cm.B // 2
    cm.TP = 2 * cm.S
    cm.TT = cm.TP // P
    with ExitStack() as ctx:
        cm.sems = ctx
        cm.bank = {n: ctx.enter_context(nc.psum_tensor("bank_" + n, [P, 512], F32))
                   for n in ("q", "t", "s0", "s1", "o0", "o1", "y0", "y1")}
        cm.x_all = ctx.enter_context(nc.sbuf_tensor("x_all", [P, cm.NT, cm.HID], F32))
        cm.ident = ctx.enter_context(nc.sbuf_tensor("ident", [P, P], F32))
        E, TOP_K, tokens = w0.shape[0], 2, cm.NT * P
        tiles = TOP_K * cm.NT + E - 1
        xn_rows = nc.dram_tensor("xn_rows", [tokens, cm.HID], F32).ap()
        y_rows = nc.dram_tensor("y_rows", [TOP_K * tokens + tiles * P, cm.HID], F32).ap()

        with ExitStack() as early:
            cm.stage = early.enter_context(nc.sbuf_tensor("stage", [P, w_qkv.shape[0] // P * cm.HID], F32))
            cm.wq_loaded, cm.ctx_loaded = ctx.enter_context(nc.semaphore("wq_loaded")), \
                ctx.enter_context(nc.semaphore("ctx_loaded"))
            wq_cols, ctx_cols = cm.HC * Wq.shape[1], cm.PAIRS * ctx_in.shape[2]
            cm.Wq_staged = cm.stage[:, 0:wq_cols].rearrange("p (c n) -> p c n", c=cm.HC)
            cm.ctx_staged = cm.stage[:, wq_cols:wq_cols + ctx_cols].rearrange("p (a d) -> p a d", a=cm.PAIRS)

            def load_cross_inputs(eng):
                eng.dma_start(cm.Wq_staged, Wq.rearrange("(c p) n -> p c n", p=P)).then_inc(cm.wq_loaded, 16)
                eng.dma_start(cm.ctx_staged, ctx_in.rearrange("(p b) s d -> (b s) p d", b=2))\
                    .then_inc(cm.ctx_loaded, 16)

            cm.load_cross_inputs = load_cross_inputs
            self_attention(nc, cm, w_qkv, w_proj)
        cross_attention(nc, cm, ctx_in, mask, Wq, Wk, Wv, Wo)
        feed_forward(nc, cm, gate, w0, w1, wo, xn_rows, y_rows, out)


_INS = ['x', 'ctx_1024', 'mask_BxS2_bf1', 'L0_attn_weight_qkv', 'L0_attn_weight_proj', 'L0_xattn_Wq', 'L0_xattn_Wk',
        'L0_xattn_Wv', 'L0_xattn_Wo', 'L0_ffn_gate_kernel', 'L0_ffn_w0_kernel', 'L0_ffn_w1_kernel',
        'L0_ffn_wo_kernel']
_OUTS = [((8, 256, 256), 'float32')]


def kernel(**inputs):
    import numpy as _np
    import concourse.bacc as _bacc
    from concourse import mybir as _mybir
    from concourse.bass_utils import run_bass_kernel_spmd as _run

    nc = _bacc.Bacc("TRN2", target_bir_lowering=False, num_devices=1)
    arrays, args = {}, []
    for name in _INS:
        a = _np.ascontiguousarray(inputs[name])
        if a.dtype.kind == "b":
            a = a.view(_np.uint8)
        arrays[f"in_{name}_dram"] = a
        args.append(nc.dram_tensor(f"in_{name}_dram", a.shape, _mybir.dt.from_np(a.dtype), kind="ExternalInput").ap())
    for i, (shape, dtype) in enumerate(_OUTS):
        dt = _mybir.dt.from_np(_np.dtype(dtype))
        args.append(nc.dram_tensor(f"out_{i}_dram", shape, dt, kind="ExternalOutput").ap())
    decoder_layer(nc, *args)
    r = _run(nc, [arrays], core_ids=[0])
    return r.results[0]["out_0_dram"]
```
